# Optimizing a Trainium2 kernel written in Bass

```python
import numpy as np
import jax
import jax.numpy as jnp

def _softmax(x, axis=-1):
    return jax.nn.softmax(x, axis=axis)

def _gelu(x):
    return jax.nn.gelu(x, approximate=True)

def _silu(x):
    return jax.nn.silu(x)

def _sigmoid(x):
    return jax.nn.sigmoid(x)

def _layernorm(x, axis=-1, eps=1e-05):
    m = jnp.mean(x, axis=axis, keepdims=True)
    v = jnp.var(x, axis=axis, keepdims=True)
    return (x - m) / jnp.sqrt(v + eps)

def _scatter_add(tgt, idx, src, axis=0):
    return tgt.at[idx].add(src)

def _segment_sum(src, seg, n):
    return jax.ops.segment_sum(src, seg, n)
kernel_name = 'mk_flamingo_gated_d2_seqx_r4_683667'

def setup_inputs(seed: int=0):
    np.random.seed(seed)
    _w = jnp.asarray

    def _rec_inputs():
        import jax
        import jax.numpy as jnp
        _rk = jax.random.key(seed)
        x = -0.000125 + 0.9999 * jax.random.normal(jax.random.fold_in(_rk, 1), (8, 256, 256), jnp.float32)
        _lenS = 256 - jax.random.randint(jax.random.fold_in(_rk, 7), (8,), 0, max(1, 256 // 4) + 1, jnp.int32)
        _lenS2 = 256 - jax.random.randint(jax.random.fold_in(_rk, 8), (8,), 0, max(1, 256 // 4) + 1, jnp.int32)
        _ctx_1024P = jax.random.normal(jax.random.fold_in(_rk, 11), (8, 16, 256), jnp.float32)
        _ctx_1024c = jax.random.dirichlet(jax.random.fold_in(_rk, 511), 0.3 * jnp.ones((16,), jnp.float32), (8, 256))
        _ctx_1024t = jnp.einsum('bsk,bkd->bsd', _ctx_1024c, _ctx_1024P)
        _ctx_1024t = _ctx_1024t * jax.lax.rsqrt(jnp.mean(jnp.square(_ctx_1024t)) + 1e-12) * 0.953939
        ctx_1024 = -1.52775e-05 + 0.999936 * (_ctx_1024t + 0.3 * jax.random.normal(jax.random.fold_in(_rk, 611), (8, 256, 256), jnp.float32))
        _g = jax.random.normal(jax.random.fold_in(_rk, 9001), (2, 2), jnp.float32)
        _g = jnp.sign(_g) * jnp.maximum(jnp.abs(_g), 1.0) + (_g == 0) * 1.0
        g_xattn = _g[0]
        g_ffn = _g[1]
        return (x, ctx_1024, g_xattn, g_ffn)
    x, ctx_1024, g_xattn, g_ffn = _rec_inputs()

    def _L0_xattn_setup():
        import jax, jax.numpy as jnp
        import numpy as np
        DECAY = 0.9
        key = jax.random.key(seed)
        k1, k2, k3 = jax.random.split(key, 3)
        B, S, D = (8, 1024, 256)
        q = jax.random.normal(k1, (B, S, D), dtype=jnp.float32)
        k = jax.random.normal(k2, (B, S, D), dtype=jnp.float32)
        v = jax.random.normal(k3, (B, S, D), dtype=jnp.float32)
        return {'q': q, 'k': k, 'v': v}
    _L0_xattn_all = _L0_xattn_setup()
    _L0_xattn_in = {k: v for k, v in _L0_xattn_all.items() if k in ()}
    del _L0_xattn_all

    def _L0_ffn_setup():
        import jax, jax.numpy as jnp
        import numpy as np
        E = 32
        H = 256
        I = 128
        G = 8
        TKG = 4
        TOPK = 8
        NSH = 2
        SCALE = 2.5
        key = jax.random.key(seed)
        ks = jax.random.split(key, 10)
        s = 0.02
        return {'hidden_states': jax.random.normal(ks[0], (2, 256, H), jnp.float32), 'gate_w': jax.random.normal(ks[1], (E, H), jnp.float32) * s, 'gate_bias': jax.random.normal(ks[2], (E,), jnp.float32) * s, 'w_gate': jax.random.normal(ks[3], (E, I, H), jnp.float32) * s, 'w_up': jax.random.normal(ks[4], (E, I, H), jnp.float32) * s, 'w_down': jax.random.normal(ks[5], (E, H, I), jnp.float32) * s, 'sh_gate': jax.random.normal(ks[6], (I * NSH, H), jnp.float32) * s, 'sh_up': jax.random.normal(ks[7], (I * NSH, H), jnp.float32) * s, 'sh_down': jax.random.normal(ks[8], (H, I * NSH), jnp.float32) * s}
    _L0_ffn_all = _L0_ffn_setup()
    _L0_ffn_in = {k: v for k, v in _L0_ffn_all.items() if k in ('gate_w', 'gate_bias', 'w_gate', 'w_up', 'w_down', 'sh_gate', 'sh_up', 'sh_down')}
    del _L0_ffn_all

    def _L1_xattn_setup():
        import jax, jax.numpy as jnp
        import numpy as np
        D_MODEL = 256
        N_HEADS = 16
        D_HEAD = D_MODEL // N_HEADS
        WINDOW = 128

        def _heads(x):
            B, S, _ = x.shape
            return x.reshape(B, S, N_HEADS, D_HEAD).transpose(0, 2, 1, 3)
        key = jax.random.key(seed)
        ks = jax.random.split(key, 11)
        B, S = (1, 1024)
        s = 1.0 / np.sqrt(D_MODEL)
        return {'query': jax.random.normal(ks[0], (B, S, D_MODEL), jnp.float32), 'key': jax.random.normal(ks[1], (B, S, D_MODEL), jnp.float32), 'value': jax.random.normal(ks[2], (B, S, D_MODEL), jnp.float32), 'Wq': jax.random.normal(ks[3], (D_MODEL, D_MODEL), jnp.float32) * s, 'bq': jnp.zeros((D_MODEL,), jnp.float32), 'Wk': jax.random.normal(ks[4], (D_MODEL, D_MODEL), jnp.float32) * s, 'bk': jnp.zeros((D_MODEL,), jnp.float32), 'Wv': jax.random.normal(ks[5], (D_MODEL, D_MODEL), jnp.float32) * s, 'bv': jnp.zeros((D_MODEL,), jnp.float32), 'Wo': jax.random.normal(ks[6], (D_MODEL, D_MODEL), jnp.float32) * s, 'bo': jnp.zeros((D_MODEL,), jnp.float32)}
    _L1_xattn_all = _L1_xattn_setup()
    _L1_xattn_in = {k: v for k, v in _L1_xattn_all.items() if k in ('Wq', 'bq', 'Wk', 'bk', 'Wv', 'bv', 'Wo', 'bo')}
    del _L1_xattn_all

    def _L1_ffn_setup():
        import jax, jax.numpy as jnp
        import numpy as np
        D_MODEL = 256
        HIDDEN = 1024
        N_ROUTING = 2
        key = jax.random.key(seed)
        ks = jax.random.split(key, 10)
        s = 0.02
        x = jax.random.normal(ks[0], (4, 1024, D_MODEL), dtype=jnp.float32)
        gate_w = jax.random.normal(ks[1], (N_ROUTING, D_MODEL), dtype=jnp.float32) * s
        w1 = jax.random.normal(ks[2], (N_ROUTING, D_MODEL, HIDDEN), dtype=jnp.float32) * s
        b1 = jax.random.normal(ks[3], (N_ROUTING, HIDDEN), dtype=jnp.float32) * s
        w2 = jax.random.normal(ks[4], (N_ROUTING, HIDDEN, D_MODEL), dtype=jnp.float32) * s
        b2 = jax.random.normal(ks[5], (N_ROUTING, D_MODEL), dtype=jnp.float32) * s
        sw1 = jax.random.normal(ks[6], (D_MODEL, HIDDEN), dtype=jnp.float32) * s
        sb1 = jax.random.normal(ks[7], (HIDDEN,), dtype=jnp.float32) * s
        sw2 = jax.random.normal(ks[8], (HIDDEN, D_MODEL), dtype=jnp.float32) * s
        sb2 = jax.random.normal(ks[9], (D_MODEL,), dtype=jnp.float32) * s
        return {'x': x, 'gate_w': gate_w, 'w1': w1, 'b1': b1, 'w2': w2, 'b2': b2, 'sw1': sw1, 'sb1': sb1, 'sw2': sw2, 'sb2': sb2}
    _L1_ffn_all = _L1_ffn_setup()
    _L1_ffn_in = {k: v for k, v in _L1_ffn_all.items() if k in ('gate_w', 'w1', 'b1', 'w2', 'b2', 'sw1', 'sb1', 'sw2', 'sb2')}
    del _L1_ffn_all
    return {'x': x, 'ctx_1024': ctx_1024, 'g_xattn': g_xattn, 'g_ffn': g_ffn, 'L0_ffn_gate_w': _L0_ffn_in['gate_w'], 'L0_ffn_gate_bias': _L0_ffn_in['gate_bias'], 'L0_ffn_w_gate': _L0_ffn_in['w_gate'], 'L0_ffn_w_up': _L0_ffn_in['w_up'], 'L0_ffn_w_down': _L0_ffn_in['w_down'], 'L0_ffn_sh_gate': _L0_ffn_in['sh_gate'], 'L0_ffn_sh_up': _L0_ffn_in['sh_up'], 'L0_ffn_sh_down': _L0_ffn_in['sh_down'], 'L1_xattn_Wq': _L1_xattn_in['Wq'], 'L1_xattn_bq': _L1_xattn_in['bq'], 'L1_xattn_Wk': _L1_xattn_in['Wk'], 'L1_xattn_bk': _L1_xattn_in['bk'], 'L1_xattn_Wv': _L1_xattn_in['Wv'], 'L1_xattn_bv': _L1_xattn_in['bv'], 'L1_xattn_Wo': _L1_xattn_in['Wo'], 'L1_xattn_bo': _L1_xattn_in['bo'], 'L1_ffn_gate_w': _L1_ffn_in['gate_w'], 'L1_ffn_w1': _L1_ffn_in['w1'], 'L1_ffn_b1': _L1_ffn_in['b1'], 'L1_ffn_w2': _L1_ffn_in['w2'], 'L1_ffn_b2': _L1_ffn_in['b2'], 'L1_ffn_sw1': _L1_ffn_in['sw1'], 'L1_ffn_sb1': _L1_ffn_in['sb1'], 'L1_ffn_sw2': _L1_ffn_in['sw2'], 'L1_ffn_sb2': _L1_ffn_in['sb2']}

def reference(x, ctx_1024, g_xattn, g_ffn, L0_ffn_gate_w, L0_ffn_gate_bias, L0_ffn_w_gate, L0_ffn_w_up, L0_ffn_w_down, L0_ffn_sh_gate, L0_ffn_sh_up, L0_ffn_sh_down, L1_xattn_Wq, L1_xattn_bq, L1_xattn_Wk, L1_xattn_bk, L1_xattn_Wv, L1_xattn_bv, L1_xattn_Wo, L1_xattn_bo, L1_ffn_gate_w, L1_ffn_w1, L1_ffn_b1, L1_ffn_w2, L1_ffn_b2, L1_ffn_sw1, L1_ffn_sb1, L1_ffn_sw2, L1_ffn_sb2):
    import jax
    import jax.numpy as jnp

    def _L0_xattn_ref(q, k, v):
        import jax, jax.numpy as jnp
        import numpy as np
        DECAY = 0.9
        kv = jnp.swapaxes(k * v, 0, 1)

        def step(r, kv_t):
            r = DECAY * r + kv_t
            return (r, r)
        r0 = jnp.zeros(q.shape[:1] + q.shape[2:], dtype=q.dtype)
        _, rs = jax.lax.scan(step, r0, kv)
        return q * jnp.swapaxes(rs, 0, 1)

    def _L0_ffn_ref(hidden_states, gate_w, gate_bias, w_gate, w_up, w_down, sh_gate, sh_up, sh_down):
        import jax, jax.numpy as jnp
        import numpy as np
        E = 32
        H = 256
        I = 128
        G = 8
        TKG = 4
        TOPK = 8
        NSH = 2
        SCALE = 2.5
        B, S, Hd = hidden_states.shape
        h = hidden_states.reshape(-1, Hd)
        logits = h.astype(jnp.float32) @ gate_w.T
        scores = jax.nn.sigmoid(logits)
        sc = scores + gate_bias
        grp = sc.reshape(-1, G, E // G)
        group_scores = jax.lax.top_k(grp, 2)[0].sum(-1)
        gidx = jax.lax.top_k(group_scores, TKG)[1]
        gmask = jnp.sum(jax.nn.one_hot(gidx, G, dtype=sc.dtype), axis=1)
        smask = jnp.repeat(gmask, E // G, axis=1)
        masked = jnp.where(smask > 0, sc, jnp.zeros_like(sc))
        tki = jax.lax.top_k(masked, TOPK)[1]
        tkw = jnp.take_along_axis(scores, tki, axis=1)
        tkw = tkw / (tkw.sum(-1, keepdims=True) + 1e-20)
        tkw = tkw * SCALE
        combine = (jax.nn.one_hot(tki, E, dtype=tkw.dtype) * tkw[..., None]).sum(1)
        g = jax.nn.silu(jnp.einsum('th,eih->tei', h, w_gate))
        u = jnp.einsum('th,eih->tei', h, w_up)
        routed = jnp.einsum('tei,ehi->th', g * u * combine[:, :, None], w_down)
        sg = jax.nn.silu(h @ sh_gate.T)
        shared = sg * (h @ sh_up.T) @ sh_down.T
        return (routed + shared).reshape(B, S, Hd)

    def _L1_xattn_ref(query, key, value, Wq, bq, Wk, bk, Wv, bv, Wo, bo):
        import jax, jax.numpy as jnp
        import numpy as np
        D_MODEL = 256
        N_HEADS = 16
        D_HEAD = D_MODEL // N_HEADS
        WINDOW = 128

        def _heads(x):
            B, S, _ = x.shape
            return x.reshape(B, S, N_HEADS, D_HEAD).transpose(0, 2, 1, 3)
        B, S, _ = query.shape
        q = _heads(query @ Wq.T + bq)
        k = _heads(key @ Wk.T + bk)
        v = _heads(value @ Wv.T + bv)
        scores = jnp.einsum('bhqd,bhkd->bhqk', q, k) / np.sqrt(D_HEAD).astype(np.float32)
        idx = jnp.arange(S)
        local = jnp.abs(idx[:, None] - idx[None, :]) <= WINDOW // 2
        scores = jnp.where(local[None, None, :, :], scores, -jnp.inf)
        attn = jax.nn.softmax(scores, axis=-1)
        ctx = jnp.einsum('bhqk,bhkd->bhqd', attn, v)
        ctx = ctx.transpose(0, 2, 1, 3).reshape(B, S, D_MODEL)
        return ctx @ Wo.T + bo

    def _L1_ffn_ref(x, gate_w, w1, b1, w2, b2, sw1, sb1, sw2, sb2):
        import jax, jax.numpy as jnp
        import numpy as np
        D_MODEL = 256
        HIDDEN = 1024
        N_ROUTING = 2
        B, S, D = x.shape
        xf = x.reshape(-1, D)
        gate_scores = xf @ gate_w.T
        gate_probs = jax.nn.softmax(gate_scores, axis=-1)
        top1 = jnp.argmax(gate_probs, axis=-1)
        one_hot = jax.nn.one_hot(top1, N_ROUTING, dtype=xf.dtype)
        masked = xf[None, :, :] * one_hot.T[:, :, None]
        h = jax.nn.relu(jnp.einsum('end,edh->enh', masked, w1) + b1[:, None, :])
        expert_out = jnp.einsum('enh,ehd->end', h, w2) + b2[:, None, :]
        routing_output = expert_out.sum(axis=0)
        shared = jax.nn.relu(xf @ sw1 + sb1) @ sw2 + sb2
        return (routing_output + shared).reshape(B, S, D)
    x = x + jnp.tanh(g_xattn[0]) * _L0_xattn_ref(_layernorm(x, axis=-1), ctx_1024, ctx_1024)
    x = x + jnp.tanh(g_ffn[0]) * _L0_ffn_ref(_layernorm(x, axis=-1), L0_ffn_gate_w, L0_ffn_gate_bias, L0_ffn_w_gate, L0_ffn_w_up, L0_ffn_w_down, L0_ffn_sh_gate, L0_ffn_sh_up, L0_ffn_sh_down)
    x = x + jnp.tanh(g_xattn[1]) * _L1_xattn_ref(_layernorm(x, axis=-1), ctx_1024, ctx_1024, L1_xattn_Wq, L1_xattn_bq, L1_xattn_Wk, L1_xattn_bk, L1_xattn_Wv, L1_xattn_bv, L1_xattn_Wo, L1_xattn_bo)
    x = x + jnp.tanh(g_ffn[1]) * _L1_ffn_ref(_layernorm(x, axis=-1), L1_ffn_gate_w, L1_ffn_w1, L1_ffn_b1, L1_ffn_w2, L1_ffn_b2, L1_ffn_sw1, L1_ffn_sb1, L1_ffn_sw2, L1_ffn_sb2)
    return x

_drawn_inputs = setup_inputs


def setup_inputs(seed=0):
    import zlib

    import numpy as np

    out = dict(_drawn_inputs(seed))
    spreads = {'g_ffn': (-1.0, 0.6),
     'L1_xattn_bq': (0.0, 2.0),
     'L1_xattn_bk': (0.0, 2.0),
     'L1_xattn_bv': (0.0, 0.8),
     'L1_xattn_bo': (0.0, 0.79)}
    factors = {'L0_ffn_gate_w': 8.0,
     'L0_ffn_gate_bias': 8.0,
     'L0_ffn_w_gate': 8.0,
     'L0_ffn_w_up': 8.0,
     'L0_ffn_w_down': 8.0,
     'L0_ffn_sh_gate': 8.0,
     'L0_ffn_sh_up': 8.0,
     'L0_ffn_sh_down': 8.0,
     'L1_ffn_gate_w': 6.243,
     'L1_ffn_w1': 5.347,
     'L1_ffn_b1': 8.0,
     'L1_ffn_w2': 4.314,
     'L1_ffn_b2': 33.09,
     'L1_ffn_sw1': 5.371,
     'L1_ffn_sb1': 22.791,
     'L1_ffn_sw2': 4.504,
     'L1_ffn_sb2': 42.595,
     'L1_xattn_Wq': 2.702}
    for name, (base, spread) in spreads.items():
        noise = np.random.default_rng([zlib.crc32(name.encode()), seed]).standard_normal(out[name].shape)
        drawn = base * np.exp(spread * noise) if base else spread * noise
        out[name] = jnp.asarray(drawn.astype(out[name].dtype))
    for name, factor in factors.items():
        out[name] = (out[name] * factor).astype(out[name].dtype)
    return out
```

```python
from contextlib import ExitStack

import concourse.bass as bass
from concourse import mybir

F32 = mybir.dt.float32
F16 = mybir.dt.float16
BF16 = mybir.dt.bfloat16
ALU = mybir.AluOpType
ACT = mybir.ActivationFunctionType
AX = mybir.AxisListType
ds = bass.ds

P = 128
B, S, D = 8, 256, 256
TOK = B * S
NT = TOK // P
KC = D // P
CH = 512
NC = TOK // CH
CT = CH // P
E, INNER, GROUPS, TOP_GROUPS, TOP_K = 32, 128, 8, 4, 8
PER_GROUP = E // GROUPS
SHARED = 2
NE = E + SHARED
EW = 3 * D
HEADS, DH, WINDOW = 16, 16, 64
SPAN = P + WINDOW
HIDDEN, SOURCES = 1024, 3
BLOCKS = SOURCES * HIDDEN // P
QD = 2 * D
W1_COLS = BLOCKS * 2 * D
ATT_COLS = KC * (QD + QD + D + D)
REST = W1_COLS + ATT_COLS
PIECES = 16
PW = REST // PIECES
WS = 64.0
EPS = 1e-5
DECAY = 0.9
SCALE = 2.5
NEG = -1e30

R_GX, R_GF, R_BIAS, R_BV, R_BO, R_B2, R_GW = 0, 2, 4, 36, 292, 548, 1316
ROWS = R_GW + 2 * D
C_BQ, C_BK, C_B1, C_GW = 0, 4, 8, 8 + BLOCKS
COLS = C_GW + KC * E


class Count:

    def __init__(self, engine, sem):
        self.engine, self.sem, self.at = engine, sem, 0

    def inc(self, ins):
        ins.then_inc(self.sem, 1)
        self.at = self.at + 1
        return ins

    def wait(self):
        self.engine.wait_ge(self.sem, self.at)


def two_layers(nc, x, ctx_in, ctxT_in, wexp, wrest, rows_in, cols_in, out, upto=4):
    st = ExitStack()
    with st:
        def sb(name, shape, dt=F32):
            return st.enter_context(nc.sbuf_tensor(name, shape, dt))

        def sem(name):
            return st.enter_context(nc.semaphore(name))

        X = sb("X", [P, NT, D])
        TM = sb("TM", [P, NT, D])
        rows = sb("rows", [P, ROWS])
        cols = sb("cols", [P, COLS])
        tg = sb("tg", [P, 4])
        tgw = sb("tgw", [P, 4])
        ident = sb("ident", [P, D])
        identb = sb("identb", [P, P], BF16)
        dec = sb("dec", [P, D])
        decay = sb("decay", [P, D])
        lower = sb("lower", [P, GROUPS, GROUPS])
        halfs = sb("halfs", [P, NT])
        stats = sb("stats", [P, NT, 6])
        mean = sb("mean", [P, NT])
        veps = sb("veps", [P, NT])
        rstd = sb("rstd", [P, NT])
        tA = sb("tA", [P, NT])
        tB = sb("tB", [P, NT])
        tC = sb("tC", [P, NT])
        rt = sb("rt", [P, NT])
        xm = sb("xm", [P, 2, D])
        hT_hi = sb("hT_hi", [P, KC, TOK], F16)
        hT_lo = sb("hT_lo", [P, KC, TOK], F16)
        uT_hi = sb("uT_hi", [P, KC, TOK], F16)
        uT_lo = sb("uT_lo", [P, KC, TOK], F16)
        sT_hi = sb("sT_hi", [P, KC, TOK], F16)
        sT_lo = sb("sT_lo", [P, KC, TOK], F16)
        gw_hi = sb("gw_hi", [P, KC * E], F16)
        gw_lo = sb("gw_lo", [P, KC * E], F16)
        stage = sb("stage", [P, 4, D])
        ew_raw = sb("ew_raw", [P, 2, EW])
        ew_hi = sb("ew_hi", [P, 2, EW], F16)
        ew_lo = sb("ew_lo", [P, 2, EW], F16)
        pc_raw = sb("pc_raw", [P, PW])
        wr_hi = sb("wr_hi", [P, REST], F16)
        wr_lo = sb("wr_lo", [P, REST], F16)
        act_s = sb("act_s", [P, 2, CH])
        prod = sb("prod", [P, 2, CH])
        H_hi = sb("H_hi", [P, 4, CH], F16)
        H_lo = sb("H_lo", [P, 4, CH], F16)
        weight = sb("weight", [P, NE, NT])

        ps = st.enter_context(nc.psum_tensor("ps", [P, 8, 512], F32))

        x_in = [sem(f"x_in{q}") for q in range(4)]
        ctx_loaded = [sem(f"ctx_loaded{q}") for q in range(4)]
        rows_loaded = sem("rows_loaded")
        cols_loaded = sem("cols_loaded")
        ident_ready = sem("ident_ready")
        pool_step = sem("pool_step")
        dve_step = sem("dve_step")
        act_step = sem("act_step")
        consts_ready = sem("consts_ready")
        tanh_ready = sem("tanh_ready")
        decay_ready = sem("decay_ready")
        squares_ready = sem("squares_ready")
        scan_done = sem("scan_done")
        veps_ready = sem("veps_ready")
        rstd_ready = sem("rstd_ready")
        ctxT_loaded = sem("ctxT_loaded")
        logit_tiles = sem("logit_tiles")
        gate_tanh_done = sem("gate_tanh_done")
        gw_split = sem("gw_split")
        router_done = sem("router_done")
        x_out = sem("x_out")

        class Turn:

            def __init__(self, name):
                self.rows_ready = sem(name + "_rows_ready")
                self.turned = sem(name + "_turned")
                self.hi_done = sem(name + "_hi_done")
                self.lo_done = sem(name + "_lo_done")

        turn0 = Turn("turn0")
        ew_loaded = [sem("ew_loaded0"), sem("ew_loaded1")]
        ew_hi_done = [sem("ew_hi_done0"), sem("ew_hi_done1")]
        ew_split = [sem("ew_split0"), sem("ew_split1")]
        pc_loaded = sem("pc_loaded")
        pc_hi_done = sem("pc_hi_done")
        pc_split = sem("pc_split")
        gate_up_done = sem("gate_up_done")
        silu_done = sem("silu_done")
        prod_done = sem("prod_done")
        H_hi_done = sem("H_hi_done")
        H_lo_done = sem("H_lo_done")
        down_done = sem("down_done")
        added = sem("added")

        DOWN_AHEAD, PROD_AHEAD, ADD_AHEAD, ONE = 2, 2, 2, 1
        ctx_hi_done = sem("ctx_hi_done")
        ctx_split = sem("ctx_split")

        def flat(t):
            return t[:, :, :].rearrange("p a n -> p (a n)")

        small_tiles = sb("small_tiles", [P, 8, NT * GROUPS])
        tops = sb("tops", [P, NT, TOP_K])
        maskb = sb("maskb", [P, 2, 2 * SPAN], BF16)
        headsel = sb("headsel", [P, HEADS, P], BF16)
        slot4 = sb("slot4", [P, 4])
        waiter = sb("waiter", [P, 1])
        slotm = sb("slotm", [P, 1])
        tgb = sb("tgb", [P, 2, D])
        nm = sb("nm", [P, 2, HEADS])
        nmT = sb("nmT", [P, 2 * P], BF16)
        rc = sb("rc", [P, 2, HEADS])
        sg = sb("sg", [P, 2, NT])
        sel = sb("sel", [P, 2, NT])
        PT = flat(TM)[:, 0:8 * 2 * SPAN].rearrange("p (n h q) -> p n h q", n=4, h=2)
        V = flat(TM)[:, 8 * 2 * SPAN:8 * 2 * SPAN + 2 * HEADS * (DH + 1)]\
            .rearrange("p (k h d) -> p k h d", k=2, h=HEADS)
        tq = sT_hi[:, 0, :].bitcast(F32)
        tk = sT_hi[:, 1, :].bitcast(F32)
        qh, qs = flat(H_hi)[:, 0:1024], flat(H_hi)[:, 1024:2048]
        kh, kl = flat(H_lo)[:, 0:1024], flat(H_lo)[:, 1024:2048]
        qs_g = qs.rearrange("p (g n) -> p g n", g=4)
        kh_g = kh.rearrange("p (g n) -> p g n", g=4)
        kl_g = kl.rearrange("p (g n) -> p g n", g=4)
        cx = act_s[:, :, 0:D]
        cT_hi = ew_hi[:, 0, 0:KC * 2 * P].rearrange("p (k n) -> p k n", k=KC)
        cT_lo = ew_lo[:, 0, 0:KC * 2 * P].rearrange("p (k n) -> p k n", k=KC)
        A_Q = W1_COLS
        A_K = A_Q + KC * QD
        A_V = A_K + KC * QD
        A_O = A_V + KC * D

        turn1, turn2, turn3 = Turn("turn1"), Turn("turn2"), Turn("turn3")
        att_consts = sem("att_consts")
        bias_rows = sem("bias_rows")
        bias_added = sem("bias_added")
        q_done, k_done, v_done = sem("q_done"), sem("k_done"), sem("v_done")
        tq_done, q_ready, k_ready, v_ready = sem("tq_done"), sem("q_ready"), sem("k_ready"), sem("v_ready")
        rows_done, max_done = sem("rows_done"), sem("max_done")
        nm_turned, nm_ready = sem("nm_turned"), sem("nm_ready")
        sT_done, exp_done, masked, av_done = sem("sT_done"), sem("exp_done"), sem("masked"), sem("av_done")
        cx_ready, cx_turned, c_hi_done, c_split = sem("cx_ready"), sem("cx_turned"), sem("c_hi_done"), sem("c_split")
        o_done, x_added = sem("o_done"), sem("x_added")
        rows3_ready = sem("rows3_ready")
        shared_ready = sem("shared_ready")
        h_done, relu_done, h_hi_done, h_split = sem("h_done"), sem("relu_done"), sem("h_hi_done"), sem("h_split")
        d_done, y_done, y_added = sem("d_done"), sem("y_done"), sem("y_added")
        AV_AHEAD, SPLIT_AHEAD, D_AHEAD = 4, 2, 4

        def tail_sync(sp):
            for c in range(NC):
                sp.wait_ge(y_added, ONE + c + 1)
                sp.dma_start(out[:, CT * c:CT * c + CT, :], X[:, CT * c:CT * c + CT, :]).then_inc(x_out, 16)
            sp.wait_ge(x_out, 16 * NC)

        def band_consts(pool, step):
            step.inc(nc.gpsimd.memset(maskb[:, :, :], 0.0))
            step.inc(nc.gpsimd.memset(headsel[:, :, :], 1.0))
            step.inc(nc.gpsimd.memset(slot4[:, :], 1.0))
            nc.gpsimd.memset(nmT[:, :], 0.0).then_inc(att_consts, 1)
            step.wait()
            for qt in range(2):
                v = maskb[:, qt, :].rearrange("p (h q) -> p h q", h=2)
                step.inc(nc.gpsimd.affine_select(out=v, in_=v, pattern=[[0, 2], [-1, SPAN]],
                                                 base=WINDOW * (1 + qt), channel_multiplier=1,
                                                 compare_op=ALU.is_ge, fill=NEG))
                step.wait()
                step.inc(nc.gpsimd.affine_select(out=v, in_=v, pattern=[[0, 2], [1, SPAN]],
                                                 base=WINDOW * (1 - qt), channel_multiplier=-1,
                                                 compare_op=ALU.is_ge, fill=NEG))
            step.inc(nc.gpsimd.affine_select(out=headsel[:, :, :], in_=headsel[:, :, :],
                                             pattern=[[-1, HEADS], [0, P]], base=0, channel_multiplier=1,
                                             compare_op=ALU.is_equal, fill=0.0))
            step.inc(nc.gpsimd.affine_select(out=slot4[:, :], in_=slot4[:, :], pattern=[[-32, 4]], base=-16,
                                             channel_multiplier=1, compare_op=ALU.is_ge, fill=0.0))
            step.wait()
            nc.gpsimd.affine_select(out=slot4[:, :], in_=slot4[:, :], pattern=[[32, 4]], base=31,
                                    channel_multiplier=-1, compare_op=ALU.is_ge, fill=0.0).then_inc(att_consts, 1)

        def tail_pool(pool, step):
            band_consts(pool, step)
            pool.wait_ge(ctx_split, 1)
            pool.wait_ge(veps_ready, 3)
            nc.gpsimd.tensor_tensor(rstd[:, :], veps[:, :], halfs[:, :], ALU.pow).then_inc(rstd_ready, 1)
            pool.wait_ge(bias_rows, 1)
            pool.wait_ge(turn1.rows_ready, 2 * NC)
            with pool.Fori(0, NT) as t:
                xt = X[:, ds(t, 1), :].rearrange("p a n -> p (a n)")
                nc.gpsimd.tensor_tensor(xt, xt, tgb[:, 0, :], ALU.add).then_inc(bias_added, 1)
            with pool.Fori(0, B) as b:
                for n in range(8):
                    pool.wait_ge(masked, ONE + 8 * b + n)
                    pool.wait_ge(exp_done, ONE + 8 * b + n + 1)
                    nc.gpsimd.tensor_tensor(waiter[:, :], halfs[:, 0:1], halfs[:, 0:1], ALU.add)
                    v = PT[:, n % 4, :, :]

                    def cut(a, size, base, sign):
                        w = v[:, :, a:a + size]
                        return nc.gpsimd.affine_select(out=w, in_=w, pattern=[[0, 2], [-sign, size]], base=base,
                                                       channel_multiplier=sign, compare_op=ALU.is_ge, fill=0.0)

                    cut(0, WINDOW, WINDOW, -1)
                    cut(WINDOW, P, 0, 1)
                    cut(SPAN, P, 0, -1)
                    cut(SPAN + P, WINDOW, 0, 1).then_inc(masked, 1)
            pool.wait_ge(veps_ready, 4)
            nc.gpsimd.tensor_tensor(rstd[:, :], veps[:, :], halfs[:, :], ALU.pow).then_inc(rstd_ready, 1)
            pool.wait_ge(rows3_ready, 1)
            with pool.Fori(0, NT) as t:
                xt = X[:, ds(t, 1), :].rearrange("p a n -> p (a n)")
                nc.gpsimd.tensor_tensor(xt, xt, tgb[:, 1, :], ALU.add).then_inc(bias_added, 1)
            pool.wait_ge(turn3.lo_done, ONE + 2 * NC)
            with pool.Fori(0, NC) as c:
                for k in range(KC):
                    cc = ds(c * CH, CH)
                    nc.gpsimd.tensor_tensor(hT_hi[:, k, cc], sT_hi[:, k, cc], uT_hi[:, k, cc], ALU.add)
                    nc.gpsimd.tensor_tensor(hT_lo[:, k, cc], sT_lo[:, k, cc], uT_lo[:, k, cc], ALU.add)\
                        .then_inc(shared_ready, 1)

        def tail_act(act):
            turn_hi(act, turn1, hT_hi)
            with act.Fori(0, B) as b:
                act.wait_ge(q_done, b + 1)
                act.wait_ge(q_ready, ONE + b)
                for g in range(4):
                    last = nc.scalar.activation(tq[:, g * D:g * D + D], ps[:, g // 2, (g % 2) * D:(g % 2) * D + D],
                                                ACT.Identity, bias=bq4[:, g:g + 1], scale=0.25 / WS)
                last.then_inc(tq_done, 1)
                for n in range(8):
                    act.wait_ge(sT_done, 8 * b + n + 1)
                    act.wait_ge(av_done, AV_AHEAD - 3 + 8 * b + n)
                    a = 2 * (n % 2)
                    nc.scalar.activation(PT[:, n % 4, :, :], ps[:, a:a + 2, 0:2 * SPAN], ACT.Exp).then_inc(exp_done, 1)
                act.wait_ge(cx_turned, b + 1)
                nc.scalar.activation(cT_hi, ps[:, 5, :].rearrange("p (k n) -> p k n", k=KC), ACT.Copy)\
                    .then_inc(c_hi_done, 1)
            turn_hi(act, turn2, sT_hi)
            turn_hi(act, turn3, uT_hi)

            def relus(c):
                for u in range(BLOCKS):
                    n = c * BLOCKS + u
                    act.wait_ge(h_done, n + 1)
                    act.wait_ge(h_split, SPLIT_AHEAD - 1 + n)
                    nc.scalar.activation(act_s[:, u % 2, :], ps[:, u % 2, :], ACT.Relu,
                                         bias=cols[:, C_B1 + u:C_B1 + u + 1], scale=1.0 / WS).then_inc(relu_done, 1)

            with act.Fori(0, NC) as c:
                relus(c)

        bq4 = sb("bq4", [P, 4])

        def tail_dve(dve, step):
            def stats_of_all():
                step.wait()
                dve.wait_ge(added, ADD_AHEAD + PAIRS * UNITS)
                with dve.Fori(0, NT) as t:
                    nc.vector.bn_stats(stats[:, ds(t, 1), :].rearrange("p a n -> p (a n)"),
                                       X[:, ds(t, 1), :].rearrange("p a n -> p (a n)"))
                step.inc(nc.vector.memset(tA[:, :], 0.0))
                step.wait()
                moments(dve, step)

            stats_of_all()
            step.inc(nc.vector.tensor_scalar(bq4[:, :], cols[:, C_BQ:C_BQ + 4], 0.25, None, ALU.mult))
            nc.vector.tensor_scalar(tgb[:, 0, :], rows[:, R_BO:R_BO + D], tg[:, 1:2], None, ALU.mult)
            step.inc(nc.vector.tensor_tensor(tgb[:, 1, :], rows[:, R_B2:R_B2 + D], rows[:, R_B2 + D:R_B2 + 2 * D],
                                             ALU.add))
            step.wait()
            step.inc(nc.vector.tensor_tensor(tgb[:, 1, :], tgb[:, 1, :], rows[:, R_B2 + 2 * D:R_B2 + 3 * D], ALU.add))
            step.wait()
            nc.vector.tensor_scalar(tgb[:, 1, :], tgb[:, 1, :], tg[:, 3:4], None, ALU.mult).then_inc(bias_rows, 1)
            dve.wait_ge(att_consts, 2)
            step.inc(nc.vector.tensor_reduce(slotm[:, :], slot4[:, :], AX.X, ALU.add, negate=True))
            dve.wait_ge(ctx_split, 1)
            step.inc(nc.vector.memset(V[:, :, :, DH], 1.0))
            step.wait()
            dve.wait_ge(rstd_ready, 3)
            turn_rows(dve, turn1, hT_hi, hT_lo)
            dve.wait_ge(bias_added, NT)
            base = step.at
            with dve.Fori(0, B) as b:
                step.at = base + 4 * b
                dve.wait_ge(tq_done, b + 1)
                step.inc(nc.vector.tensor_copy(qh, tq))
                step.wait()
                nc.vector.scalar_tensor_tensor(qs, qh, slotm[:, 0:1], tq, ALU.mult, ALU.add).then_inc(q_ready, 1)
                dve.wait_ge(k_done, b + 1)
                bk = cols[:, C_BK:C_BK + 4].unsqueeze(2).broadcast_to([P, 4, D])
                step.inc(nc.vector.scalar_tensor_tensor(
                    tk.rearrange("p (g n) -> p g n", g=4), ps[:, 2:4, :].rearrange("p a (g n) -> p (a g) n", g=2),
                    1.0 / WS, bk, ALU.mult, ALU.add))
                step.wait()
                step.inc(nc.vector.tensor_copy(kh, tk))
                step.wait()
                nc.vector.tensor_tensor(kl, tk, kh, ALU.subtract).then_inc(k_ready, 1)
                dve.wait_ge(v_done, b + 1)
                bv = rows[:, R_BV:R_BV + D].rearrange("p (h d) -> p h d", h=HEADS)
                for kt in range(2):
                    last = nc.vector.scalar_tensor_tensor(
                        V[:, kt, :, 0:DH], ps[:, 4, kt * D:kt * D + D].rearrange("p (h d) -> p h d", h=HEADS),
                        1.0 / WS, bv, ALU.mult, ALU.add)
                last.then_inc(v_ready, 1)
                for n in range(8):
                    qt, gp, jp = n // 4, (n // 2) % 2, n % 2
                    dve.wait_ge(rows_done, 8 * b + n + 1)
                    a = 2 * (n % 2)
                    o = nm[:, qt, gp * 8 + jp * 4:gp * 8 + jp * 4 + 4].rearrange("p (j g) -> p j g", j=2)
                    nc.vector.tensor_reduce(o, ps[:, a:a + 2, 0:2 * SPAN].rearrange("p a (g q) -> p a g q", g=2),
                                            AX.X, ALU.max, negate=True).then_inc(max_done, 1)
                dve.wait_ge(nm_turned, b + 1)
                nc.vector.tensor_copy(nmT[0:HEADS, :], ps[0:HEADS, 5, 0:2 * P]).then_inc(nm_ready, 1)
                dve.wait_ge(av_done, AV_AHEAD + 8 * b + 8)
                av = ps[:, 6:8, 0:HEADS * (DH + 1)].rearrange("p a (h d) -> p a h d", h=HEADS)
                step.inc(nc.vector.reciprocal(rc[:, :, :], av[:, :, :, DH]))
                step.wait()
                for qt in range(2):
                    last = nc.vector.tensor_tensor(
                        cx[:, qt, :].rearrange("p (h d) -> p h d", h=HEADS), av[:, qt, :, 0:DH],
                        rc[:, qt, :].unsqueeze(2).broadcast_to([P, HEADS, DH]), ALU.mult)
                last.then_inc(cx_ready, 1)
                dve.wait_ge(c_hi_done, b + 1)
                nc.vector.tensor_tensor(cT_lo, ps[:, 5, :].rearrange("p (k n) -> p k n", k=KC), cT_hi,
                                        ALU.subtract).then_inc(c_split, 1)
                dve.wait_ge(o_done, b + 1)
                xb = X[:, ds(2 * b, 2), :].rearrange("p a n -> p (a n)")
                nc.vector.scalar_tensor_tensor(xb, ps[:, 4, :], tgw[:, 1:2], xb, ALU.mult, ALU.add)\
                    .then_inc(x_added, 1)
            step.at = base + 4 * B
            dve.wait_ge(x_added, ONE + B)

            stats_of_all()
            dve.wait_ge(rstd_ready, 4)
            with dve.Fori(0, NT) as t:
                nc.vector.tensor_scalar(TM[:, ds(t, 1), :].rearrange("p a n -> p (a n)"),
                                        X[:, ds(t, 1), :].rearrange("p a n -> p (a n)"),
                                        mean[:, ds(t, 1)], rstd[:, ds(t, 1)], ALU.subtract, ALU.mult)
            nc.vector.memset(tA[:, :], 0.0).then_inc(rows3_ready, 1)
            dve.wait_ge(rows3_ready, 1)
            for t in range(NT):
                for e in range(2):
                    last = nc.vector.tensor_tensor_reduce(
                        xm[:, e, :], TM[:, t, :], rows[:, R_GW + e * D:R_GW + e * D + D], 1.0, 0.0, ALU.mult, ALU.add,
                        sg[:, e, t:t + 1])
                step.inc(last)
                step.wait()
            step.inc(nc.vector.tensor_tensor(sel[:, 1, :], sg[:, 1, :], sg[:, 0, :], ALU.is_gt))
            step.wait()
            step.inc(nc.vector.tensor_scalar(sel[:, 0, :], sel[:, 1, :], -1.0, 1.0, ALU.mult, ALU.add))
            step.wait()
            for e, (t_sems, hi, lo) in enumerate(((turn2, sT_hi, sT_lo), (turn3, uT_hi, uT_lo))):
                turn_rows(dve, t_sems, hi, lo, sel[:, e, :])

            dve.wait_ge(bias_added, 2 * NT)
            with dve.Fori(0, NC) as c:
                for u in range(BLOCKS):
                    n = c * BLOCKS + u
                    dve.wait_ge(relu_done, n + 1)
                    dve.wait_ge(d_done, D_AHEAD - 3 + n)
                    nc.vector.tensor_copy(H_hi[:, u % 4, :], act_s[:, u % 2, :]).then_inc(h_hi_done, 1)
                    dve.wait_ge(h_hi_done, n + 1)
                    nc.vector.tensor_tensor(H_lo[:, u % 4, :], act_s[:, u % 2, :], H_hi[:, u % 4, :], ALU.subtract)\
                        .then_inc(h_split, 1)
                dve.wait_ge(d_done, D_AHEAD + BLOCKS * c + BLOCKS)
                for t in range(CT):
                    xt = X[:, ds(CT * c + t, 1), :].rearrange("p a n -> p (a n)")
                    last = nc.vector.scalar_tensor_tensor(xt, ps[:, 4 + t // 2, (t % 2) * D:(t % 2) * D + D],
                                                          tgw[:, 3:4], xt, ALU.mult, ALU.add)
                last.then_inc(y_added, 1)

        def tail_pe(pe):
            pe.wait_ge(added, ADD_AHEAD + PAIRS * UNITS)
            turn_pe(pe, turn1)
            pe.wait_ge(turn1.lo_done, ONE + 2 * NC)
            pe.wait_ge(consts_ready, 1)
            pe.wait_ge(att_consts, 2)
            pe.wait_ge(ctx_split, 1)

            def three(o, a_hi, a_lo, b_hi, b_lo, start, stop):
                nc.tensor.matmul(o, a_hi, b_hi, start=start, stop=False)
                nc.tensor.matmul(o, a_hi, b_lo, start=False, stop=False)
                return nc.tensor.matmul(o, a_lo, b_hi, start=False, stop=stop)

            with pe.Fori(0, B) as b:
                tok = ds(b * S, S)
                pe.wait_ge(exp_done, ONE + 8 * b)
                for bank, at, hi, lo, done in ((0, A_Q, hT_hi, hT_lo, q_done), (2, A_K, uT_hi, uT_lo, k_done)):
                    for g in range(4):
                        o = ps[:, bank + g // 2, (g % 2) * D:(g % 2) * D + D]
                        for k in range(KC):
                            w = ds(at + k * QD + g * P, P) if False else slice(at + k * QD + g * P,
                                                                              at + k * QD + g * P + P)
                            last = three(o, wr_hi[:, w], wr_lo[:, w], hi[:, k, tok], lo[:, k, tok], k == 0, k == KC - 1)
                    last.then_inc(done, 1)
                pe.wait_ge(x_added, ONE + b)
                for kt in range(2):
                    o = ps[:, 4, kt * D:kt * D + D]
                    for k in range(KC):
                        w = slice(A_V + k * D, A_V + k * D + D)
                        c = ds(b * S + kt * P, P)
                        last = three(o, uT_hi[:, k, c], uT_lo[:, k, c], wr_hi[:, w], wr_lo[:, w], k == 0, k == KC - 1)
                last.then_inc(v_done, 1)

                pe.wait_ge(q_ready, ONE + b + 1)
                pe.wait_ge(k_ready, b + 1)
                for n in range(8):
                    qt, gp, jp = n // 4, (n // 2) % 2, n % 2
                    if n >= 2:
                        pe.wait_ge(max_done, 8 * b + n - 1)
                    for jj in range(2):
                        bank = 2 * (n % 2) + jj
                        j = 2 * jp + jj
                        sl = slice(32 * j, 32 * j + 32)
                        nc.tensor.matmul(ps[:, bank, 0:2 * SPAN], identb[:, :], maskb[:, qt, :], start=True,
                                         stop=False, skip_group_check=True)
                        for gg in range(2):
                            last = nc.tensor.matmul(
                                ps[:, bank, gg * SPAN:gg * SPAN + SPAN],
                                qs_g[sl, 2 * gp + gg, qt * P:qt * P + P],
                                kh_g[sl, 2 * gp + gg, qt * WINDOW:qt * WINDOW + SPAN],
                                start=False, stop=(gg == 1), skip_group_check=True)
                    last.then_inc(rows_done, 1)
                pe.wait_ge(max_done, 8 * b + 8)
                pe.wait_ge(c_split, ONE + b)
                for qt in range(2):
                    last = nc.tensor.transpose(ps[0:HEADS, 5, qt * P:qt * P + P], nm[:, qt, :], ident[:, 0:P])
                last.then_inc(nm_turned, 1)
                pe.wait_ge(nm_ready, b + 1)

                def scores_T(n):
                    g, jp = n // 2, n % 2
                    if n >= 2:
                        pe.wait_ge(exp_done, ONE + 8 * b + n - 1)
                    for jj in range(2):
                        j = 2 * jp + jj
                        bank = 2 * (n % 2) + jj
                        at_h = (g // 2) * 8 + j * 2 + g % 2
                        sl = slice(32 * j, 32 * j + 32)
                        for kt in range(2):
                            o = ps[:, bank, kt * SPAN:kt * SPAN + SPAN]
                            q = qs_g[sl, g, kt * WINDOW:kt * WINDOW + SPAN]
                            kk = slice(kt * P, kt * P + P)
                            nc.tensor.matmul(o, headsel[:, at_h, :], nmT[:, kt * WINDOW:kt * WINDOW + SPAN],
                                             start=True, stop=False)
                            nc.tensor.matmul(o, kh_g[sl, g, kk], q, start=False, stop=False)
                            last = nc.tensor.matmul(o, kl_g[sl, g, kk], q, start=False, stop=True)
                    last.then_inc(sT_done, 1)

                def values(n):
                    g, jp = n // 2, n % 2
                    pe.wait_ge(masked, ONE + 8 * b + n + 1)
                    for jj in range(2):
                        h = 4 * g + 2 * jp + jj
                        w = slice(h * (DH + 1), (h + 1) * (DH + 1))
                        p = PT[:, n % 4, jj, :]
                        nc.tensor.matmul(ps[:, 6, w], p[:, 0:P], V[:, 0, h, :], start=True, stop=False,
                                         skip_group_check=True)
                        nc.tensor.matmul(ps[WINDOW:P, 6, w], p[:, SPAN:SPAN + WINDOW], V[:, 1, h, :], start=False,
                                         stop=True, skip_group_check=True)
                        nc.tensor.matmul(ps[:, 7, w], p[:, SPAN + WINDOW:2 * SPAN], V[:, 1, h, :], start=True,
                                         stop=False, skip_group_check=True)
                        last = nc.tensor.matmul(ps[0:WINDOW, 7, w], p[:, P:SPAN], V[:, 0, h, :], start=False,
                                                stop=True, skip_group_check=True)
                    last.then_inc(av_done, 1)

                scores_T(0)
                scores_T(1)
                pe.wait_ge(v_ready, b + 1)
                pe.wait_ge(cx_ready, ONE + b)
                for n in range(8):
                    if n < 6:
                        scores_T(n + 2)
                    values(n)
                pe.wait_ge(cx_ready, ONE + b + 1)
                for k in range(KC):
                    for qt in range(2):
                        last = nc.tensor.transpose(ps[:, 5, k * 2 * P + qt * P:k * 2 * P + qt * P + P],
                                                   cx[:, qt, k * P:k * P + P], ident[:, 0:P])
                last.then_inc(cx_turned, 1)
                pe.wait_ge(c_split, ONE + b + 1)
                for qt in range(2):
                    o = ps[:, 4, qt * D:qt * D + D]
                    for k in range(KC):
                        w = slice(A_O + k * D, A_O + k * D + D)
                        c = slice(qt * P, qt * P + P)
                        last = three(o, cT_hi[:, k, c], cT_lo[:, k, c], wr_hi[:, w], wr_lo[:, w], k == 0, k == KC - 1)
                last.then_inc(o_done, 1)

            turn_pe(pe, turn2)
            turn_pe(pe, turn3)
            pe.wait_ge(turn3.lo_done, ONE + 2 * NC)
            sources = ((sT_hi, sT_lo), (uT_hi, uT_lo), (hT_hi, hT_lo))

            def hidden(c, u):
                hi, lo = sources[u // (HIDDEN // P)]
                n = c * BLOCKS + u
                if not isinstance(n, int) or n >= 2:
                    pe.wait_ge(relu_done, n - 1)
                if u == 2 * HIDDEN // P:
                    pe.wait_ge(shared_ready, KC * (c + 1))
                o = ps[:, u % 2, :]
                for k in range(KC):
                    a = u * 2 * D + k * P
                    cc = ds(c * CH, CH)
                    last = three(o, wr_hi[:, a:a + P], wr_lo[:, a:a + P], hi[:, k, cc], lo[:, k, cc], k == 0,
                                 k == KC - 1)
                last.then_inc(h_done, 1)

            def second(c, u):
                n = c * BLOCKS + u
                pe.wait_ge(h_split, SPLIT_AHEAD + n + 1)
                if u == 0:
                    pe.wait_ge(y_added, ONE + c)
                w = slice(u * 2 * D + D, (u + 1) * 2 * D)
                for t in range(CT):
                    o = ps[:, 4 + t // 2, (t % 2) * D:(t % 2) * D + D]
                    c4 = slice(t * P, t * P + P)
                    hi, lo = H_hi[:, u % 4, c4], H_lo[:, u % 4, c4]
                    nc.tensor.matmul(o, hi, wr_hi[:, w], start=(u == 0 and t % 2 == 0), stop=False,
                                     skip_group_check=True)
                    nc.tensor.matmul(o, hi, wr_lo[:, w], start=False, stop=False, skip_group_check=True)
                    last = nc.tensor.matmul(o, lo, wr_hi[:, w], start=False, stop=(u == BLOCKS - 1),
                                            skip_group_check=True)
                last.then_inc(d_done, 1)

            hidden(0, 0)
            hidden(0, 1)
            with pe.Fori(0, NC - 1) as c:
                for u in range(BLOCKS):
                    hidden(c, u + 2) if u + 2 < BLOCKS else hidden(c + 1, u + 2 - BLOCKS)
                    second(c, u)
            for u in range(BLOCKS):
                if u + 2 < BLOCKS:
                    hidden(NC - 1, u + 2)
                second(NC - 1, u)

        block = st.enter_context(nc.Block())
        PAIRS = NE // 2
        UNITS = 2 * NC

        def gate_col(e_reg, t):
            return weight[:, ds(e_reg, 1), t]

        def turn_hi(act, t, hi):
            with act.Fori(0, NC) as i:
                for p in range(2):
                    act.wait_ge(t.turned, ONE + 2 * i + p + 1)
                    nc.scalar.activation(hi[:, :, ds(CH * i + p * 2 * P, 2 * P)],
                                         ps[:, p, :].rearrange("p (k n) -> p k n", k=KC), ACT.Copy)\
                        .then_inc(t.hi_done, 1)

        def turn_rows(dve, t, hi, lo, scale_by=None):
            with dve.Fori(0, NC) as i:
                for p in range(2):
                    dve.wait_ge(t.turned, ONE + 2 * i)
                    for h in range(2):
                        c = 4 * i + 2 * p + h
                        if scale_by is None:
                            last = nc.vector.tensor_scalar(
                                stage[:, 2 * p + h, :], X[:, ds(c, 1), :].rearrange("p a n -> p (a n)"),
                                mean[:, ds(c, 1)], rstd[:, ds(c, 1)], ALU.subtract, ALU.mult)
                        else:
                            last = nc.vector.tensor_scalar(
                                stage[:, 2 * p + h, :], TM[:, ds(c, 1), :].rearrange("p a n -> p (a n)"),
                                scale_by[:, ds(c, 1)], None, ALU.mult)
                    last.then_inc(t.rows_ready, 1)
                for p in range(2):
                    dve.wait_ge(t.hi_done, 2 * i + p + 1)
                    cut = ds(CH * i + p * 2 * P, 2 * P)
                    nc.vector.tensor_tensor(lo[:, :, cut], ps[:, p, :].rearrange("p (k n) -> p k n", k=KC),
                                            hi[:, :, cut], ALU.subtract).then_inc(t.lo_done, 1)

        def turn_pe(pe, t):
            with pe.Fori(0, NC) as i:
                for p in range(2):
                    pe.wait_ge(t.rows_ready, 2 * i + p + 1)
                    pe.wait_ge(t.lo_done, ONE + 2 * i)
                    for k in range(KC):
                        for h in range(2):
                            last = nc.tensor.transpose(ps[:, p, k * 2 * P + h * P:k * 2 * P + h * P + P],
                                                       stage[:, 2 * p + h, k * P:k * P + P], ident[:, 0:P])
                    last.then_inc(t.turned, 1)

        def moments(dve, step):
            v = lambda n: stats[:, :, n]
            step.inc(nc.vector.tensor_tensor(tA[:, :], v(1), v(4), ALU.add))
            step.inc(nc.vector.tensor_tensor(tB[:, :], v(1), v(4), ALU.subtract))
            step.inc(nc.vector.tensor_tensor(tC[:, :], v(2), v(5), ALU.add))
            step.wait()
            nc.vector.tensor_scalar(mean[:, :], tA[:, :], 0.5, None, ALU.mult)
            step.inc(nc.vector.tensor_tensor(tB[:, :], tB[:, :], tB[:, :], ALU.mult))
            step.wait()
            step.inc(nc.vector.scalar_tensor_tensor(tC[:, :], tB[:, :], D / 4.0, tC[:, :], ALU.mult, ALU.add))
            step.wait()
            nc.vector.tensor_scalar(veps[:, :], tC[:, :], 1.0 / D, EPS, ALU.mult, ALU.add).then_inc(veps_ready, 1)

        def router(dve, step):
            N = NT * E
            lg = act_s[:, 0, :]
            score = prod[:, 0, :]
            sc = prod[:, 1, :]
            w = act_s[:, 1, :]
            big = [flat(stage), flat(H_hi).bitcast(F32)]
            small = small_tiles
            dve.wait_ge(gate_tanh_done, 1)
            step.inc(nc.vector.tensor_scalar(score, lg, 0.5, 0.5, ALU.mult, ALU.add))
            step.wait()
            bias = rows[:, R_BIAS:R_BIAS + E].unsqueeze(1).broadcast_to([P, NT, E])
            step.inc(nc.vector.tensor_tensor(sc.rearrange("p (t e) -> p t e", e=E),
                                             score.rearrange("p (t e) -> p t e", e=E), bias, ALU.add))
            step.wait()
            v = sc.rearrange("p (g f) -> p g f", f=PER_GROUP)
            mx1, mn1, mx2, mn2, top, mid, low2, sec = (small[:, n, :] for n in range(8))
            nc.vector.tensor_tensor(mx1, v[:, :, 0], v[:, :, 1], ALU.max)
            nc.vector.tensor_tensor(mn1, v[:, :, 0], v[:, :, 1], ALU.min)
            nc.vector.tensor_tensor(mx2, v[:, :, 2], v[:, :, 3], ALU.max)
            step.inc(nc.vector.tensor_tensor(mn2, v[:, :, 2], v[:, :, 3], ALU.min))
            step.wait()
            nc.vector.tensor_tensor(top, mx1, mx2, ALU.max)
            nc.vector.tensor_tensor(mid, mx1, mx2, ALU.min)
            step.inc(nc.vector.tensor_tensor(low2, mn1, mn2, ALU.max))
            step.wait()
            step.inc(nc.vector.tensor_tensor(sec, mid, low2, ALU.max))
            step.wait()
            step.inc(nc.vector.tensor_tensor(mid, top, sec, ALU.add))
            step.wait()
            gs = mid.rearrange("p (t g) -> p t g", g=GROUPS)
            other = gs.unsqueeze(2).broadcast_to([P, NT, GROUPS, GROUPS])
            own = gs.unsqueeze(3).broadcast_to([P, NT, GROUPS, GROUPS])
            four = lambda a: a[:, 0:NT * GROUPS * GROUPS].rearrange("p (t g j) -> p t g j", g=GROUPS, j=GROUPS)
            low4 = lower[:, :, :].unsqueeze(1).broadcast_to([P, NT, GROUPS, GROUPS])
            nc.vector.tensor_tensor(four(big[0]), other, own, ALU.is_gt)
            step.inc(nc.vector.tensor_tensor(four(big[1]), other, own, ALU.is_ge))
            step.wait()
            step.inc(nc.vector.tensor_tensor(four(big[1]), four(big[1]), low4, ALU.mult))
            step.wait()
            step.inc(nc.vector.tensor_tensor(four(big[0]), four(big[0]), four(big[1]), ALU.max))
            step.wait()
            step.inc(nc.vector.tensor_reduce(mx1.rearrange("p (t g) -> p t g", g=GROUPS), four(big[0]), AX.X, ALU.add))
            step.wait()
            step.inc(nc.vector.tensor_scalar(mn1, mx1, TOP_GROUPS - 0.5, None, ALU.is_lt))
            step.wait()
            keep = mn1.unsqueeze(2).broadcast_to([P, NT * GROUPS, PER_GROUP])
            step.inc(nc.vector.tensor_tensor(v, v, keep, ALU.mult))
            step.wait()
            step.inc(nc.vector.tensor_scalar(sc, sc, 0.0, None, ALU.add))
            step.wait()
            for t in range(NT):
                last = nc.vector.max(tops[:, t, :], sc[:, t * E:t * E + E])
            step.inc(last)
            step.wait()
            for t in range(NT):
                last = nc.vector.match_replace(w[:, t * E:t * E + E], tops[:, t, :], sc[:, t * E:t * E + E], NEG)
            step.inc(last)
            step.wait()
            step.inc(nc.vector.tensor_scalar(w, w, 0.1 * NEG, None, ALU.is_lt))
            step.wait()
            step.inc(nc.vector.tensor_tensor(w, w, score, ALU.mult))
            step.wait()
            w3 = w.rearrange("p (t e) -> p t e", e=E)
            step.inc(nc.vector.tensor_reduce(tA[:, :], w3, AX.X, ALU.add))
            step.wait()
            step.inc(nc.vector.tensor_scalar(tA[:, :], tA[:, :], 1e-20, None, ALU.add))
            step.wait()
            step.inc(nc.vector.reciprocal(tB[:, :], tA[:, :]))
            step.wait()
            step.inc(nc.vector.tensor_scalar(tB[:, :], tB[:, :], tgw[:, 2:3], SCALE, ALU.mult, ALU.mult))
            step.inc(nc.vector.tensor_copy(weight[:, 0:SHARED, :], tgw[:, 2:3].unsqueeze(2).broadcast_to([P, SHARED, NT])))
            step.wait()
            nc.vector.tensor_tensor(weight[:, SHARED:NE, :], w.rearrange("p (t e) -> p e t", e=E),
                                    tB[:, :].unsqueeze(1).broadcast_to([P, E, NT]), ALU.mult).then_inc(router_done, 1)
            dve.wait_ge(router_done, 1)


        @block.sync
        def _(sp):
            sp.dma_start(rows[:, :], rows_in.broadcast_to([P, ROWS])).then_inc(rows_loaded, 16)
            sp.dma_start(cols[:, :], cols_in).then_inc(cols_loaded, 16)
            for q in range(4):
                sp.dma_start(TM[:, 4 * q:4 * q + 4, :], ctx_in[:, 4 * q:4 * q + 4, :]).then_inc(ctx_loaded[q], 16)
                sp.dma_start(X[:, 4 * q:4 * q + 4, :], x[:, 4 * q:4 * q + 4, :]).then_inc(x_in[q], 16)
            for k in range(2):
                sp.dma_start(ew_raw[:, k, :], wexp[k, :, :]).then_inc(ew_loaded[k], 16)
            sp.wait_ge(scan_done, B)
            sp.dma_start(TM[:, :, :].rearrange("p a n -> p (a n)"), ctxT_in).then_inc(ctxT_loaded, 16)
            with sp.Fori(0, PAIRS - 1) as i:
                sp.wait_ge(pc_split, ONE + i)
                sp.dma_start(pc_raw[:, :], wrest[:, ds(i * PW, PW)]).then_inc(pc_loaded, 16)
                sp.wait_ge(ew_split[0], i + 1)
                sp.dma_start(ew_raw[:, 0, :], wexp[ds(2 * i + 2, 1), :, :].rearrange("a p n -> p (a n)"))\
                    .then_inc(ew_loaded[0], 16)
                sp.wait_ge(ew_split[1], i + 1)
                sp.dma_start(ew_raw[:, 1, :], wexp[ds(2 * i + 3, 1), :, :].rearrange("a p n -> p (a n)"))\
                    .then_inc(ew_loaded[1], 16)
            tail_sync(sp)

        @block.gpsimd
        def _(pool):
            step = Count(pool, pool_step)
            pool.sem_inc(masked, ONE)
            step.inc(nc.gpsimd.memset(ident[:, :], 0.0))
            step.wait()
            nc.gpsimd.affine_select(out=ident[:, 0:P], in_=ident[:, 0:P], pattern=[[-1, P]], base=0,
                                    channel_multiplier=1, compare_op=ALU.not_equal, fill=1.0).then_inc(ident_ready, 1)
            nc.gpsimd.memset(halfs[:, :], -0.5)
            step.inc(nc.gpsimd.memset(lower[:, :, :], 1.0))
            step.wait()
            step.inc(nc.gpsimd.affine_select(out=lower[:, :, :], in_=lower[:, :, :],
                                             pattern=[[1, GROUPS], [-1, GROUPS]], base=0, channel_multiplier=0,
                                             compare_op=ALU.is_gt, fill=0.0))
            step.wait()
            pool.wait_ge(ident_ready, 1)
            nc.gpsimd.tensor_copy(identb[:, :], ident[:, 0:P]).then_inc(consts_ready, 1)
            for n in range(2):
                pool.wait_ge(veps_ready, n + 1)
                nc.gpsimd.tensor_tensor(rstd[:, :], veps[:, :], halfs[:, :], ALU.pow).then_inc(rstd_ready, 1)
            with pool.Fori(0, PAIRS) as i:
                for u in range(UNITS):
                    n = i * UNITS + u
                    pool.wait_ge(H_hi_done, n + 1)
                    nc.gpsimd.tensor_tensor(H_lo[:, u % 4, :], prod[:, u % 2, :], H_hi[:, u % 4, :], ALU.subtract)\
                        .then_inc(H_lo_done, 1)
            tail_pool(pool, step)

        @block.scalar
        def _(act):
            act.sem_inc(exp_done, ONE)
            act.wait_ge(rows_loaded, 16)
            nc.scalar.activation(tg[:, :], rows[:, R_GX:R_GX + 4], ACT.Tanh).then_inc(tanh_ready, 1)
            for q in range(4):
                act.wait_ge(ctx_loaded[q], 16)
                nc.scalar.activation(TM[:, 4 * q:4 * q + 4, :], TM[:, 4 * q:4 * q + 4, :], ACT.Square)\
                    .then_inc(squares_ready, 1)
            act.wait_ge(cols_loaded, 16)
            nc.scalar.activation(gw_hi[:, :], cols[:, C_GW:C_GW + KC * E], ACT.Copy, scale=WS).then_inc(gw_split, 1)
            turn_hi(act, turn0, hT_hi)
            act.wait_ge(logit_tiles, NT)
            nc.scalar.activation(act_s[:, 0, :], ps[:, 4, :], ACT.Tanh, scale=0.5 / WS).then_inc(gate_tanh_done, 1)

            def weights_hi(k, n):
                act.wait_ge(ew_loaded[k], 16 * n + 16)
                act.wait_ge(down_done, DOWN_AHEAD + done_before[k](n))
                nc.scalar.activation(ew_hi[:, k, :], ew_raw[:, k, :], ACT.Copy, scale=WS).then_inc(ew_hi_done[k], 1)

            done_before = [lambda n: UNITS * n - NC, lambda n: UNITS * n]
            act.wait_ge(ew_loaded[0], 16)
            nc.scalar.activation(ew_hi[:, 0, :], ew_raw[:, 0, :], ACT.Copy, scale=WS).then_inc(ew_hi_done[0], 1)

            act.wait_ge(router_done, 1)

            def silu_pair(i, last):
                for u in range(UNITS):
                    n = i * UNITS + u
                    act.wait_ge(gate_up_done, n + 1)
                    act.wait_ge(prod_done, PROD_AHEAD - 1 + n)
                    nc.scalar.activation(act_s[:, u % 2, :], ps[:, u % 2, :], ACT.Silu, scale=1.0 / WS)\
                        .then_inc(silu_done, 1)
                    if u == 1:
                        weights_hi(1, i)
                    if u == 3 and last:
                        act.wait_ge(ctxT_loaded, 16)
                        nc.scalar.activation(flat(uT_hi), flat(TM), ACT.Copy).then_inc(ctx_hi_done, 1)
                    if u == 3 and not last:
                        act.wait_ge(pc_loaded, 16 * i + 16)
                        nc.scalar.activation(wr_hi[:, ds(i * PW, PW)], pc_raw[:, :], ACT.Copy, scale=WS)\
                            .then_inc(pc_hi_done, 1)
                    if u == 5 and not last:
                        weights_hi(0, i + 1)

            with act.Fori(0, PAIRS - 1) as i:
                silu_pair(i, False)
            silu_pair(PAIRS - 1, True)
            tail_act(act)

        @block.vector
        def _(dve):
            step = Count(dve, dve_step)
            for ahead, by in ((pc_split, ONE), (prod_done, PROD_AHEAD), (added, ADD_AHEAD), (q_ready, ONE),
                              (x_added, ONE), (c_split, ONE), (cx_ready, ONE), (h_split, SPLIT_AHEAD),
                              (y_added, ONE), (turn0.lo_done, ONE), (turn1.lo_done, ONE), (turn2.lo_done, ONE),
                              (turn3.lo_done, ONE)):
                dve.sem_inc(ahead, by)
            nc.vector.memset(dec[:, :], DECAY).then_inc(decay_ready, 1)
            dve.wait_ge(decay_ready, 1)
            dve.wait_ge(ident_ready, 1)
            nc.vector.tensor_tensor_scan(decay[:, :], dec[:, :], ident[:, :], 0.0, ALU.mult, ALU.add)\
                .then_inc(decay_ready, 1)
            dve.wait_ge(tanh_ready, 1)
            step.inc(nc.vector.tensor_scalar(tgw[:, :], tg[:, :], 1.0 / WS, None, ALU.mult))
            for q in range(4):
                dve.wait_ge(x_in[q], 16)
                with dve.Fori(4 * q, 4 * q + 4) as t:
                    nc.vector.bn_stats(stats[:, ds(t, 1), :].rearrange("p a n -> p (a n)"),
                                       X[:, ds(t, 1), :].rearrange("p a n -> p (a n)"))
            step.inc(nc.vector.memset(tA[:, :], 0.0))
            step.wait()
            moments(dve, step)
            dve.wait_ge(rstd_ready, 1)
            step.inc(nc.vector.tensor_scalar(rt[:, :], rstd[:, :], tg[:, 0:1], None, ALU.mult))
            step.wait()
            base = step.at
            with dve.Fori(0, B) as b:
                step.at = base + 4 * b
                for h in range(2):
                    last = nc.vector.tensor_scalar(
                        xm[:, h, :], X[:, ds(2 * b + h, 1), :].rearrange("p a n -> p (a n)"),
                        mean[:, ds(2 * b + h, 1)], rt[:, ds(2 * b + h, 1)], ALU.subtract, ALU.mult)
                step.inc(last)
                dve.wait_ge(scan_done, b + 1)
                step.wait()
                xmf = xm[:, :, :].rearrange("p a n -> p (a n)")
                step.inc(nc.vector.tensor_tensor(xmf, ps[:, ds(b, 1), :].rearrange("p a n -> p (a n)"), xmf, ALU.mult))
                step.wait()
                xb = X[:, ds(2 * b, 2), :].rearrange("p a n -> p (a n)")
                step.inc(nc.vector.tensor_tensor(xb, xmf, xb, ALU.add))
                step.wait()
                for h in range(2):
                    last = nc.vector.bn_stats(stats[:, ds(2 * b + h, 1), :].rearrange("p a n -> p (a n)"),
                                              X[:, ds(2 * b + h, 1), :].rearrange("p a n -> p (a n)"))
                step.inc(last)
            step.at = base + 4 * B
            step.wait()
            moments(dve, step)
            dve.wait_ge(gw_split, 1)
            nc.vector.scalar_tensor_tensor(gw_lo[:, :], cols[:, C_GW:C_GW + KC * E], WS, gw_hi[:, :], ALU.mult,
                                           ALU.subtract).then_inc(gw_split, 1)
            dve.wait_ge(rstd_ready, 2)
            turn_rows(dve, turn0, hT_hi, hT_lo)
            router(dve, step)

            def weights_lo(k, n):
                dve.wait_ge(ew_hi_done[k], n + 1)
                nc.vector.scalar_tensor_tensor(ew_lo[:, k, :], ew_raw[:, k, :], WS, ew_hi[:, k, :], ALU.mult,
                                               ALU.subtract).then_inc(ew_split[k], 1)

            weights_lo(0, 0)

            def gated(n, u):
                dve.wait_ge(silu_done, n + 1)
                if not isinstance(n, int) or n >= 2:
                    dve.wait_ge(H_lo_done, n - 1)
                nc.vector.scalar_tensor_tensor(prod[:, u % 2, :], ps[:, 2 + u % 2, :], 1.0 / WS, act_s[:, u % 2, :],
                                               ALU.mult, ALU.mult).then_inc(prod_done, 1)

            def high(n, u):
                dve.wait_ge(prod_done, PROD_AHEAD + n + 1)
                if not isinstance(n, int) or n >= 2:
                    dve.wait_ge(down_done, DOWN_AHEAD + n - 3)
                nc.vector.tensor_copy(H_hi[:, u % 4, :], prod[:, u % 2, :]).then_inc(H_hi_done, 1)

            def add_down(i, u):
                n = i * UNITS + u
                dve.wait_ge(down_done, DOWN_AHEAD + n + 1)
                for t in range(CT):
                    tile = (u % NC) * CT + t
                    wcol = weight[:, 2 * i + u // NC, tile:tile + 1] if isinstance(i, int) else \
                        weight[:, ds(2 * i + u // NC, 1), tile]
                    last = nc.vector.scalar_tensor_tensor(
                        X[:, tile, :], ps[:, 4 + 2 * (u % 2) + t // 2, (t % 2) * D:(t % 2) * D + D], wcol,
                        X[:, tile, :], ALU.mult, ALU.add)
                last.then_inc(added, 1)

            def dve_pair(i, last):
                for u in range(UNITS):
                    if not (last and u >= UNITS - 2):
                        gated(i * UNITS + u + 2, u)
                        high(i * UNITS + u + 2, u + 2)
                    add_down(i, u)
                    if u == 0:
                        weights_lo(1, i)
                    if u == 2 and last:
                        dve.wait_ge(ctx_hi_done, 1)
                        nc.vector.tensor_tensor(flat(uT_lo), flat(TM), flat(uT_hi), ALU.subtract)\
                            .then_inc(ctx_split, 1)
                    if u == 2 and not last:
                        dve.wait_ge(pc_hi_done, i + 1)
                        nc.vector.scalar_tensor_tensor(wr_lo[:, ds(i * PW, PW)], pc_raw[:, :], WS,
                                                       wr_hi[:, ds(i * PW, PW)], ALU.mult, ALU.subtract)\
                            .then_inc(pc_split, 1)
                    if u == 4 and not last:
                        weights_lo(0, i + 1)

            for n in range(2):
                gated(n, n)
                high(n, n)
            with dve.Fori(0, PAIRS - 1) as i:
                dve_pair(i, False)
            dve_pair(PAIRS - 1, True)
            tail_dve(dve, step)

        @block.tensor
        def _(pe):
            for ahead, by in ((down_done, DOWN_AHEAD), (av_done, AV_AHEAD), (d_done, D_AHEAD), (turn0.turned, ONE),
                              (turn1.turned, ONE), (turn2.turned, ONE), (turn3.turned, ONE)):
                pe.sem_inc(ahead, by)
            pe.wait_ge(decay_ready, 2)
            with pe.Fori(0, B) as b:
                pe.wait_ge(squares_ready, 4)
                sq = lambda h: TM[:, ds(2 * b + h, 1), :].rearrange("p a n -> p (a n)")
                o = lambda h: ps[:, ds(b, 1), h * D:h * D + D].rearrange("p a n -> p (a n)")
                nc.tensor.matmul(o(0), decay[:, 0:P], sq(0), start=True, stop=True)
                nc.tensor.matmul(o(1), decay[:, P:D], sq(0), start=True, stop=False)
                nc.tensor.matmul(o(1), decay[:, 0:P], sq(1), start=False, stop=True).then_inc(scan_done, 1)
            turn_pe(pe, turn0)
            pe.wait_ge(turn0.lo_done, ONE + 2 * NC)
            pe.wait_ge(gw_split, 2)
            with pe.Fori(0, NT) as t:
                o = ps[:, 4, ds(t * E, E)]
                for k in range(KC):
                    hi, lo = hT_hi[:, k, ds(t * P, P)], hT_lo[:, k, ds(t * P, P)]
                    w_hi, w_lo = gw_hi[:, k * E:k * E + E], gw_lo[:, k * E:k * E + E]
                    nc.tensor.matmul(o, hi, w_hi, start=(k == 0), stop=False)
                    nc.tensor.matmul(o, hi, w_lo, start=False, stop=False)
                    last = nc.tensor.matmul(o, lo, w_hi, start=False, stop=(k == KC - 1))
                last.then_inc(logit_tiles, 1)
            pe.wait_ge(router_done, 1)

            def gate_up(i, u):
                buf = (u // NC) % 2
                c = (u % NC) * CH
                n = i * UNITS + u
                if u % NC == 0:
                    pe.wait_ge(ew_split[buf], i + 1 if u < UNITS else i + 2)
                if not isinstance(n, int) or n >= 2:
                    pe.wait_ge(prod_done, PROD_AHEAD + n - 1)
                for which in range(2):
                    o = ps[:, 2 * which + u % 2, :]
                    for k in range(KC):
                        a = which * D + k * P
                        w_hi, w_lo = ew_hi[:, buf, a:a + P], ew_lo[:, buf, a:a + P]
                        nc.tensor.matmul(o, w_hi, hT_hi[:, k, c:c + CH], start=(k == 0), stop=False)
                        nc.tensor.matmul(o, w_hi, hT_lo[:, k, c:c + CH], start=False, stop=False)
                        last = nc.tensor.matmul(o, w_lo, hT_hi[:, k, c:c + CH], start=False, stop=(k == KC - 1))
                last.then_inc(gate_up_done, 1)

            def down(i, u):
                buf = u // NC
                n = i * UNITS + u
                pe.wait_ge(H_lo_done, n + 1)
                pe.wait_ge(added, ADD_AHEAD - 1 + n)
                w_hi, w_lo = ew_hi[:, buf, 2 * D:3 * D], ew_lo[:, buf, 2 * D:3 * D]
                for t in range(CT):
                    o = ps[:, 4 + 2 * (u % 2) + t // 2, (t % 2) * D:(t % 2) * D + D]
                    hi, lo = H_hi[:, u % 4, t * P:t * P + P], H_lo[:, u % 4, t * P:t * P + P]
                    nc.tensor.matmul(o, hi, w_hi, start=True, stop=False)
                    nc.tensor.matmul(o, hi, w_lo, start=False, stop=False)
                    last = nc.tensor.matmul(o, lo, w_hi, start=False, stop=True)
                last.then_inc(down_done, 1)

            gate_up(0, 0)
            gate_up(0, 1)
            with pe.Fori(0, PAIRS - 1) as i:
                for u in range(UNITS):
                    gate_up(i, u + 2)
                    down(i, u)
            for u in range(UNITS):
                if u < UNITS - 2:
                    gate_up(PAIRS - 1, u + 2)
                down(PAIRS - 1, u)
            tail_pe(pe)


_INS = None


def _layout(a):
    import numpy as np

    c = np.ascontiguousarray

    def halves(w):
        return w.reshape(KC, P, -1).transpose(1, 0, 2).reshape(P, -1)

    x = c(a["x"].reshape(NT, P, D).transpose(1, 0, 2))
    ctx = c(a["ctx_1024"].reshape(NT, P, D).transpose(1, 0, 2))
    ctxT = c(halves(a["ctx_1024"].reshape(TOK, D).T))
    experts = []
    for s in range(SHARED):
        cut = slice(s * P, s * P + P)
        experts.append(np.concatenate([halves(a["L0_ffn_sh_gate"][cut].T), halves(a["L0_ffn_sh_up"][cut].T),
                                       a["L0_ffn_sh_down"][:, cut].T], 1))
    for e in range(E):
        experts.append(np.concatenate([halves(a["L0_ffn_w_gate"][e].T), halves(a["L0_ffn_w_up"][e].T),
                                       a["L0_ffn_w_down"][e].T], 1))
    wexp = c(np.stack(experts))
    rest = []
    firsts = [a["L1_ffn_w1"][0], a["L1_ffn_w1"][1], a["L1_ffn_sw1"]]
    seconds = [a["L1_ffn_w2"][0], a["L1_ffn_w2"][1], a["L1_ffn_sw2"]]
    for w1, w2 in zip(firsts, seconds):
        for n in range(HIDDEN // P):
            rest += [halves(w1[:, n * P:n * P + P]), w2[n * P:n * P + P]]
    twice = np.stack([np.arange(D).reshape(HEADS, DH)] * 2, 1).reshape(-1)
    rest += [halves(a["L1_xattn_Wq"].T[:, twice]), halves(a["L1_xattn_Wk"].T[:, twice]),
             halves(a["L1_xattn_Wv"].T), halves(a["L1_xattn_Wo"].T)]
    wrest = c(np.concatenate(rest, 1))
    rows = c(np.concatenate([a["g_xattn"], a["g_ffn"], a["L0_ffn_gate_bias"], a["L1_xattn_bv"], a["L1_xattn_bo"],
                             a["L1_ffn_b2"][0], a["L1_ffn_b2"][1], a["L1_ffn_sb2"],
                             a["L1_ffn_gate_w"].reshape(-1)]).reshape(1, -1))
    b1 = np.concatenate([a["L1_ffn_b1"].reshape(-1), a["L1_ffn_sb1"]]).reshape(BLOCKS, P).T
    cols = c(np.concatenate([a["L1_xattn_bq"][twice].reshape(4, P).T, a["L1_xattn_bk"][twice].reshape(4, P).T, b1,
                             halves(a["L0_ffn_gate_w"].T)], 1))
    return {"x": x, "ctx": ctx, "ctxT": ctxT, "wexp": wexp, "wrest": wrest, "rows": rows, "cols": cols}


def kernel(**inputs):
    import numpy as np
    import concourse.bacc as bacc
    from concourse.bass_utils import run_bass_kernel_spmd

    packed = _layout({k: np.asarray(v) for k, v in inputs.items()})
    nc = bacc.Bacc("TRN2", target_bir_lowering=False, num_devices=1)
    args = [nc.dram_tensor(f"in_{n}", v.shape, F32, kind="ExternalInput").ap() for n, v in packed.items()]
    out = nc.dram_tensor("out_x", [P, NT, D], F32, kind="ExternalOutput").ap()
    two_layers(nc, *args, out)
    r = run_bass_kernel_spmd(nc, [{f"in_{n}": v for n, v in packed.items()}], core_ids=[0])
    return r.results[0]["out_x"].reshape(P, NT, D).transpose(1, 0, 2).reshape(B, S, D)
```

```python
from contextlib import ExitStack

import concourse.bass as bass
from concourse import mybir

F32 = mybir.dt.float32
F16 = mybir.dt.float16
BF16 = mybir.dt.bfloat16
ALU = mybir.AluOpType
ACT = mybir.ActivationFunctionType
AX = mybir.AxisListType
ds = bass.ds

P = 128
B, S, D = 8, 256, 256
TOK = B * S
NT = TOK // P
KC = D // P
CH = 512
NC = TOK // CH
CT = CH // P
E, INNER, GROUPS, TOP_GROUPS, TOP_K = 32, 128, 8, 4, 8
PER_GROUP = E // GROUPS
SHARED = 2
NE = E + SHARED
EW = 3 * D
HEADS, DH, WINDOW = 16, 16, 64
SPAN = P + WINDOW
HIDDEN, SOURCES = 1024, 3
BLOCKS = SOURCES * HIDDEN // P
QD = 2 * D
W1_COLS = BLOCKS * 2 * D
ATT_COLS = KC * (QD + QD + D + D)
REST = W1_COLS + ATT_COLS
PIECES = 16
PW = REST // PIECES
WS = 64.0
EPS = 1e-5
DECAY = 0.9
SCALE = 2.5
NEG = -1e30

R_G, R_BIAS = 0, 4
R_BV = R_BIAS + E
R_BO = R_BV + D
R_B2 = R_BO + D
ROWS = R_B2 + SOURCES * D
C_BQ, C_BK, C_B1 = 0, 4, 8
C_GW = C_B1 + BLOCKS
C_GD = C_GW + KC * E
COLS = C_GD + KC * 2


class Count:

    def __init__(self, engine, sem):
        self.engine, self.sem, self.at = engine, sem, 0

    def inc(self, ins):
        ins.then_inc(self.sem, 1)
        self.at = self.at + 1
        return ins

    def wait(self):
        self.engine.wait_ge(self.sem, self.at)


def since(engine, sem, count):
    if not isinstance(count, int) or count > 0:
        engine.wait_ge(sem, count)


def flat(t):
    return t[:, :, :].rearrange("p a n -> p (a n)")


def one(a):
    return a.rearrange("p a n -> p (a n)")


def two_layers(nc, x, ctx_in, ctxT_in, wexp, wrest, rows_in, cols_in, out):
    st = ExitStack()
    with st:
        def sb(name, shape, dt=F32):
            return st.enter_context(nc.sbuf_tensor(name, shape, dt))

        def sem(name):
            return st.enter_context(nc.semaphore(name))

        PAIRS = NE // 2
        UNITS = 2 * NC
        LAST = PAIRS - 1

        X = sb("X", [P, NT, D])
        TM = sb("TM", [P, NT, D])
        rows = sb("rows", [P, ROWS])
        cols = sb("cols", [P, COLS])
        tg = sb("tg", [P, 4])
        tgw = sb("tgw", [P, 4])
        ident = sb("ident", [P, D])
        identb = sb("identb", [P, P], BF16)
        dec = sb("dec", [P, D])
        decay = sb("decay", [P, D])
        lower = sb("lower", [P, GROUPS, GROUPS])
        halfs = sb("halfs", [P, NT])
        stats = sb("stats", [P, NT, 6])
        mean = sb("mean", [P, NT])
        veps = sb("veps", [P, NT])
        rstd = sb("rstd", [P, NT])
        tA = sb("tA", [P, NT])
        tB = sb("tB", [P, NT])
        tC = sb("tC", [P, NT])
        rt = sb("rt", [P, NT])
        xm = sb("xm", [P, 2, D])
        hT_hi = sb("hT_hi", [P, KC, TOK], F16)
        hT_lo = sb("hT_lo", [P, KC, TOK], F16)
        uT_hi = sb("uT_hi", [P, KC, TOK], F16)
        uT_lo = sb("uT_lo", [P, KC, TOK], F16)
        sT_hi = sb("sT_hi", [P, KC, TOK], F16)
        sT_lo = sb("sT_lo", [P, KC, TOK], F16)
        gw_hi = sb("gw_hi", [P, KC * E], F16)
        gw_lo = sb("gw_lo", [P, KC * E], F16)
        stage = sb("stage", [P, 4, D])
        ew_raw = sb("ew_raw", [P, 2, EW])
        ew_hi = sb("ew_hi", [P, 2, EW], F16)
        ew_lo = sb("ew_lo", [P, 2, EW], F16)
        pc_raw = sb("pc_raw", [P, PW])
        wr_hi = sb("wr_hi", [P, REST], F16)
        wr_lo = sb("wr_lo", [P, REST], F16)
        act_s = sb("act_s", [P, 2, CH])
        prod = sb("prod", [P, 2, CH])
        H_hi = sb("H_hi", [P, 4, CH], F16)
        H_lo = sb("H_lo", [P, 4, CH], F16)
        weight = sb("weight", [P, NE, NT])
        tops = sb("tops", [P, NT, TOP_K])
        maskb = sb("maskb", [P, 2, 2 * SPAN], BF16)
        headsel = sb("headsel", [P, HEADS, P], BF16)
        slot4 = sb("slot4", [P, 4])
        waiter = sb("waiter", [P, 1])
        slotm = sb("slotm", [P, 1])
        bq4 = sb("bq4", [P, 4])
        bkc = sb("bkc", [P, 4])
        tgb = sb("tgb", [P, 2, D])
        nm = sb("nm", [P, 2, HEADS])
        nmT = sb("nmT", [P, 2 * P], BF16)
        rc = sb("rc", [P, 2, HEADS // 2])
        gd = sb("gd", [P, KC])
        gd_hi = sb("gd_hi", [P, KC, P], F16)
        gd_lo = sb("gd_lo", [P, KC, P], F16)

        r_room = wr_lo[:, REST - 8192:REST].bitcast(F32)
        score, sc, w8, lg = (r_room[:, n * 512:n * 512 + 512] for n in range(4))
        cmp_a, cmp_b = r_room[:, 2048:3072], r_room[:, 3072:4096]
        g_room = wr_hi[:, REST - 2048:REST].bitcast(F32).rearrange("p (a n) -> p a n", a=8)
        PT = flat(TM)[:, 0:8 * 2 * SPAN].rearrange("p (n h q) -> p n h q", n=4, h=2)
        HV = DH + 1
        avs = flat(TM)[:, 8 * 2 * SPAN:8 * 2 * SPAN + HEADS * HV].rearrange("p (a h d) -> p a h d", a=2, h=8)
        tq = sT_hi[:, 0, :].bitcast(F32)
        tk = sT_hi[:, 1, :].bitcast(F32)
        P_hi = flat(sT_lo)[:, 0:8 * 2 * SPAN].rearrange("p (n h q) -> p n h q", n=4, h=2)
        qh = flat(sT_lo)[:, 8 * 2 * SPAN:8 * 2 * SPAN + 1024]
        P_lo = flat(ew_raw).bitcast(F16).rearrange("p (n h q) -> p n h q", n=4, h=2)
        qs = [flat(H_hi)[:, n * 1024:n * 1024 + 1024] for n in range(2)]
        kh = [flat(H_lo)[:, n * 1024:n * 1024 + 1024] for n in range(2)]
        kl = [flat(stage).bitcast(F16)[:, n * 1024:n * 1024 + 1024] for n in range(2)]
        V2 = [flat(t)[:, 0:2 * HEADS * 2 * HV].rearrange("p (n d) -> p n d", d=2 * HV) for t in (ew_hi, ew_lo)]
        vt = prod[:, 1, :]
        cT = prod[:, 0, :].bitcast(F16).rearrange("p (s k n) -> p s k n", s=2, k=KC)
        cT_hi, cT_lo = cT[:, 0, :, :], cT[:, 1, :, :]
        cx = act_s[:, :, 0:D]
        A_Q = W1_COLS
        A_K = A_Q + KC * QD
        A_V = A_K + KC * QD
        A_O = A_V + KC * D
        s0_hi, s0_lo, s1_hi, s1_lo = (t[:, :, 0:CH] for t in (sT_hi, sT_lo, uT_hi, uT_lo))
        second_mask = sT_hi[:, 0, CH:2 * CH]

        ps = st.enter_context(nc.psum_tensor("ps", [P, 8, 512], F32))

        x_in = [sem(f"x_in{q}") for q in range(4)]
        ctx_loaded = [sem(f"ctx_loaded{q}") for q in range(4)]
        rows_loaded, cols_loaded, ctxT_loaded = sem("rows_loaded"), sem("cols_loaded"), sem("ctxT_loaded")
        ident_ready, consts_ready, att_consts = sem("ident_ready"), sem("consts_ready"), sem("att_consts")
        pool_step, dve_step = sem("pool_step"), sem("dve_step")
        tanh_ready, decay_ready, squares_ready = sem("tanh_ready"), sem("decay_ready"), sem("squares_ready")
        scan_done, veps_ready, rstd_ready = sem("scan_done"), sem("veps_ready"), sem("rstd_ready")
        logits_done, gate_tanh_done, gw_split = sem("logits_done"), sem("gate_tanh_done"), sem("gw_split")
        router_done, weight_ready, x_out = sem("router_done"), sem("weight_ready"), sem("x_out")

        class Turn:

            def __init__(self, name):
                self.rows_ready = sem(name + "_rows_ready")
                self.turned = sem(name + "_turned")
                self.hi_done = sem(name + "_hi_done")
                self.lo_done = sem(name + "_lo_done")

        turns = [Turn(f"turn{n}") for n in range(3)]
        ew_loaded = [sem("ew_loaded0"), sem("ew_loaded1")]
        ew_hi_done = [sem("ew_hi_done0"), sem("ew_hi_done1")]
        ew_split = [sem("ew_split0"), sem("ew_split1")]
        pc_loaded, pc_hi_done, pc_split = sem("pc_loaded"), sem("pc_hi_done"), sem("pc_split")
        gate_up_done, silu_done, prod_done = sem("gate_up_done"), sem("silu_done"), sem("prod_done")
        H_hi_done, H_lo_done = sem("H_hi_done"), sem("H_lo_done")
        down_done, added = sem("down_done"), sem("added")
        ctx_hi_done, ctx_split = sem("ctx_hi_done"), sem("ctx_split")
        bias_rows, bias_added = sem("bias_rows"), sem("bias_added")
        q_done, k_done, v_done = sem("q_done"), sem("k_done"), sem("v_done")
        tq_done, tk_done, kh_done = sem("tq_done"), sem("tk_done"), sem("kh_done")
        q_ready, k_ready, v_ready = sem("q_ready"), sem("k_ready"), sem("v_ready")
        rows_done, max_done = sem("rows_done"), sem("max_done")
        nm_turned, nm_ready = sem("nm_turned"), sem("nm_ready")
        sT_done, exp_done, masked = sem("sT_done"), sem("exp_done"), sem("masked")
        p_hi_done, p_split, av_done, av_read = sem("p_hi_done"), sem("p_split"), sem("av_done"), sem("av_read")
        cx_ready, cx_turned, c_hi_done, c_split = sem("cx_ready"), sem("cx_turned"), sem("c_hi_done"), sem("c_split")
        o_done, x_added = sem("o_done"), sem("x_added")
        gd_ready, diff_done, mask_ready, sources_ready = \
            sem("gd_ready"), sem("diff_done"), sem("mask_ready"), sem("sources_ready")
        h_done, relu_done, h_hi_done, h_split = sem("h_done"), sem("relu_done"), sem("h_hi_done"), sem("h_split")
        d_done, y_added = sem("d_done"), sem("y_added")

        MASKED_AHEAD, SPLIT_AHEAD, D_AHEAD, Y_AHEAD = 1, 2, 4, 1

        block = st.enter_context(nc.Block())

        @block.sync
        def _(sp):
            sp.dma_start(rows[:, :], rows_in.broadcast_to([P, ROWS])).then_inc(rows_loaded, 16)
            for q in range(4):
                sp.dma_start(X[:, 4 * q:4 * q + 4, :], x[:, 4 * q:4 * q + 4, :]).then_inc(x_in[q], 16)
            for q in range(4):
                sp.dma_start(TM[:, 4 * q:4 * q + 4, :], ctx_in[:, 4 * q:4 * q + 4, :]).then_inc(ctx_loaded[q], 16)
            sp.dma_start(cols[:, :], cols_in).then_inc(cols_loaded, 16)
            for k in range(2):
                sp.dma_start(ew_raw[:, k, :], wexp[k, :, :]).then_inc(ew_loaded[k], 16)
            sp.dma_start(pc_raw[:, :], wrest[:, 0:PW]).then_inc(pc_loaded, 16)
            sp.wait_ge(scan_done, B)
            sp.dma_start(flat(TM), ctxT_in).then_inc(ctxT_loaded, 16)

            def next_experts(i):
                for k in range(2):
                    sp.wait_ge(ew_split[k], i + 1)
                    sp.dma_start(ew_raw[:, k, :], one(wexp[ds(2 * i + 2 + k, 1), :, :].rearrange("a p n -> p a n")))\
                        .then_inc(ew_loaded[k], 16)

            with sp.Fori(0, PIECES - 1) as i:
                next_experts(i)
                sp.wait_ge(pc_split, i + 1)
                sp.dma_start(pc_raw[:, :], wrest[:, ds((i + 1) * PW, PW)]).then_inc(pc_loaded, 16)
            next_experts(LAST - 1)
            for c in range(NC):
                sp.wait_ge(y_added, Y_AHEAD + c + 1)
                sp.dma_start(out[:, CT * c:CT * c + CT, :], X[:, CT * c:CT * c + CT, :]).then_inc(x_out, 16)
            sp.wait_ge(x_out, 16 * NC)

        @block.gpsimd
        def _(pool):
            step = Count(pool, pool_step)
            pool.sem_inc(masked, MASKED_AHEAD)
            step.inc(nc.gpsimd.memset(ident[:, :], 0.0))
            step.wait()
            nc.gpsimd.affine_select(out=ident[:, 0:P], in_=ident[:, 0:P], pattern=[[-1, P]], base=0,
                                    channel_multiplier=1, compare_op=ALU.not_equal, fill=1.0).then_inc(ident_ready, 1)
            nc.gpsimd.memset(halfs[:, :], -0.5)
            step.inc(nc.gpsimd.memset(lower[:, :, :], 1.0))
            step.wait()
            nc.gpsimd.affine_select(out=lower[:, :, :], in_=lower[:, :, :], pattern=[[1, GROUPS], [-1, GROUPS]],
                                    base=0, channel_multiplier=0, compare_op=ALU.is_gt, fill=0.0)
            pool.wait_ge(ident_ready, 1)
            nc.gpsimd.tensor_copy(identb[:, :], ident[:, 0:P]).then_inc(consts_ready, 1)

            def inverse_root(n):
                pool.wait_ge(veps_ready, n)
                nc.gpsimd.tensor_tensor(rstd[:, :], veps[:, :], halfs[:, :], ALU.pow).then_inc(rstd_ready, 1)

            def add_bias(n, normalised):
                pool.wait_ge(normalised.rows_ready, NT // 2)
                with pool.Fori(0, NT) as t:
                    xt = one(X[:, ds(t, 1), :])
                    nc.gpsimd.tensor_tensor(xt, xt, tgb[:, n, :], ALU.add).then_inc(bias_added, 1)

            inverse_root(1)
            inverse_root(2)
            step.inc(nc.gpsimd.memset(maskb[:, :, :], 0.0))
            step.inc(nc.gpsimd.memset(headsel[:, :, :], 1.0))
            step.inc(nc.gpsimd.memset(slot4[:, :], 1.0))
            nc.gpsimd.memset(nmT[:, :], 0.0)
            step.wait()
            for qt in range(2):
                v = maskb[:, qt, :].rearrange("p (h q) -> p h q", h=2)
                step.inc(nc.gpsimd.affine_select(out=v, in_=v, pattern=[[0, 2], [-1, SPAN]],
                                                 base=WINDOW * (1 + qt), channel_multiplier=1,
                                                 compare_op=ALU.is_ge, fill=NEG))
                step.wait()
                step.inc(nc.gpsimd.affine_select(out=v, in_=v, pattern=[[0, 2], [1, SPAN]],
                                                 base=WINDOW * (1 - qt), channel_multiplier=-1,
                                                 compare_op=ALU.is_ge, fill=NEG))
            step.inc(nc.gpsimd.affine_select(out=headsel[:, :, :], in_=headsel[:, :, :],
                                             pattern=[[-1, HEADS], [0, P]], base=0, channel_multiplier=1,
                                             compare_op=ALU.is_equal, fill=0.0))
            step.inc(nc.gpsimd.affine_select(out=slot4[:, :], in_=slot4[:, :], pattern=[[-32, 4]], base=-16,
                                             channel_multiplier=1, compare_op=ALU.is_ge, fill=0.0))
            step.wait()
            nc.gpsimd.affine_select(out=slot4[:, :], in_=slot4[:, :], pattern=[[32, 4]], base=31,
                                    channel_multiplier=-1, compare_op=ALU.is_ge, fill=0.0).then_inc(att_consts, 1)

            with pool.Fori(0, PAIRS) as i:
                for u in range(UNITS):
                    pool.wait_ge(H_hi_done, i * UNITS + u + 1)
                    nc.gpsimd.tensor_tensor(H_lo[:, u % 4, :], prod[:, u % 2, :], H_hi[:, u % 4, :], ALU.subtract)\
                        .then_inc(H_lo_done, 1)
            inverse_root(3)
            pool.wait_ge(bias_rows, 1)
            add_bias(0, turns[1])
            with pool.Fori(0, B) as b:
                for n in range(8):
                    pool.wait_ge(masked, MASKED_AHEAD + 8 * b + n)
                    pool.wait_ge(exp_done, 8 * b + n + 1)
                    nc.gpsimd.tensor_tensor(waiter[:, :], halfs[:, 0:1], halfs[:, 0:1], ALU.add)

                    def cut(a, size, base, sign):
                        w = PT[:, n % 4, :, a:a + size]
                        return nc.gpsimd.affine_select(out=w, in_=w, pattern=[[0, 2], [-sign, size]], base=base,
                                                       channel_multiplier=sign, compare_op=ALU.is_ge, fill=0.0)

                    cut(0, WINDOW, WINDOW, -1)
                    cut(WINDOW, P, 0, 1)
                    cut(SPAN, P, 0, -1)
                    cut(SPAN + P, WINDOW, 0, 1).then_inc(masked, 1)
            inverse_root(4)
            add_bias(1, turns[2])

        @block.scalar
        def _(act):
            act.wait_ge(rows_loaded, 16)
            nc.scalar.activation(tg[:, :], rows[:, R_G:R_G + 4], ACT.Tanh).then_inc(tanh_ready, 1)
            for q in range(4):
                act.wait_ge(ctx_loaded[q], 16)
                nc.scalar.activation(TM[:, 4 * q:4 * q + 4, :], TM[:, 4 * q:4 * q + 4, :], ACT.Square)\
                    .then_inc(squares_ready, 1)
            act.wait_ge(cols_loaded, 16)
            nc.scalar.activation(gw_hi[:, :], cols[:, C_GW:C_GW + KC * E], ACT.Copy, scale=WS).then_inc(gw_split, 1)

            def weights_hi(k, n):
                act.wait_ge(ew_loaded[k], 16 * n + 16)
                since(act, down_done, UNITS * n - NC * (1 - k))
                nc.scalar.activation(ew_hi[:, k, :], ew_raw[:, k, :], ACT.Copy, scale=WS).then_inc(ew_hi_done[k], 1)

            weights_hi(0, 0)

            def turn_hi(t):
                for n in range(NT // 2):
                    act.wait_ge(t.turned, n + 1)
                    nc.scalar.activation(hT_hi[:, :, n * 2 * P:(n + 1) * 2 * P],
                                         ps[:, n % 4, :].rearrange("p (k n) -> p k n", k=KC), ACT.Copy)\
                        .then_inc(t.hi_done, 1)

            turn_hi(turns[0])
            act.wait_ge(logits_done, 1)
            nc.scalar.activation(lg, ps[:, 4, :], ACT.Tanh, scale=0.5 / WS).then_inc(gate_tanh_done, 1)

            def silu_pair(i):
                for u in range(UNITS):
                    n = i * UNITS + u
                    act.wait_ge(gate_up_done, n + 1)
                    since(act, prod_done, n - 1)
                    nc.scalar.activation(act_s[:, u % 2, :], ps[:, u % 2, :], ACT.Silu, scale=1.0 / WS)\
                        .then_inc(silu_done, 1)
                    if u == 1:
                        weights_hi(1, i)
                    if u == 3 and i is LAST:
                        act.wait_ge(ctxT_loaded, 16)
                        nc.scalar.activation(flat(uT_hi), flat(TM), ACT.Copy).then_inc(ctx_hi_done, 1)
                    if u == 3 and i is not LAST:
                        act.wait_ge(pc_loaded, 16 * i + 16)
                        nc.scalar.activation(wr_hi[:, ds(i * PW, PW)], pc_raw[:, :], ACT.Copy, scale=WS)\
                            .then_inc(pc_hi_done, 1)
                    if u == 5 and i is not LAST:
                        weights_hi(0, i + 1)

            silu_pair(0)
            with act.Fori(1, LAST) as i:
                silu_pair(i)
            silu_pair(LAST)

            turn_hi(turns[1])

            def query_key(b, par):
                act.wait_ge(q_done, b + 1)
                since(act, q_ready, b)
                for g in range(4):
                    last = nc.scalar.activation(tq[:, g * D:g * D + D], ps[:, g // 2, (g % 2) * D:(g % 2) * D + D],
                                                ACT.Identity, bias=bq4[:, g:g + 1], scale=0.25 / WS)
                last.then_inc(tq_done, 1)
                act.wait_ge(k_done, b + 1)
                since(act, k_ready, b)
                for g in range(4):
                    last = nc.scalar.activation(tk[:, g * D:g * D + D],
                                                ps[:, 2 + g // 2, (g % 2) * D:(g % 2) * D + D],
                                                ACT.Identity, bias=bkc[:, g:g + 1], scale=1.0 / WS)
                last.then_inc(tk_done, 1)
                act.wait_ge(tk_done, b + 1)
                nc.scalar.activation(kh[par], tk, ACT.Copy).then_inc(kh_done, 1)

            def context_hi(b):
                act.wait_ge(cx_turned, b + 1)
                nc.scalar.activation(cT_hi, ps[:, 5, :].rearrange("p (k n) -> p k n", k=KC), ACT.Copy)\
                    .then_inc(c_hi_done, 1)

            def probabilities_hi(b, n):
                act.wait_ge(masked, MASKED_AHEAD + 8 * b + n + 1)
                since(act, av_done, 8 * b + n - 3)
                nc.scalar.activation(P_hi[:, n % 4, :, :], PT[:, n % 4, :, :], ACT.Copy).then_inc(p_hi_done, 1)

            def attend(b, par):
                if b is not 0:
                    context_hi(b - 1)
                if b is not B - 1:
                    query_key(b + 1, 1 - par)
                for n in range(8):
                    act.wait_ge(sT_done, 8 * b + n + 1)
                    since(act, p_split, 8 * b + n - 3)
                    a = 2 * (n % 2)
                    nc.scalar.activation(PT[:, n % 4, :, :], ps[:, a:a + 2, 0:2 * SPAN], ACT.Exp).then_inc(exp_done, 1)
                    if n >= 2:
                        probabilities_hi(b, n - 2)
                probabilities_hi(b, 6)
                probabilities_hi(b, 7)

            act.wait_ge(bias_rows, 1)
            query_key(0, 0)
            attend(0, 0)
            with act.Fori(0, (B - 2) // 2) as i:
                attend(2 * i + 1, 1)
                attend(2 * i + 2, 0)
            attend(B - 1, 1)
            context_hi(B - 1)

            turn_hi(turns[2])
            with act.Fori(0, NC) as c:
                for u in range(BLOCKS):
                    n = c * BLOCKS + u
                    act.wait_ge(h_done, n + 1)
                    act.wait_ge(h_split, SPLIT_AHEAD + n - 1)
                    nc.scalar.activation(act_s[:, u % 2, :], ps[:, u % 2, :], ACT.Relu,
                                         bias=cols[:, C_B1 + u:C_B1 + u + 1], scale=1.0 / WS).then_inc(relu_done, 1)

        @block.vector
        def _(dve):
            step = Count(dve, dve_step)
            dve.sem_inc(h_split, SPLIT_AHEAD)
            dve.sem_inc(y_added, Y_AHEAD)
            nc.vector.memset(dec[:, :], DECAY).then_inc(decay_ready, 1)
            dve.wait_ge(decay_ready, 1)
            dve.wait_ge(ident_ready, 1)
            nc.vector.tensor_tensor_scan(decay[:, :], dec[:, :], ident[:, :], 0.0, ALU.mult, ALU.add)\
                .then_inc(decay_ready, 1)
            dve.wait_ge(tanh_ready, 1)
            step.inc(nc.vector.tensor_scalar(tgw[:, :], tg[:, :], 1.0 / WS, None, ALU.mult))

            def tile_stats(t):
                return nc.vector.bn_stats(stats[:, t, :] if isinstance(t, int) else one(stats[:, ds(t, 1), :]),
                                          X[:, t, :] if isinstance(t, int) else one(X[:, ds(t, 1), :]))

            def moments():
                step.inc(nc.vector.tensor_tensor(tA[:, :], stats[:, :, 1], stats[:, :, 4], ALU.add))
                step.inc(nc.vector.tensor_tensor(tB[:, :], stats[:, :, 1], stats[:, :, 4], ALU.subtract))
                step.inc(nc.vector.tensor_tensor(tC[:, :], stats[:, :, 2], stats[:, :, 5], ALU.add))
                step.wait()
                nc.vector.tensor_scalar(mean[:, :], tA[:, :], 0.5, None, ALU.mult)
                step.inc(nc.vector.tensor_tensor(tB[:, :], tB[:, :], tB[:, :], ALU.mult))
                step.wait()
                step.inc(nc.vector.scalar_tensor_tensor(tC[:, :], tB[:, :], D / 4.0, tC[:, :], ALU.mult, ALU.add))
                step.wait()
                nc.vector.tensor_scalar(veps[:, :], tC[:, :], 1.0 / D, EPS, ALU.mult, ALU.add).then_inc(veps_ready, 1)

            for q in range(4):
                dve.wait_ge(x_in[q], 16)
                for t in range(4 * q, 4 * q + 4):
                    last = tile_stats(t)
            step.inc(last)
            step.wait()
            moments()
            dve.wait_ge(rstd_ready, 1)
            step.inc(nc.vector.tensor_scalar(rt[:, :], rstd[:, :], tg[:, 0:1], None, ALU.mult))
            step.wait()
            base = step.at
            with dve.Fori(0, B) as b:
                step.at = base + 3 * b
                dve.wait_ge(scan_done, b + 1)
                for h in range(2):
                    c = ds(2 * b + h, 1)
                    last = nc.vector.scalar_tensor_tensor(xm[:, h, :], one(X[:, c, :]), mean[:, c],
                                                          one(ps[:, ds(b, 1), h * D:h * D + D]), ALU.subtract, ALU.mult)
                step.inc(last)
                step.wait()
                for h in range(2):
                    c = ds(2 * b + h, 1)
                    last = nc.vector.scalar_tensor_tensor(one(X[:, c, :]), xm[:, h, :], rt[:, c], one(X[:, c, :]),
                                                          ALU.mult, ALU.add)
                step.inc(last)
                step.wait()
                for h in range(2):
                    last = tile_stats(2 * b + h)
                step.inc(last)
            step.at = base + 3 * B
            step.wait()
            moments()
            dve.wait_ge(gw_split, 1)
            nc.vector.scalar_tensor_tensor(gw_lo[:, :], cols[:, C_GW:C_GW + KC * E], WS, gw_hi[:, :], ALU.mult,
                                           ALU.subtract).then_inc(gw_split, 1)

            def turn_rows(t, n):
                since(dve, t.turned, n - 1)
                for h in range(2):
                    c = 2 * n + h
                    last = nc.vector.tensor_scalar(stage[:, 2 * (n % 2) + h, :], X[:, c, :], mean[:, c:c + 1],
                                                   rstd[:, c:c + 1], ALU.subtract, ALU.mult)
                last.then_inc(t.rows_ready, 1)

            def turn(t):
                turn_rows(t, 0)
                turn_rows(t, 1)
                for n in range(NT // 2):
                    if n + 2 < NT // 2:
                        turn_rows(t, n + 2)
                    dve.wait_ge(t.hi_done, n + 1)
                    cut = slice(n * 2 * P, (n + 1) * 2 * P)
                    nc.vector.tensor_tensor(hT_lo[:, :, cut], ps[:, n % 4, :].rearrange("p (k n) -> p k n", k=KC),
                                            hT_hi[:, :, cut], ALU.subtract).then_inc(t.lo_done, 1)

            dve.wait_ge(rstd_ready, 2)
            turn(turns[0])
            nc.vector.tensor_copy(weight[:, 0:SHARED, :], tgw[:, 2:3].unsqueeze(2).broadcast_to([P, SHARED, NT]))\
                .then_inc(weight_ready, 1)

            v4 = sc.rearrange("p (g f) -> p g f", f=PER_GROUP)
            mx1, mn1, mx2, mn2, top, mid, low2, sec = (g_room[:, n, :] for n in range(8))

            def group_scores():
                dve.wait_ge(gate_tanh_done, 1)
                step.inc(nc.vector.tensor_scalar(score, lg, 0.5, 0.5, ALU.mult, ALU.add))
                step.wait()
                step.inc(nc.vector.tensor_tensor(
                    sc.rearrange("p (t e) -> p t e", e=E), score.rearrange("p (t e) -> p t e", e=E),
                    rows[:, R_BIAS:R_BIAS + E].unsqueeze(1).broadcast_to([P, NT, E]), ALU.add))
                step.wait()
                nc.vector.tensor_tensor(mx1, v4[:, :, 0], v4[:, :, 1], ALU.max)
                nc.vector.tensor_tensor(mn1, v4[:, :, 0], v4[:, :, 1], ALU.min)
                nc.vector.tensor_tensor(mx2, v4[:, :, 2], v4[:, :, 3], ALU.max)
                step.inc(nc.vector.tensor_tensor(mn2, v4[:, :, 2], v4[:, :, 3], ALU.min))
                step.wait()
                nc.vector.tensor_tensor(top, mx1, mx2, ALU.max)
                nc.vector.tensor_tensor(mid, mx1, mx2, ALU.min)
                step.inc(nc.vector.tensor_tensor(low2, mn1, mn2, ALU.max))
                step.wait()
                step.inc(nc.vector.tensor_tensor(sec, mid, low2, ALU.max))
                step.wait()
                step.inc(nc.vector.tensor_tensor(mid, top, sec, ALU.add))
                step.wait()

            def four(a):
                return a.rearrange("p (t g j) -> p t g j", g=GROUPS, j=GROUPS)

            def group_ranks():
                gs = mid.rearrange("p (t g) -> p t g", g=GROUPS)
                other = gs.unsqueeze(2).broadcast_to([P, NT, GROUPS, GROUPS])
                own = gs.unsqueeze(3).broadcast_to([P, NT, GROUPS, GROUPS])
                nc.vector.tensor_tensor(four(cmp_a), other, own, ALU.is_gt)
                step.inc(nc.vector.tensor_tensor(four(cmp_b), other, own, ALU.is_ge))
                step.wait()
                step.inc(nc.vector.tensor_tensor(
                    four(cmp_b), four(cmp_b), lower[:, :, :].unsqueeze(1).broadcast_to([P, NT, GROUPS, GROUPS]),
                    ALU.mult))
                step.wait()

            def groups_kept():
                step.inc(nc.vector.tensor_tensor(cmp_a, cmp_a, cmp_b, ALU.max))
                step.wait()
                step.inc(nc.vector.tensor_reduce(mx1.rearrange("p (t g) -> p t g", g=GROUPS), four(cmp_a), AX.X,
                                                 ALU.add))
                step.wait()
                step.inc(nc.vector.tensor_scalar(mn1, mx1, TOP_GROUPS - 0.5, None, ALU.is_lt))
                step.wait()
                step.inc(nc.vector.tensor_tensor(v4, v4, mn1.unsqueeze(2).broadcast_to([P, NT * GROUPS, PER_GROUP]),
                                                 ALU.mult))
                step.wait()
                step.inc(nc.vector.tensor_scalar(sc, sc, 0.0, None, ALU.add))
                step.wait()

            def greatest():
                for t in range(NT):
                    last = nc.vector.max(tops[:, t, :], sc[:, t * E:t * E + E])
                step.inc(last)
                step.wait()

            def struck():
                for t in range(NT):
                    last = nc.vector.match_replace(w8[:, t * E:t * E + E], tops[:, t, :], sc[:, t * E:t * E + E], NEG)
                step.inc(last)
                step.wait()

            def weights():
                step.inc(nc.vector.scalar_tensor_tensor(w8, w8, 0.1 * NEG, score, ALU.is_lt, ALU.mult))
                step.wait()
                step.inc(nc.vector.tensor_reduce(tA[:, :], w8.rearrange("p (t e) -> p t e", e=E), AX.X, ALU.add))
                step.wait()
                step.inc(nc.vector.tensor_scalar(tA[:, :], tA[:, :], 1e-20, None, ALU.add))
                step.wait()
                step.inc(nc.vector.reciprocal(tB[:, :], tA[:, :]))
                step.wait()
                step.inc(nc.vector.tensor_scalar(tB[:, :], tB[:, :], tgw[:, 2:3], SCALE, ALU.mult, ALU.mult))
                step.wait()
                nc.vector.tensor_tensor(weight[:, SHARED:NE, :], w8.rearrange("p (t e) -> p e t", e=E),
                                        tB[:, :].unsqueeze(1).broadcast_to([P, E, NT]), ALU.mult)\
                    .then_inc(weight_ready, 1)
                dve.wait_ge(weight_ready, 2)

            router_parts = (group_scores, group_ranks, groups_kept, greatest, struck, weights)

            def weights_lo(k, n):
                dve.wait_ge(ew_hi_done[k], n + 1)
                nc.vector.scalar_tensor_tensor(ew_lo[:, k, :], ew_raw[:, k, :], WS, ew_hi[:, k, :], ALU.mult,
                                               ALU.subtract).then_inc(ew_split[k], 1)

            def gated(n, u):
                dve.wait_ge(silu_done, n + 1)
                since(dve, H_lo_done, n - 1)
                nc.vector.scalar_tensor_tensor(prod[:, u % 2, :], ps[:, 2 + u % 2, :], 1.0 / WS, act_s[:, u % 2, :],
                                               ALU.mult, ALU.mult).then_inc(prod_done, 1)
                dve.wait_ge(prod_done, n + 1)
                since(dve, down_done, n - 3)
                nc.vector.tensor_copy(H_hi[:, u % 4, :], prod[:, u % 2, :]).then_inc(H_hi_done, 1)

            def add_down(i, u):
                dve.wait_ge(down_done, i * UNITS + u + 1)
                e = 2 * i + u // NC
                for t in range(CT):
                    tile = (u % NC) * CT + t
                    of = weight[:, e, tile:tile + 1] if isinstance(i, int) else weight[:, ds(e, 1), tile]
                    last = nc.vector.scalar_tensor_tensor(
                        X[:, tile, :], ps[:, 4 + 2 * (u % 2) + t // 2, (t % 2) * D:(t % 2) * D + D], of,
                        X[:, tile, :], ALU.mult, ALU.add)
                last.then_inc(added, 1)

            def chunk_stats(u):
                dve.wait_ge(added, LAST * UNITS + u + 1)
                for t in range(CT):
                    last = tile_stats((u % NC) * CT + t)
                return last

            def pair(i):
                for u in range(UNITS):
                    if i is not LAST or u < UNITS - 2:
                        gated(i * UNITS + u + 2, u + 2)
                    add_down(i, u)
                    if u == 0:
                        weights_lo(1, i)
                    if i is 0 and 1 <= u < 7:
                        router_parts[u - 1]()
                    if u == 2 and i is LAST:
                        dve.wait_ge(ctx_hi_done, 1)
                        nc.vector.tensor_tensor(flat(uT_lo), flat(TM), flat(uT_hi), ALU.subtract)\
                            .then_inc(ctx_split, 1)
                    if u == 2 and i is not LAST:
                        dve.wait_ge(pc_hi_done, i + 1)
                        nc.vector.scalar_tensor_tensor(wr_lo[:, ds(i * PW, PW)], pc_raw[:, :], WS,
                                                       wr_hi[:, ds(i * PW, PW)], ALU.mult, ALU.subtract)\
                            .then_inc(pc_split, 1)
                    if u == 4 and i is not LAST:
                        weights_lo(0, i + 1)
                    if i is LAST and u > NC:
                        chunk_stats(u - 1)

            weights_lo(0, 0)
            gated(0, 0)
            gated(1, 1)
            dve.wait_ge(weight_ready, 1)
            pair(0)
            with dve.Fori(1, LAST) as i:
                pair(i)
            pair(LAST)
            step.inc(chunk_stats(UNITS - 1))
            step.wait()
            moments()

            step.inc(nc.vector.tensor_tensor(gd[:, :], cols[:, C_GD + 1:C_GD + 4:2], cols[:, C_GD:C_GD + 3:2],
                                             ALU.subtract))
            step.wait()
            step.inc(nc.vector.tensor_scalar(gd[:, :], gd[:, :], WS, None, ALU.mult))
            step.wait()
            wide = gd[:, :].unsqueeze(2).broadcast_to([P, KC, P])
            step.inc(nc.vector.tensor_copy(gd_hi[:, :, :], wide))
            step.wait()
            nc.vector.tensor_tensor(gd_lo[:, :, :], wide, gd_hi[:, :, :], ALU.subtract).then_inc(gd_ready, 1)
            nc.vector.tensor_scalar(bq4[:, :], cols[:, C_BQ:C_BQ + 4], 0.25, None, ALU.mult)
            nc.vector.tensor_copy(bkc[:, :], cols[:, C_BK:C_BK + 4])
            nc.vector.tensor_scalar(tgb[:, 0, :], rows[:, R_BO:R_BO + D], tg[:, 1:2], None, ALU.mult)
            step.inc(nc.vector.tensor_tensor(tgb[:, 1, :], rows[:, R_B2:R_B2 + D], rows[:, R_B2 + D:R_B2 + 2 * D],
                                             ALU.add))
            step.wait()
            step.inc(nc.vector.tensor_tensor(tgb[:, 1, :], tgb[:, 1, :], rows[:, R_B2 + 2 * D:R_B2 + 3 * D], ALU.add))
            step.wait()
            nc.vector.tensor_scalar(tgb[:, 1, :], tgb[:, 1, :], tg[:, 3:4], None, ALU.mult).then_inc(bias_rows, 1)
            dve.wait_ge(att_consts, 1)
            nc.vector.tensor_reduce(slotm[:, :], slot4[:, :], AX.X, ALU.add, negate=True)
            for par in range(2):
                nc.vector.memset(V2[par][:, :, DH], 1.0)
                last = nc.vector.memset(V2[par][:, :, DH + HV], 0.0)
            step.inc(last)
            step.wait()
            dve.wait_ge(rstd_ready, 3)
            turn(turns[1])

            def split_qkv(b, par):
                dve.wait_ge(tq_done, b + 1)
                step.inc(nc.vector.tensor_copy(qh, tq))
                step.wait()
                nc.vector.scalar_tensor_tensor(qs[par], qh, slotm[:, 0:1], tq, ALU.mult, ALU.add).then_inc(q_ready, 1)
                dve.wait_ge(kh_done, b + 1)
                nc.vector.tensor_tensor(kl[par], tk, kh[par], ALU.subtract).then_inc(k_ready, 1)
                dve.wait_ge(v_done, b + 1)
                step.inc(nc.vector.scalar_tensor_tensor(
                    vt.rearrange("p (k n) -> p k n", k=2), ps[:, 4, :].rearrange("p (k n) -> p k n", k=2), 1.0 / WS,
                    rows[:, R_BV:R_BV + D].unsqueeze(1).broadcast_to([P, 2, D]), ALU.mult, ALU.add))
                step.wait()
                vh = vt.rearrange("p (n d) -> p n d", d=DH)
                step.inc(nc.vector.tensor_copy(V2[par][:, :, 0:DH], vh))
                step.wait()
                nc.vector.tensor_tensor(V2[par][:, :, HV:HV + DH], vh, V2[par][:, :, 0:DH], ALU.subtract)\
                    .then_inc(v_ready, 1)

            def maxima(b, n):
                qt, gp, jp = n // 4, (n // 2) % 2, n % 2
                dve.wait_ge(rows_done, 8 * b + n + 1)
                a = 2 * (n % 2)
                o = nm[:, qt, gp * 8 + jp * 4:gp * 8 + jp * 4 + 4].rearrange("p (j g) -> p j g", j=2)
                nc.vector.tensor_reduce(o, ps[:, a:a + 2, 0:2 * SPAN].rearrange("p a (g q) -> p a g q", g=2),
                                        AX.X, ALU.max, negate=True).then_inc(max_done, 1)

            def context_lo(b):
                dve.wait_ge(c_hi_done, b + 1)
                nc.vector.tensor_tensor(cT_lo, ps[:, 5, :].rearrange("p (k n) -> p k n", k=KC), cT_hi,
                                        ALU.subtract).then_inc(c_split, 1)

            def add_attention(b):
                dve.wait_ge(o_done, b + 1)
                xb = flat(X[:, ds(2 * b, 2), :])
                nc.vector.scalar_tensor_tensor(xb, ps[:, 4, :], tgw[:, 1:2], xb, ALU.mult, ALU.add)\
                    .then_inc(x_added, 1)
                dve.wait_ge(x_added, b + 1)
                tile_stats(2 * b)
                return tile_stats(2 * b + 1)

            def half_context(b, half):
                dve.wait_ge(av_done, 8 * b + 4 * half + 4)
                for qt in range(2):
                    last = nc.vector.tensor_reduce(
                        avs[:, qt, :, :], ps[:, 6 + qt, 0:8 * 2 * HV].rearrange("p (h s d) -> p h d s", h=8, s=2),
                        AX.X, ALU.add)
                last.then_inc(av_read, 1)
                dve.wait_ge(av_read, 2 * b + half + 1)
                step.inc(nc.vector.reciprocal(rc[:, :, :], avs[:, :, :, DH]))
                step.wait()
                for qt in range(2):
                    last = nc.vector.tensor_tensor(
                        cx[:, qt, half * P:half * P + P].rearrange("p (h d) -> p h d", h=8), avs[:, qt, :, 0:DH],
                        rc[:, qt, :].unsqueeze(2).broadcast_to([P, 8, DH]), ALU.mult)
                last.then_inc(cx_ready, 1)

            def probabilities_lo(b, n):
                dve.wait_ge(p_hi_done, 8 * b + n + 1)
                nc.vector.tensor_tensor(P_lo[:, n % 4, :, :], PT[:, n % 4, :, :], P_hi[:, n % 4, :, :], ALU.subtract)\
                    .then_inc(p_split, 1)

            def attend(b, par):
                for n in range(4):
                    maxima(b, n)
                if b is not 0:
                    context_lo(b - 1)
                for n in range(4, 8):
                    maxima(b, n)
                dve.wait_ge(nm_turned, b + 1)
                nc.vector.tensor_copy(nmT[0:HEADS, :], ps[0:HEADS, 5, 0:2 * P]).then_inc(nm_ready, 1)
                if b is not 0:
                    add_attention(b - 1)
                if b is not B - 1:
                    split_qkv(b + 1, 1 - par)
                for half in range(2):
                    for n in range(4 * half, 4 * half + 4):
                        probabilities_lo(b, n)
                    half_context(b, half)

            STEPS = 5
            split_qkv(0, 0)
            dve.wait_ge(bias_added, NT)
            attend(0, 0)
            base = step.at
            with dve.Fori(0, (B - 2) // 2) as i:
                for par in (1, 0):
                    step.at = base + 2 * STEPS * i + STEPS * (1 - par)
                    attend(2 * i + 2 - par, par)
            step.at = base + STEPS * (B - 2)
            attend(B - 1, 1)
            context_lo(B - 1)
            step.inc(add_attention(B - 1))
            step.wait()
            moments()
            dve.wait_ge(rstd_ready, 4)
            turn(turns[2])

            def source(c, n):
                cc = ds(c * CH, CH)
                if n == 0:
                    dve.wait_ge(diff_done, c + 1)
                    nc.vector.tensor_scalar(second_mask, ps[:, 2, :], 0.0, None, ALU.is_gt).then_inc(mask_ready, 1)
                    dve.wait_ge(mask_ready, c + 1)
                if n in (1, 2):
                    mine, of = ((s1_hi, hT_hi), (s1_lo, hT_lo))[n - 1]
                    nc.vector.tensor_tensor(mine, of[:, :, cc], second_mask.unsqueeze(1).broadcast_to([P, KC, CH]),
                                            ALU.mult).then_inc(sources_ready, 1)
                if n in (3, 4):
                    mine, of, other = ((s0_hi, hT_hi, s1_hi), (s0_lo, hT_lo, s1_lo))[n - 3]
                    dve.wait_ge(sources_ready, 4 * c + n - 2)
                    nc.vector.tensor_tensor(mine, of[:, :, cc], other, ALU.subtract).then_inc(sources_ready, 1)

            dve.wait_ge(bias_added, 2 * NT)
            with dve.Fori(0, NC) as c:
                for u in range(BLOCKS):
                    n = c * BLOCKS + u
                    dve.wait_ge(relu_done, n + 1)
                    dve.wait_ge(d_done, D_AHEAD + n - 3)
                    nc.vector.tensor_copy(H_hi[:, u % 4, :], act_s[:, u % 2, :]).then_inc(h_hi_done, 1)
                    dve.wait_ge(h_hi_done, n + 1)
                    nc.vector.tensor_tensor(H_lo[:, u % 4, :], act_s[:, u % 2, :], H_hi[:, u % 4, :], ALU.subtract)\
                        .then_inc(h_split, 1)
                    source(c, u)
                dve.wait_ge(d_done, D_AHEAD + BLOCKS * c + BLOCKS)
                for t in range(CT):
                    xt = one(X[:, ds(CT * c + t, 1), :])
                    last = nc.vector.scalar_tensor_tensor(xt, ps[:, 4 + t // 2, (t % 2) * D:(t % 2) * D + D],
                                                          tgw[:, 3:4], xt, ALU.mult, ALU.add)
                last.then_inc(y_added, 1)

        @block.tensor
        def _(pe):
            pe.sem_inc(d_done, D_AHEAD)

            def three(o, a_hi, a_lo, b_hi, b_lo, start, stop, **kw):
                nc.tensor.matmul(o, a_hi, b_hi, start=start, stop=False, **kw)
                nc.tensor.matmul(o, a_hi, b_lo, start=False, stop=False, **kw)
                return nc.tensor.matmul(o, a_lo, b_hi, start=False, stop=stop, **kw)

            pe.wait_ge(decay_ready, 2)
            for q in range(4):
                pe.wait_ge(squares_ready, q + 1)
                with pe.Fori(2 * q, 2 * q + 2) as b:
                    sq = [one(TM[:, ds(2 * b + h, 1), :]) for h in range(2)]
                    o = [one(ps[:, ds(b, 1), h * D:h * D + D]) for h in range(2)]
                    nc.tensor.matmul(o[0], decay[:, 0:P], sq[0], start=True, stop=True)
                    nc.tensor.matmul(o[1], decay[:, P:D], sq[0], start=True, stop=False)
                    nc.tensor.matmul(o[1], decay[:, 0:P], sq[1], start=False, stop=True).then_inc(scan_done, 1)

            def turn(t):
                for n in range(NT // 2):
                    pe.wait_ge(t.rows_ready, n + 1)
                    since(pe, t.lo_done, n - 3)
                    for k in range(KC):
                        for h in range(2):
                            last = nc.tensor.transpose(ps[:, n % 4, k * 2 * P + h * P:k * 2 * P + h * P + P],
                                                       stage[:, 2 * (n % 2) + h, k * P:k * P + P], ident[:, 0:P])
                    last.then_inc(t.turned, 1)

            turn(turns[0])
            pe.wait_ge(gw_split, 2)
            for t in range(NT):
                if t % 2 == 0:
                    pe.wait_ge(turns[0].lo_done, t // 2 + 1)
                c = slice(t * P, t * P + P)
                for k in range(KC):
                    w = slice(k * E, k * E + E)
                    last = three(ps[:, 4, t * E:t * E + E], hT_hi[:, k, c], hT_lo[:, k, c], gw_hi[:, w], gw_lo[:, w],
                                 k == 0, k == KC - 1)
            last.then_inc(logits_done, 1)

            def gate_up(i, u):
                buf = (u // NC) % 2
                c = slice((u % NC) * CH, (u % NC) * CH + CH)
                if u % NC == 0:
                    pe.wait_ge(ew_split[buf], i + 1 + u // UNITS)
                since(pe, prod_done, i * UNITS + u - 1)
                for which in range(2):
                    for k in range(KC):
                        w = slice(which * D + k * P, which * D + k * P + P)
                        last = three(ps[:, 2 * which + u % 2, :], ew_hi[:, buf, w], ew_lo[:, buf, w],
                                     hT_hi[:, k, c], hT_lo[:, k, c], k == 0, k == KC - 1)
                last.then_inc(gate_up_done, 1)

            def down(i, u):
                buf = u // NC
                n = i * UNITS + u
                pe.wait_ge(H_lo_done, n + 1)
                since(pe, added, n - 1)
                for t in range(CT):
                    c = slice(t * P, t * P + P)
                    last = three(ps[:, 4 + 2 * (u % 2) + t // 2, (t % 2) * D:(t % 2) * D + D],
                                 H_hi[:, u % 4, c], H_lo[:, u % 4, c],
                                 ew_hi[:, buf, 2 * D:3 * D], ew_lo[:, buf, 2 * D:3 * D], True, True)
                last.then_inc(down_done, 1)

            def pair(i):
                for u in range(UNITS):
                    if i is not LAST or u < UNITS - 2:
                        gate_up(i, u + 2)
                    down(i, u)

            gate_up(0, 0)
            gate_up(0, 1)
            pe.wait_ge(gate_tanh_done, 1)
            pair(0)
            with pe.Fori(1, LAST) as i:
                pair(i)
            pair(LAST)

            turn(turns[1])
            pe.wait_ge(turns[1].lo_done, NT // 2)
            pe.wait_ge(consts_ready, 1)
            pe.wait_ge(ctx_split, 1)

            def project(b):
                tok = ds(b * S, S)
                since(pe, max_done, 8 * b)
                for bank, at, hi, lo, done in ((0, A_Q, hT_hi, hT_lo, q_done), (2, A_K, uT_hi, uT_lo, k_done)):
                    for g in range(4):
                        for k in range(KC):
                            w = slice(at + k * QD + g * P, at + k * QD + g * P + P)
                            last = three(ps[:, bank + g // 2, (g % 2) * D:(g % 2) * D + D], wr_hi[:, w], wr_lo[:, w],
                                         hi[:, k, tok], lo[:, k, tok], k == 0, k == KC - 1)
                    last.then_inc(done, 1)
                since(pe, x_added, b - 1)
                for kt in range(2):
                    for k in range(KC):
                        w = slice(A_V + k * D, A_V + k * D + D)
                        c = ds(b * S + kt * P, P)
                        last = three(ps[:, 4, kt * D:kt * D + D], uT_hi[:, k, c], uT_lo[:, k, c], wr_hi[:, w],
                                     wr_lo[:, w], k == 0, k == KC - 1)
                last.then_inc(v_done, 1)

            def by_group(t):
                return t.rearrange("p (g n) -> p g n", g=4)

            def score_rows(b, par, n):
                qt, gp, jp = n // 4, (n // 2) % 2, n % 2
                if n < 2:
                    since(pe, exp_done, 8 * b)
                else:
                    pe.wait_ge(max_done, 8 * b + n - 1)
                for jj in range(2):
                    j = 2 * jp + jj
                    bank = 2 * (n % 2) + jj
                    sl = slice(32 * j, 32 * j + 32)
                    nc.tensor.matmul(ps[:, bank, 0:2 * SPAN], identb[:, :], maskb[:, qt, :], start=True,
                                     stop=False, skip_group_check=True)
                    for gg in range(2):
                        last = nc.tensor.matmul(
                            ps[:, bank, gg * SPAN:gg * SPAN + SPAN],
                            by_group(qs[par])[sl, 2 * gp + gg, qt * P:qt * P + P],
                            by_group(kh[par])[sl, 2 * gp + gg, qt * WINDOW:qt * WINDOW + SPAN],
                            start=False, stop=(gg == 1), skip_group_check=True)
                last.then_inc(rows_done, 1)

            def score_columns(b, par, n):
                g, jp = n // 2, n % 2
                if n >= 2:
                    pe.wait_ge(exp_done, 8 * b + n - 1)
                elif b is not B - 1:
                    pe.wait_ge((tq_done, tk_done)[n], b + 2)
                for jj in range(2):
                    j = 2 * jp + jj
                    bank = 2 * (n % 2) + jj
                    at_h = (g // 2) * 8 + j * 2 + g % 2
                    sl = slice(32 * j, 32 * j + 32)
                    for kt in range(2):
                        o = ps[:, bank, kt * SPAN:kt * SPAN + SPAN]
                        q = by_group(qs[par])[sl, g, kt * WINDOW:kt * WINDOW + SPAN]
                        keys = slice(kt * P, kt * P + P)
                        nc.tensor.matmul(o, headsel[:, at_h, :], nmT[:, kt * WINDOW:kt * WINDOW + SPAN],
                                         start=True, stop=False)
                        nc.tensor.matmul(o, by_group(kh[par])[sl, g, keys], q, start=False, stop=False)
                        last = nc.tensor.matmul(o, by_group(kl[par])[sl, g, keys], q, start=False, stop=True)
                last.then_inc(sT_done, 1)

            def values(b, par, n):
                g, jp = n // 2, n % 2
                pe.wait_ge(p_split, 8 * b + n + 1)
                if n % 4 == 0:
                    since(pe, av_read, 2 * b + n // 4)
                for jj in range(2):
                    h = 4 * g + 2 * jp + jj
                    w = slice((h % 8) * 2 * HV, (h % 8 + 1) * 2 * HV)
                    v = [V2[par][:, kt * HEADS + h, :] for kt in range(2)]
                    for bank, full, q_full, part, q_part, rows_part in (
                            (6, 0, slice(0, P), 1, slice(SPAN, SPAN + WINDOW), slice(WINDOW, P)),
                            (7, 1, slice(SPAN + WINDOW, 2 * SPAN), 0, slice(P, SPAN), slice(0, WINDOW))):
                        for first, p in ((True, P_hi), (False, P_lo)):
                            nc.tensor.matmul(ps[:, bank, w], p[:, n % 4, jj, q_full], v[full], start=first,
                                             stop=False, skip_group_check=True)
                        for end, p in ((False, P_hi), (True, P_lo)):
                            last = nc.tensor.matmul(ps[rows_part, bank, w], p[:, n % 4, jj, q_part], v[part],
                                                    start=False, stop=end, skip_group_check=True)
                last.then_inc(av_done, 1)

            def turn_context(b):
                pe.wait_ge(cx_ready, 2 * b + 2)
                for k in range(KC):
                    for qt in range(2):
                        last = nc.tensor.transpose(ps[:, 5, k * 2 * P + qt * P:k * 2 * P + qt * P + P],
                                                   cx[:, qt, k * P:k * P + P], ident[:, 0:P])
                last.then_inc(cx_turned, 1)

            def project_out(b):
                pe.wait_ge(c_split, b + 1)
                if b is not B - 1:
                    pe.wait_ge(v_ready, b + 2)
                for qt in range(2):
                    for k in range(KC):
                        w = slice(A_O + k * D, A_O + k * D + D)
                        c = slice(qt * P, qt * P + P)
                        last = three(ps[:, 4, qt * D:qt * D + D], cT_hi[:, k, c], cT_lo[:, k, c], wr_hi[:, w],
                                     wr_lo[:, w], k == 0, k == KC - 1)
                last.then_inc(o_done, 1)

            def attend(b, par):
                pe.wait_ge(q_ready, b + 1)
                pe.wait_ge(k_ready, b + 1)
                for n in range(4):
                    score_rows(b, par, n)
                if b is not 0:
                    turn_context(b - 1)
                for n in range(4, 8):
                    score_rows(b, par, n)
                if b is not 0:
                    project_out(b - 1)
                pe.wait_ge(max_done, 8 * b + 8)
                for qt in range(2):
                    last = nc.tensor.transpose(ps[0:HEADS, 5, qt * P:qt * P + P], nm[:, qt, :], ident[:, 0:P])
                last.then_inc(nm_turned, 1)
                if b is not B - 1:
                    project(b + 1)
                pe.wait_ge(nm_ready, b + 1)
                pe.wait_ge(v_ready, b + 1)
                for n in range(3):
                    score_columns(b, par, n)
                for n in range(8):
                    if n < 5:
                        score_columns(b, par, n + 3)
                    values(b, par, n)

            project(0)
            attend(0, 0)
            with pe.Fori(0, (B - 2) // 2) as i:
                attend(2 * i + 1, 1)
                attend(2 * i + 2, 0)
            attend(B - 1, 1)
            turn_context(B - 1)
            project_out(B - 1)

            turn(turns[2])
            pe.wait_ge(gd_ready, 1)
            pe.wait_ge(turns[2].lo_done, NT // 2)
            sources = ((hT_hi, hT_lo), (s0_hi, s0_lo), (s1_hi, s1_lo))

            def difference(c):
                cc = ds(c * CH, CH)
                for k in range(KC):
                    last = three(ps[:, 2, :], gd_hi[:, k, :], gd_lo[:, k, :], hT_hi[:, k, cc], hT_lo[:, k, cc],
                                 k == 0, k == KC - 1)
                last.then_inc(diff_done, 1)

            def hidden(c, u):
                which = u // (HIDDEN // P)
                hi, lo = sources[which]
                since(pe, relu_done, c * BLOCKS + u - 1)
                if u == HIDDEN // P:
                    pe.wait_ge(sources_ready, 4 * c + 4)
                cc = slice(0, CH) if which else ds(c * CH, CH)
                for k in range(KC):
                    a = u * 2 * D + k * P
                    last = three(ps[:, u % 2, :], wr_hi[:, a:a + P], wr_lo[:, a:a + P], hi[:, k, cc], lo[:, k, cc],
                                 k == 0, k == KC - 1)
                last.then_inc(h_done, 1)

            def second(c, u):
                pe.wait_ge(h_split, SPLIT_AHEAD + c * BLOCKS + u + 1)
                if u == 0:
                    pe.wait_ge(y_added, Y_AHEAD + c)
                w = slice(u * 2 * D + D, (u + 1) * 2 * D)
                for t in range(CT):
                    c4 = slice(t * P, t * P + P)
                    last = three(ps[:, 4 + t // 2, (t % 2) * D:(t % 2) * D + D], H_hi[:, u % 4, c4],
                                 H_lo[:, u % 4, c4], wr_hi[:, w], wr_lo[:, w], u == 0 and t % 2 == 0,
                                 u == BLOCKS - 1, skip_group_check=True)
                last.then_inc(d_done, 1)

            def chunk(c):
                for u in range(BLOCKS):
                    if u + 2 < BLOCKS:
                        hidden(c, u + 2)
                    elif c is not NC - 1:
                        if u + 2 == BLOCKS:
                            difference(c + 1)
                        hidden(c + 1, u + 2 - BLOCKS)
                    second(c, u)

            difference(0)
            hidden(0, 0)
            hidden(0, 1)
            with pe.Fori(0, NC - 1) as c:
                chunk(c)
            chunk(NC - 1)


def _layout(a):
    import numpy as np

    c = np.ascontiguousarray

    def halves(w):
        return w.reshape(KC, P, -1).transpose(1, 0, 2).reshape(P, -1)

    x = c(a["x"].reshape(NT, P, D).transpose(1, 0, 2))
    ctx = c(a["ctx_1024"].reshape(NT, P, D).transpose(1, 0, 2))
    ctxT = c(halves(a["ctx_1024"].reshape(TOK, D).T))
    experts = []
    for s in range(SHARED):
        cut = slice(s * P, s * P + P)
        experts.append(np.concatenate([halves(a["L0_ffn_sh_gate"][cut].T), halves(a["L0_ffn_sh_up"][cut].T),
                                       a["L0_ffn_sh_down"][:, cut].T], 1))
    for e in range(E):
        experts.append(np.concatenate([halves(a["L0_ffn_w_gate"][e].T), halves(a["L0_ffn_w_up"][e].T),
                                       a["L0_ffn_w_down"][e].T], 1))
    wexp = c(np.stack(experts))
    rest = []
    firsts = [a["L1_ffn_sw1"], a["L1_ffn_w1"][0], a["L1_ffn_w1"][1]]
    seconds = [a["L1_ffn_sw2"], a["L1_ffn_w2"][0], a["L1_ffn_w2"][1]]
    for w1, w2 in zip(firsts, seconds):
        for n in range(HIDDEN // P):
            rest += [halves(w1[:, n * P:n * P + P]), w2[n * P:n * P + P]]
    twice = np.stack([np.arange(D).reshape(HEADS, DH)] * 2, 1).reshape(-1)
    rest += [halves(a["L1_xattn_Wq"].T[:, twice]), halves(a["L1_xattn_Wk"].T[:, twice]),
             halves(a["L1_xattn_Wv"].T), halves(a["L1_xattn_Wo"].T)]
    wrest = c(np.concatenate(rest, 1))
    rows = c(np.concatenate([a["g_xattn"], a["g_ffn"], a["L0_ffn_gate_bias"], a["L1_xattn_bv"], a["L1_xattn_bo"],
                             a["L1_ffn_sb2"], a["L1_ffn_b2"][0], a["L1_ffn_b2"][1]]).reshape(1, -1))
    b1 = np.concatenate([a["L1_ffn_sb1"], a["L1_ffn_b1"].reshape(-1)]).reshape(BLOCKS, P).T
    cols = c(np.concatenate([a["L1_xattn_bq"][twice].reshape(4, P).T, a["L1_xattn_bk"][twice].reshape(4, P).T, b1,
                             halves(a["L0_ffn_gate_w"].T), halves(a["L1_ffn_gate_w"].T)], 1))
    return {"x": x, "ctx": ctx, "ctxT": ctxT, "wexp": wexp, "wrest": wrest, "rows": rows, "cols": cols}


def kernel(**inputs):
    import numpy as np
    import concourse.bacc as bacc
    from concourse.bass_utils import run_bass_kernel_spmd

    packed = _layout({k: np.asarray(v) for k, v in inputs.items()})
    nc = bacc.Bacc("TRN2", target_bir_lowering=False, num_devices=1)
    args = [nc.dram_tensor(f"in_{n}", v.shape, F32, kind="ExternalInput").ap() for n, v in packed.items()]
    out = nc.dram_tensor("out_x", [P, NT, D], F32, kind="ExternalOutput").ap()
    two_layers(nc, *args, out)
    r = run_bass_kernel_spmd(nc, [{f"in_{n}": v for n, v in packed.items()}], core_ids=[0])
    return r.results[0]["out_x"].reshape(P, NT, D).transpose(1, 0, 2).reshape(B, S, D)
```

```python
from contextlib import ExitStack

import concourse.bass as bass
from concourse import mybir

F32 = mybir.dt.float32
F16 = mybir.dt.float16
BF16 = mybir.dt.bfloat16
ALU = mybir.AluOpType
ACT = mybir.ActivationFunctionType
AX = mybir.AxisListType
ds = bass.ds

P = 128
B, S, D = 8, 256, 256
TOK = B * S
NT = TOK // P
KC = D // P
CH = 512
NC = TOK // CH
CT = CH // P
E, INNER, GROUPS, TOP_GROUPS, TOP_K = 32, 128, 8, 4, 8
PER_GROUP = E // GROUPS
SHARED = 2
NE = E + SHARED
EW = 3 * D
HEADS, DH, WINDOW = 16, 16, 64
SPAN = P + WINDOW
HIDDEN, SOURCES = 1024, 3
BLOCKS = SOURCES * HIDDEN // P
QD = 2 * D
W1_COLS = BLOCKS * 2 * D
ATT_COLS = KC * (QD + QD + D + D)
REST = W1_COLS + ATT_COLS
PIECES = 16
PW = REST // PIECES
WS = 64.0
EPS = 1e-5
DECAY = 0.9
SCALE = 2.5
NEG = -1e30

R_G, R_BIAS = 0, 4
R_BV = R_BIAS + E
R_BO = R_BV + D
R_B2 = R_BO + D
ROWS = R_B2 + SOURCES * D
C_BQ, C_BK, C_B1 = 0, 4, 8
C_GW = C_B1 + BLOCKS
C_GD = C_GW + KC * E
COLS = C_GD + KC * 2


class Count:

    def __init__(self, engine, sem):
        self.engine, self.sem, self.at = engine, sem, 0

    def inc(self, ins):
        ins.then_inc(self.sem, 1)
        self.at = self.at + 1
        return ins

    def wait(self):
        self.engine.wait_ge(self.sem, self.at)


def since(engine, sem, count):
    if not isinstance(count, int) or count > 0:
        engine.wait_ge(sem, count)


def flat(t):
    return t[:, :, :].rearrange("p a n -> p (a n)")


def one(a):
    return a.rearrange("p a n -> p (a n)")


def two_layers(nc, x, ctx_in, ctxT_in, wexp, wrest, rows_in, cols_in, out):
    st = ExitStack()
    with st:
        def sb(name, shape, dt=F32):
            return st.enter_context(nc.sbuf_tensor(name, shape, dt))

        def sem(name):
            return st.enter_context(nc.semaphore(name))

        PAIRS = NE // 2
        UNITS = 2 * NC
        LAST = PAIRS - 1

        X = sb("X", [P, NT, D])
        TM = sb("TM", [P, NT, D])
        rows = sb("rows", [P, ROWS])
        cols = sb("cols", [P, COLS])
        tg = sb("tg", [P, 4])
        tgw = sb("tgw", [P, 4])
        ident = sb("ident", [P, D])
        identb = sb("identb", [P, P], BF16)
        decs = sb("decs", [P, 2, D])
        dec, decay = decs[:, 0, :], decs[:, 1, :]
        halfs = sb("halfs", [P, NT])
        stats = sb("stats", [P, NT, 6])
        mean = sb("mean", [P, NT])
        veps = sb("veps", [P, NT])
        rstd = sb("rstd", [P, NT])
        tA = sb("tA", [P, NT])
        tB = sb("tB", [P, NT])
        tC = sb("tC", [P, NT])
        rt = sb("rt", [P, NT])
        shift = sb("shift", [P, NT])
        hT_hi = sb("hT_hi", [P, KC, TOK], F16)
        hT_lo = sb("hT_lo", [P, KC, TOK], F16)
        uT_hi = sb("uT_hi", [P, KC, TOK], F16)
        uT_lo = sb("uT_lo", [P, KC, TOK], F16)
        sT_hi = sb("sT_hi", [P, KC, TOK], F16)
        sT_lo = sb("sT_lo", [P, KC, TOK], F16)
        gw_hi = sb("gw_hi", [P, KC * E], F16)
        gw_lo = sb("gw_lo", [P, KC * E], F16)
        stage = sb("stage", [P, 4, D])
        ew_raw = sb("ew_raw", [P, 2, EW])
        ew_hi = sb("ew_hi", [P, 2, EW], F16)
        ew_lo = sb("ew_lo", [P, 2, EW], F16)
        pc_raw = sb("pc_raw", [P, PW])
        wr_hi = sb("wr_hi", [P, REST], F16)
        wr_lo = sb("wr_lo", [P, REST], F16)
        act_s = sb("act_s", [P, 2, CH])
        prod = sb("prod", [P, 2, CH])
        H_hi = sb("H_hi", [P, 4, CH], F16)
        H_lo = sb("H_lo", [P, 4, CH], F16)
        weight = sb("weight", [P, NE, NT])
        tops = sb("tops", [P, NT, TOP_K])
        maskb = sb("maskb", [P, 2, 2 * SPAN], BF16)
        headsel = sb("headsel", [P, HEADS, P], BF16)
        slot4 = sb("slot4", [P, 4])
        waiter = sb("waiter", [P, 1])
        slotm = sb("slotm", [P, 1])
        bq4 = sb("bq4", [P, 4])
        bkc = sb("bkc", [P, 4])
        qa = sb("qa", [P, 3, 4 * S], F16)
        tgb = sb("tgb", [P, 2, D])
        nm = sb("nm", [P, 2, HEADS])
        LOW_ROWS = 32
        nmT = sb("nmT", [P, 2 * P], BF16)
        rc = sb("rc", [P, 2, HEADS // 2])
        gd = sb("gd", [P, KC])
        gd_hi = sb("gd_hi", [P, KC, P], F16)
        gd_lo = sb("gd_lo", [P, KC, P], F16)

        r_room = wr_lo[:, REST - 4096:REST].bitcast(F32)
        score, sc, w8, lg = (r_room[:, n * 512:n * 512 + 512] for n in range(4))
        g_room = wr_hi[:, REST - 2048:REST].bitcast(F32).rearrange("p (a n) -> p a n", a=8)
        PT = flat(TM)[:, 0:8 * 2 * SPAN].rearrange("p (n h q) -> p n h q", n=4, h=2)
        HV = DH + 1
        avs = flat(TM)[:, 8 * 2 * SPAN:8 * 2 * SPAN + HEADS * HV].rearrange("p (a h d) -> p a h d", a=2, h=8)
        tq = sT_hi[:, 0, :].bitcast(F32)
        tk = sT_hi[:, 1, :].bitcast(F32)
        P_hi = flat(sT_lo)[:, 0:8 * 2 * SPAN].rearrange("p (n h q) -> p n h q", n=4, h=2)
        qh = flat(sT_lo)[:, 8 * 2 * SPAN:8 * 2 * SPAN + 1024]
        P_lo = flat(ew_raw).bitcast(F16).rearrange("p (n h q) -> p n h q", n=4, h=2)
        qs = flat(H_hi)[:, 0:1024]
        alone = [qa[:, n, :] for n in range(3)] + [pc_raw[:, 0:2 * S].bitcast(F16)]
        kh = [flat(H_lo)[:, n * 1024:n * 1024 + 1024] for n in range(2)]
        kl = [flat(stage).bitcast(F16)[:, n * 1024:n * 1024 + 1024] for n in range(2)]
        V2 = [flat(t)[:, 0:2 * HEADS * 2 * HV].rearrange("p (n d) -> p n d", d=2 * HV) for t in (ew_hi, ew_lo)]
        vt = prod[:, 1, :]
        cT = prod[:, 0, :].bitcast(F16).rearrange("p (s k n) -> p s k n", s=2, k=KC)
        cT_hi, cT_lo = cT[:, 0, :, :], cT[:, 1, :, :]
        cx = decs
        A_Q = W1_COLS
        A_K = A_Q + KC * QD
        A_V = A_K + KC * QD
        A_O = A_V + KC * D
        s0_hi, s0_lo, s1_hi, s1_lo = (t[:, :, 0:CH] for t in (sT_hi, sT_lo, uT_hi, uT_lo))
        second_mask = sT_hi[:, 0, CH:2 * CH]

        ps = st.enter_context(nc.psum_tensor("ps", [P, 8, 512], F32))

        x_in = [sem(f"x_in{q}") for q in range(4)]
        ctx_loaded = [sem(f"ctx_loaded{q}") for q in range(4)]
        rows_loaded, cols_loaded, ctxT_loaded = sem("rows_loaded"), sem("cols_loaded"), sem("ctxT_loaded")
        ident_ready, consts_ready, att_consts = sem("ident_ready"), sem("consts_ready"), sem("att_consts")
        pool_step, dve_step = sem("pool_step"), sem("dve_step")
        tanh_ready, decay_ready, squares_ready = sem("tanh_ready"), sem("decay_ready"), sem("squares_ready")
        mix_done, mix_scaled, x_mixed = sem("mix_done"), sem("mix_scaled"), sem("x_mixed")
        shift_ready, odd_rows_ready = sem("shift_ready"), sem("odd_rows_ready")
        scan_done, veps_ready, rstd_ready = sem("scan_done"), sem("veps_ready"), sem("rstd_ready")
        logits_done, gate_tanh_done, gw_split = sem("logits_done"), sem("gate_tanh_done"), sem("gw_split")
        weight_ready, x_out = sem("weight_ready"), sem("x_out")

        class Turn:

            def __init__(self, name):
                self.rows_ready = sem(name + "_rows_ready")
                self.turned = sem(name + "_turned")
                self.hi_done = sem(name + "_hi_done")
                self.lo_done = sem(name + "_lo_done")

        turns = [Turn(f"turn{n}") for n in range(3)]
        ew_loaded = [sem("ew_loaded0"), sem("ew_loaded1")]
        ew_hi_done = [sem("ew_hi_done0"), sem("ew_hi_done1")]
        ew_split = [sem("ew_split0"), sem("ew_split1")]
        pc_loaded, pc_hi_done, pc_split = sem("pc_loaded"), sem("pc_hi_done"), sem("pc_split")
        gate_up_done, silu_done, prod_done = sem("gate_up_done"), sem("silu_done"), sem("prod_done")
        H_hi_done, H_lo_done = sem("H_hi_done"), sem("H_lo_done")
        down_done, added = sem("down_done"), sem("added")
        ctx_hi_done, ctx_split = sem("ctx_hi_done"), sem("ctx_split")
        bias_rows, bias_added, bias2_added = sem("bias_rows"), sem("bias_added"), sem("bias2_added")
        q_done, k_done, v_done = sem("q_done"), sem("k_done"), sem("v_done")
        tq_done, tk_done, qh_done, kh_done = sem("tq_done"), sem("tk_done"), sem("qh_done"), sem("kh_done")
        alone_zero, alone_loaded, v_hi_done = sem("alone_zero"), sem("alone_loaded"), sem("v_hi_done")
        q_ready, k_ready, v_ready = sem("q_ready"), sem("k_ready"), sem("v_ready")
        rows_done, max_done = sem("rows_done"), sem("max_done")
        nm_turned, nm_hi_done, nm_ready = sem("nm_turned"), sem("nm_hi_done"), sem("nm_ready")
        sT_done, exp_done, masked = sem("sT_done"), sem("exp_done"), sem("masked")
        p_hi_done, p_split, av_done, av_read = sem("p_hi_done"), sem("p_split"), sem("av_done"), sem("av_read")
        cx_ready, cx_turned, c_hi_done, c_split = sem("cx_ready"), sem("cx_turned"), sem("c_hi_done"), sem("c_split")
        o_done, x_added = sem("o_done"), sem("x_added")
        gd_ready, diff_done, mask_ready, sources_ready = \
            sem("gd_ready"), sem("diff_done"), sem("mask_ready"), sem("sources_ready")
        h_done, relu_done, h_hi_done, h_split = sem("h_done"), sem("relu_done"), sem("h_hi_done"), sem("h_split")
        d_done, y_added = sem("d_done"), sem("y_added")

        MASKED_AHEAD, SPLIT_AHEAD, D_AHEAD, Y_AHEAD = 1, 2, 4, 1

        LOOPED = (B - 4) // 2 * 2

        GATES_AFTER, FIRST_UNITS = (3, 5), (5, 7)
        TURN_ROWS, TURN, TURN_HI, TURN_LO = (6, 12), (8, 14), (9, 15), (10, 16)
        HALF = NT // 2
        EARLY = 4
        FFN_EARLY = 12

        def context_bank(b):
            return 5 if within(b + 1) else 3

        def output_bank(b):
            return 4 if within(b + 1) else 2

        def turn_bank(n):
            return n if n < 2 else 5 + (n - 2) % 3

        def later(i):
            return not isinstance(i, int) or i > 0

        def last_pair(i):
            return isinstance(i, int) and i == LAST

        def last_chunk(c):
            return isinstance(c, int) and c == NC - 1

        def within(b):
            return not isinstance(b, int) or b < B

        block = st.enter_context(nc.Block())

        @block.sync
        def _(sp):
            sp.dma_start(rows[:, :], rows_in.broadcast_to([P, ROWS])).then_inc(rows_loaded, 16)
            for q in range(4):
                sp.dma_start(TM[:, 4 * q:4 * q + 4, :], ctx_in[:, 4 * q:4 * q + 4, :]).then_inc(ctx_loaded[q], 16)
                sp.dma_start(X[:, 4 * q:4 * q + 4, :], x[:, 4 * q:4 * q + 4, :]).then_inc(x_in[q], 16)
            sp.dma_start(cols[:, :], cols_in).then_inc(cols_loaded, 16)
            for k in range(2):
                sp.dma_start(ew_raw[:, k, :], wexp[k, :, :]).then_inc(ew_loaded[k], 16)
            sp.dma_start(pc_raw[:, :], wrest[:, 0:PW]).then_inc(pc_loaded, 16)
            sp.wait_ge(x_mixed, B)
            sp.dma_start(flat(TM), ctxT_in).then_inc(ctxT_loaded, 16)

            def next_experts(i):
                for k in range(2):
                    sp.wait_ge(ew_split[k], i + 1)
                    sp.dma_start(ew_raw[:, k, :], one(wexp[ds(2 * i + 2 + k, 1), :, :].rearrange("a p n -> p a n")))\
                        .then_inc(ew_loaded[k], 16)

            with sp.Fori(0, PIECES - 1) as i:
                next_experts(i)
                sp.wait_ge(pc_split, i + 1)
                sp.dma_start(pc_raw[:, :], wrest[:, ds((i + 1) * PW, PW)]).then_inc(pc_loaded, 16)
            next_experts(LAST - 1)

            def set_apart(b):
                sp.wait_ge(q_ready, b + 1)
                since(sp, exp_done, 8 * b)
                for j in range(4):
                    sl = slice(32 * j, 32 * j + 32)
                    sp.dma_start(alone[j][sl, :], qs[sl, :]).then_inc(alone_loaded, 16)

            sp.wait_ge(alone_zero, 1)
            for b in range(B):
                set_apart(b)
            for c in range(NC):
                sp.wait_ge(y_added, Y_AHEAD + c + 1)
                sp.dma_start(out[:, CT * c:CT * c + CT, :], X[:, CT * c:CT * c + CT, :]).then_inc(x_out, 16)
            sp.wait_ge(x_out, 16 * NC)

        @block.gpsimd
        def _(pool):
            step = Count(pool, pool_step)
            pool.sem_inc(masked, MASKED_AHEAD)
            step.inc(nc.gpsimd.memset(ident[:, :], 0.0))
            step.wait()
            nc.gpsimd.affine_select(out=ident[:, 0:P], in_=ident[:, 0:P], pattern=[[-1, P]], base=0,
                                    channel_multiplier=1, compare_op=ALU.not_equal, fill=1.0).then_inc(ident_ready, 1)
            nc.gpsimd.memset(halfs[:, :], -0.5)
            pool.wait_ge(ident_ready, 1)
            nc.gpsimd.tensor_copy(identb[:, :], ident[:, 0:P]).then_inc(consts_ready, 1)

            def inverse_root(n, a=0, z=NT):
                pool.wait_ge(veps_ready, n)
                nc.gpsimd.tensor_tensor(rstd[:, a:z], veps[:, a:z], halfs[:, a:z], ALU.pow).then_inc(rstd_ready, 1)

            for t in alone[:3]:
                nc.gpsimd.memset(t, 0.0)
            step.inc(nc.gpsimd.memset(maskb[:, :, :], 0.0))
            step.inc(nc.gpsimd.memset(headsel[:, :, :], 0.0))
            step.inc(nc.gpsimd.memset(slot4[:, :], 1.0))
            nc.gpsimd.memset(nmT[:, :], 0.0)
            step.wait()
            for qt in range(2):
                v = maskb[:, qt, :].rearrange("p (h q) -> p h q", h=2)
                step.inc(nc.gpsimd.affine_select(out=v, in_=v, pattern=[[0, 2], [-1, SPAN]],
                                                 base=WINDOW * (1 + qt), channel_multiplier=1,
                                                 compare_op=ALU.is_ge, fill=NEG))
                step.wait()
                step.inc(nc.gpsimd.affine_select(out=v, in_=v, pattern=[[0, 2], [1, SPAN]],
                                                 base=WINDOW * (1 - qt), channel_multiplier=-1,
                                                 compare_op=ALU.is_ge, fill=NEG))
            for base in (0, -LOW_ROWS):
                step.inc(nc.gpsimd.affine_select(out=headsel[:, :, :], in_=headsel[:, :, :],
                                                 pattern=[[-1, HEADS], [0, P]], base=base, channel_multiplier=1,
                                                 compare_op=ALU.not_equal, fill=1.0))
                step.wait()
            step.inc(nc.gpsimd.affine_select(out=slot4[:, :], in_=slot4[:, :], pattern=[[-32, 4]], base=-16,
                                             channel_multiplier=1, compare_op=ALU.is_ge, fill=0.0))
            step.wait()
            nc.gpsimd.affine_select(out=slot4[:, :], in_=slot4[:, :], pattern=[[32, 4]], base=31,
                                    channel_multiplier=-1, compare_op=ALU.is_ge, fill=0.0).then_inc(att_consts, 1)

            def add_mixed(b):
                pool.wait_ge(mix_scaled, b + 1)
                xb = X[:, 2 * b:2 * b + 2, :]
                nc.gpsimd.tensor_tensor(xb, xb, TM[:, 2 * b:2 * b + 2, :], ALU.add).then_inc(x_mixed, 1)

            inverse_root(1, 0, HALF)
            for b in range(B):
                if b == 2:
                    inverse_root(2, HALF, NT)
                if b == 5:
                    inverse_root(3, 0, HALF)
                add_mixed(b)
            inverse_root(4, HALF, NT)

            def hidden_lo(i, u):
                pool.wait_ge(H_hi_done, i * UNITS + u + 1)
                nc.gpsimd.tensor_tensor(H_lo[:, u % 4, :], prod[:, u % 2, :], H_hi[:, u % 4, :], ALU.subtract)\
                    .then_inc(H_lo_done, 1)

            with pool.Fori(0, LAST) as i:
                for u in range(UNITS):
                    hidden_lo(i, u)
            for u in range(UNITS):
                hidden_lo(LAST, u)
                if u == UNITS - 2:
                    inverse_root(5, 0, EARLY)
                pool.wait_ge(ctx_hi_done, 1 + u // (UNITS // 2))
                w = slice(u * TOK * KC // UNITS, (u + 1) * TOK * KC // UNITS)
                nc.gpsimd.tensor_tensor(flat(uT_lo)[:, w], flat(TM)[:, w], flat(uT_hi)[:, w], ALU.subtract)\
                    .then_inc(ctx_split, 1)
            pool.wait_ge(pc_split, PIECES)
            nc.gpsimd.memset(alone[3], 0.0).then_inc(alone_zero, 1)
            inverse_root(6, EARLY, NT)

            def mask(b, n):
                pool.wait_ge(masked, MASKED_AHEAD + 8 * b + n)
                pool.wait_ge(exp_done, 8 * b + n + 1)
                nc.gpsimd.tensor_tensor(waiter[:, :], halfs[:, 0:1], halfs[:, 0:1], ALU.add)

                def cut(a, size, base, sign):
                    w = PT[:, n % 4, :, a:a + size]
                    return nc.gpsimd.affine_select(out=w, in_=w, pattern=[[0, 2], [-sign, size]], base=base,
                                                   channel_multiplier=sign, compare_op=ALU.is_ge, fill=0.0)

                cut(0, WINDOW, WINDOW, -1)
                cut(WINDOW, P, 0, 1)
                cut(SPAN, P, 0, -1)
                cut(SPAN + P, WINDOW, 0, 1).then_inc(masked, 1)

            def keys_lo(b, par):
                pool.wait_ge(kh_done, b + 1)
                nc.gpsimd.tensor_tensor(kl[par], tk, kh[par], ALU.subtract).then_inc(k_ready, 1)

            def values_lo(b, par):
                pool.wait_ge(v_hi_done, b + 1)
                nc.gpsimd.tensor_tensor(V2[par][:, :, HV:HV + DH], vt.rearrange("p (n d) -> p n d", d=DH),
                                        V2[par][:, :, 0:DH], ALU.subtract).then_inc(v_ready, 1)

            def add_bias(b):
                pool.wait_ge(turns[1].rows_ready, NT // 2)
                xb = X[:, ds(2 * b, 2), :]
                nc.gpsimd.tensor_tensor(xb, xb, tgb[:, 0, :].unsqueeze(1).broadcast_to([P, 2, D]), ALU.add)\
                    .then_inc(bias_added, 1)

            def attend(b, par):
                for n in range(8):
                    mask(b, n)
                    if n == 3:
                        add_bias(b)
                        if not within(b + 1):
                            inverse_root(7, 0, FFN_EARLY)
                if within(b + 2):
                    keys_lo(b + 2, par)
                    values_lo(b + 2, par)

            values_lo(0, 0)
            pool.wait_ge(turns[1].turned, NT // 2)
            keys_lo(0, 0)
            keys_lo(1, 1)
            values_lo(1, 1)
            attend(0, 0)
            with pool.Fori(0, LOOPED // 2) as i:
                attend(2 * i + 1, 1)
                attend(2 * i + 2, 0)
            for b in range(LOOPED + 1, B):
                attend(b, b % 2)
            inverse_root(8, FFN_EARLY, NT)
            with pool.Fori(0, NC) as c:
                pool.wait_ge(turns[2].rows_ready, 2 * c + 2)
                xc = X[:, ds(CT * c, CT), :]
                nc.gpsimd.tensor_tensor(xc, xc, tgb[:, 1, :].unsqueeze(1).broadcast_to([P, CT, D]), ALU.add)\
                    .then_inc(bias2_added, 1)

        @block.scalar
        def _(act):
            act.wait_ge(rows_loaded, 16)
            nc.scalar.activation(tg[:, :], rows[:, R_G:R_G + 4], ACT.Tanh).then_inc(tanh_ready, 1)
            for q in range(4):
                act.wait_ge(ctx_loaded[q], 16)
                nc.scalar.activation(TM[:, 4 * q:4 * q + 4, :], TM[:, 4 * q:4 * q + 4, :], ACT.Square)\
                    .then_inc(squares_ready, 1)
            act.wait_ge(cols_loaded, 16)
            nc.scalar.activation(gw_hi[:, :], cols[:, C_GW:C_GW + KC * E], ACT.Copy, scale=WS).then_inc(gw_split, 1)

            def weights_hi(k, n):
                act.wait_ge(ew_loaded[k], 16 * n + 16)
                since(act, down_done, UNITS * n - NC * (1 - k))
                nc.scalar.activation(ew_hi[:, k, :], ew_raw[:, k, :], ACT.Copy, scale=WS).then_inc(ew_hi_done[k], 1)

            def piece_hi(i):
                act.wait_ge(pc_loaded, 16 * i + 16)
                nc.scalar.activation(wr_hi[:, ds(i * PW, PW)], pc_raw[:, :], ACT.Copy, scale=WS)\
                    .then_inc(pc_hi_done, 1)

            weights_hi(0, 0)
            for b in range(B):
                act.wait_ge(mix_done, b + 1)
                for h in range(2):
                    c = 2 * b + h
                    last = nc.scalar.activation(TM[:, c, :], TM[:, c, :], ACT.Copy, scale=rt[:, c:c + 1])
                last.then_inc(mix_scaled, 1)

            def turn_hi(t, n, bank):
                act.wait_ge(t.turned, n + 1)
                nc.scalar.activation(hT_hi[:, :, ds(n * 2 * P, 2 * P)],
                                     ps[:, bank, :].rearrange("p (k n) -> p k n", k=KC), ACT.Copy)\
                    .then_inc(t.hi_done, 1)

            def odd_rows(n):
                since(act, turns[0].turned, n - 1)
                c = 2 * n + 1
                nc.scalar.activation(stage[:, 2 * (n % 2) + 1, :], X[:, c, :], ACT.Identity, bias=shift[:, c:c + 1],
                                     scale=rstd[:, c:c + 1]).then_inc(odd_rows_ready, 1)

            def silu(n, u):
                act.wait_ge(gate_up_done, n + 1)
                since(act, prod_done, n - 1)
                nc.scalar.activation(act_s[:, u % 2, :], ps[:, u % 2, :], ACT.Silu, scale=1.0 / WS)\
                    .then_inc(silu_done, 1)

            def hidden_hi(u):
                act.wait_ge(prod_done, u + 1)
                since(act, down_done, u - 3)
                nc.scalar.activation(H_hi[:, u % 4, :], prod[:, u % 2, :], ACT.Copy).then_inc(H_hi_done, 1)

            act.wait_ge(shift_ready, 1)
            odd_rows(0)
            odd_rows(1)
            for n in range(NT // 2):
                if n + 2 == HALF // 2:
                    act.wait_ge(shift_ready, 2)
                if n + 2 < NT // 2:
                    odd_rows(n + 2)
                turn_hi(turns[0], n, 4 + n % 3)
                if n in FIRST_UNITS:
                    silu(FIRST_UNITS.index(n), FIRST_UNITS.index(n))
                    hidden_hi(FIRST_UNITS.index(n))
                if n == 3:
                    weights_hi(1, 0)
            piece_hi(0)
            act.wait_ge(logits_done, 1)
            nc.scalar.activation(lg, ps[:, 7, :], ACT.Tanh, scale=0.5 / WS).then_inc(gate_tanh_done, 1)

            def silu_pair(i):
                for u in range(UNITS):
                    if later(i) or u >= 2:
                        silu(i * UNITS + u, u)
                        if not later(i):
                            hidden_hi(u)
                    if u == 1 and later(i):
                        weights_hi(1, i)
                    if u in (0, 2) and last_pair(i):
                        act.wait_ge(ctxT_loaded, 16)
                        nc.scalar.activation(flat(uT_hi)[:, u // 2 * TOK:(u // 2 + 1) * TOK],
                                             flat(TM)[:, u // 2 * TOK:(u // 2 + 1) * TOK], ACT.Copy)\
                            .then_inc(ctx_hi_done, 1)
                    if u == 3 and later(i) and not last_pair(i):
                        piece_hi(i)
                    if u == 5 and not last_pair(i):
                        weights_hi(0, i + 1)

            silu_pair(0)
            with act.Fori(1, LAST) as i:
                silu_pair(i)
            silu_pair(LAST)

            def query_key(b, par):
                act.wait_ge(q_done, b + 1)
                since(act, q_ready, b)
                for g in range(4):
                    last = nc.scalar.activation(tq[:, g * D:g * D + D], ps[:, g // 2, (g % 2) * D:(g % 2) * D + D],
                                                ACT.Identity, bias=bq4[:, g:g + 1], scale=0.25 / WS)
                last.then_inc(tq_done, 1)
                act.wait_ge(tq_done, b + 1)
                nc.scalar.activation(qh, tq, ACT.Copy).then_inc(qh_done, 1)
                act.wait_ge(k_done, b + 1)
                since(act, k_ready, b)
                for g in range(4):
                    last = nc.scalar.activation(tk[:, g * D:g * D + D],
                                                ps[:, 2 + g // 2, (g % 2) * D:(g % 2) * D + D],
                                                ACT.Identity, bias=bkc[:, g:g + 1], scale=1.0 / WS)
                last.then_inc(tk_done, 1)
                act.wait_ge(tk_done, b + 1)
                nc.scalar.activation(kh[par], tk, ACT.Copy).then_inc(kh_done, 1)

            def context_hi(b):
                act.wait_ge(cx_turned, b + 1)
                nc.scalar.activation(cT_hi, ps[:, context_bank(b), :].rearrange("p (k n) -> p k n", k=KC), ACT.Copy)\
                    .then_inc(c_hi_done, 1)

            def probabilities_hi(b, n):
                act.wait_ge(masked, MASKED_AHEAD + 8 * b + n + 1)
                since(act, av_done, 8 * b + n - 3)
                nc.scalar.activation(P_hi[:, n % 4, :, :], PT[:, n % 4, :, :], ACT.Copy).then_inc(p_hi_done, 1)

            def attend(b, par):
                for n in range(8):
                    act.wait_ge(sT_done, 8 * b + n + 1)
                    since(act, p_split, 8 * b + n - 3)
                    nc.scalar.activation(PT[:, n % 4, :, :], ps[:, 0:2, 0:2 * SPAN], ACT.Exp).then_inc(exp_done, 1)
                    if n >= 1:
                        probabilities_hi(b, n - 1)
                    if n == 2 and later(b):
                        context_hi(b - 1)
                    if n in (5, 6) and not within(b + 1):
                        turn_hi(turns[2], n - 5, 3)
                probabilities_hi(b, 7)
                if within(b + 2):
                    query_key(b + 2, par)

            for n in range(2):
                turn_hi(turns[1], n, turn_bank(n))
            act.wait_ge(bias_rows, 1)
            query_key(0, 0)
            for n in range(2, NT // 2):
                turn_hi(turns[1], n, turn_bank(n))
            query_key(1, 1)
            attend(0, 0)
            with act.Fori(0, LOOPED // 2) as i:
                attend(2 * i + 1, 1)
                attend(2 * i + 2, 0)
            for b in range(LOOPED + 1, B):
                attend(b, b % 2)

            def relu_chunk(c):
                for u in range(BLOCKS):
                    n = c * BLOCKS + u
                    act.wait_ge(h_done, n + 1)
                    act.wait_ge(h_split, SPLIT_AHEAD + n - 1)
                    nc.scalar.activation(act_s[:, u % 2, :], ps[:, u % 2, :], ACT.Relu,
                                         bias=cols[:, C_B1 + u:C_B1 + u + 1], scale=1.0 / WS).then_inc(relu_done, 1)
                    if not later(c) and u == 1:
                        context_hi(B - 1)
                    if u in TURN_HI and not last_chunk(c):
                        turn_hi(turns[2], 2 * c + 2 + TURN_HI.index(u), 3)

            relu_chunk(0)
            with act.Fori(1, NC - 1) as c:
                relu_chunk(c)
            relu_chunk(NC - 1)

        @block.vector
        def _(dve):
            step = Count(dve, dve_step)
            dve.sem_inc(h_split, SPLIT_AHEAD)
            dve.sem_inc(y_added, Y_AHEAD)
            nc.vector.memset(dec[:, :], DECAY).then_inc(decay_ready, 1)
            dve.wait_ge(decay_ready, 1)
            dve.wait_ge(ident_ready, 1)
            nc.vector.tensor_tensor_scan(decay[:, :], dec[:, :], ident[:, :], 0.0, ALU.mult, ALU.add)\
                .then_inc(decay_ready, 1)
            dve.wait_ge(tanh_ready, 1)
            step.inc(nc.vector.tensor_scalar(tgw[:, :], tg[:, :], 1.0 / WS, None, ALU.mult))

            def tile_stats(t):
                return nc.vector.bn_stats(stats[:, t, :] if isinstance(t, int) else one(stats[:, ds(t, 1), :]),
                                          X[:, t, :] if isinstance(t, int) else one(X[:, ds(t, 1), :]))

            def moments(a=0, z=NT):
                w = slice(a, z)
                step.inc(nc.vector.tensor_tensor(tA[:, w], stats[:, w, 1], stats[:, w, 4], ALU.add))
                step.inc(nc.vector.tensor_tensor(tB[:, w], stats[:, w, 1], stats[:, w, 4], ALU.subtract))
                step.inc(nc.vector.tensor_tensor(tC[:, w], stats[:, w, 2], stats[:, w, 5], ALU.add))
                step.wait()
                nc.vector.tensor_scalar(mean[:, w], tA[:, w], 0.5, None, ALU.mult)
                step.inc(nc.vector.tensor_tensor(tB[:, w], tB[:, w], tB[:, w], ALU.mult))
                step.wait()
                step.inc(nc.vector.scalar_tensor_tensor(tC[:, w], tB[:, w], D / 4.0, tC[:, w], ALU.mult, ALU.add))
                step.wait()
                nc.vector.tensor_scalar(veps[:, w], tC[:, w], 1.0 / D, EPS, ALU.mult, ALU.add).then_inc(veps_ready, 1)

            def mix(b):
                dve.wait_ge(scan_done, b + 1)
                for h in range(2):
                    c = 2 * b + h
                    last = nc.vector.scalar_tensor_tensor(TM[:, c, :], X[:, c, :], mean[:, c:c + 1],
                                                          ps[:, b, h * D:h * D + D], ALU.subtract, ALU.mult)
                last.then_inc(mix_done, 1)

            def mixed_stats(b):
                dve.wait_ge(x_mixed, b + 1)
                tile_stats(2 * b)
                return tile_stats(2 * b + 1)

            def shifts(n, a, z):
                dve.wait_ge(rstd_ready, n)
                step.inc(nc.vector.tensor_tensor(shift[:, a:z], mean[:, a:z], rstd[:, a:z], ALU.mult))
                step.wait()
                nc.vector.tensor_scalar(shift[:, a:z], shift[:, a:z], -1.0, None, ALU.mult).then_inc(shift_ready, 1)

            def even_rows(n):
                since(dve, turns[0].turned, n - 1)
                c = 2 * n
                nc.vector.tensor_scalar(stage[:, 2 * (n % 2), :], X[:, c, :], mean[:, c:c + 1], rstd[:, c:c + 1],
                                        ALU.subtract, ALU.mult).then_inc(turns[0].rows_ready, 1)

            def first_stats(q):
                dve.wait_ge(x_in[q], 16)
                for t in range(4 * q, 4 * q + 4):
                    last = tile_stats(t)
                return last

            def gated_root(n, a, z):
                dve.wait_ge(rstd_ready, n)
                step.inc(nc.vector.tensor_scalar(rt[:, a:z], rstd[:, a:z], tg[:, 0:1], None, ALU.mult))
                step.wait()

            def after(last):
                step.inc(last)
                step.wait()

            first_stats(0)
            after(first_stats(1))
            moments(0, HALF)
            first_stats(2)
            gated_root(1, 0, HALF)
            for b in range(3):
                mix(b)
            after(first_stats(3))
            moments(HALF, NT)
            mix(3)
            mixed_stats(0)
            mixed_stats(1)
            gated_root(2, HALF, NT)
            mix(4)
            mixed_stats(2)
            mix(5)
            after(mixed_stats(3))
            dve.wait_ge(mix_done, B // 2)
            moments(0, HALF)
            mix(6)
            mixed_stats(4)
            mix(7)
            shifts(3, 0, HALF)
            even_rows(0)
            even_rows(1)
            for b in range(5, B):
                last = mixed_stats(b)
            after(last)
            dve.wait_ge(mix_done, B)
            moments(HALF, NT)
            dve.wait_ge(gw_split, 1)
            nc.vector.scalar_tensor_tensor(gw_lo[:, :], cols[:, C_GW:C_GW + KC * E], WS, gw_hi[:, :], ALU.mult,
                                           ALU.subtract).then_inc(gw_split, 1)

            def turn_rows(t, n, at=None):
                if at is None:
                    since(dve, t.turned, n - 1)
                    at = n % 2
                for h in range(2):
                    c = ds(2 * n + h, 1)
                    last = nc.vector.tensor_scalar(stage[:, 2 * at + h, :], one(X[:, c, :]), mean[:, c],
                                                   rstd[:, c], ALU.subtract, ALU.mult)
                last.then_inc(t.rows_ready, 1)

            def turn_lo(t, n, bank):
                dve.wait_ge(t.hi_done, n + 1)
                cut = ds(n * 2 * P, 2 * P)
                nc.vector.tensor_tensor(hT_lo[:, :, cut], ps[:, bank, :].rearrange("p (k n) -> p k n", k=KC),
                                        hT_hi[:, :, cut], ALU.subtract).then_inc(t.lo_done, 1)

            def weights_lo(k, n):
                dve.wait_ge(ew_hi_done[k], n + 1)
                nc.vector.scalar_tensor_tensor(ew_lo[:, k, :], ew_raw[:, k, :], WS, ew_hi[:, k, :], ALU.mult,
                                               ALU.subtract).then_inc(ew_split[k], 1)

            def gated(n, u):
                dve.wait_ge(silu_done, n + 1)
                since(dve, H_lo_done, n - 1)
                nc.vector.scalar_tensor_tensor(prod[:, u % 2, :], ps[:, 2 + u % 2, :], 1.0 / WS, act_s[:, u % 2, :],
                                               ALU.mult, ALU.mult).then_inc(prod_done, 1)
                if isinstance(n, int) and n < UNITS:
                    return
                dve.wait_ge(prod_done, n + 1)
                since(dve, down_done, n - 3)
                nc.vector.tensor_copy(H_hi[:, u % 4, :], prod[:, u % 2, :]).then_inc(H_hi_done, 1)

            def piece_lo(i):
                dve.wait_ge(pc_hi_done, i + 1)
                nc.vector.scalar_tensor_tensor(wr_lo[:, ds(i * PW, PW)], pc_raw[:, :], WS, wr_hi[:, ds(i * PW, PW)],
                                               ALU.mult, ALU.subtract).then_inc(pc_split, 1)

            weights_lo(0, 0)
            for n in range(NT // 2):
                if n + 2 == HALF // 2:
                    shifts(4, HALF, NT)
                if n + 2 < NT // 2:
                    even_rows(n + 2)
                turn_lo(turns[0], n, 4 + n % 3)
                if n in FIRST_UNITS:
                    gated(FIRST_UNITS.index(n), FIRST_UNITS.index(n))
                if n == NT // 2 - 2:
                    weights_lo(1, 0)
            piece_lo(0)
            nc.vector.tensor_copy(weight[:, 0:SHARED, :], tgw[:, 2:3].unsqueeze(2).broadcast_to([P, SHARED, NT]))\
                .then_inc(weight_ready, 1)

            v4 = sc.rearrange("p (g f) -> p g f", f=PER_GROUP)
            mx1, mn1, mx2, mn2, top, mid, low2, sec = (g_room[:, n, :] for n in range(8))

            def group_scores():
                dve.wait_ge(gate_tanh_done, 1)
                step.inc(nc.vector.tensor_scalar(score, lg, 0.5, 0.5, ALU.mult, ALU.add))
                step.wait()
                step.inc(nc.vector.tensor_tensor(
                    sc.rearrange("p (t e) -> p t e", e=E), score.rearrange("p (t e) -> p t e", e=E),
                    rows[:, R_BIAS:R_BIAS + E].unsqueeze(1).broadcast_to([P, NT, E]), ALU.add))
                step.wait()
                nc.vector.tensor_tensor(mx1, v4[:, :, 0], v4[:, :, 1], ALU.max)
                nc.vector.tensor_tensor(mn1, v4[:, :, 0], v4[:, :, 1], ALU.min)
                nc.vector.tensor_tensor(mx2, v4[:, :, 2], v4[:, :, 3], ALU.max)
                step.inc(nc.vector.tensor_tensor(mn2, v4[:, :, 2], v4[:, :, 3], ALU.min))
                step.wait()
                nc.vector.tensor_tensor(top, mx1, mx2, ALU.max)
                nc.vector.tensor_tensor(mid, mx1, mx2, ALU.min)
                step.inc(nc.vector.tensor_tensor(low2, mn1, mn2, ALU.max))
                step.wait()
                step.inc(nc.vector.tensor_tensor(sec, mid, low2, ALU.max))
                step.wait()
                step.inc(nc.vector.tensor_tensor(mid, top, sec, ALU.add))
                step.wait()

            def groups_struck():
                for t in range(NT):
                    last = nc.vector.max(tops[:, t, :], mid[:, t * GROUPS:t * GROUPS + GROUPS])
                step.inc(last)
                step.wait()
                step.inc(nc.vector.memset(tops[:, :, TOP_GROUPS:], -3 * NEG))
                step.wait()
                for t in range(NT):
                    last = nc.vector.match_replace(mx1[:, t * GROUPS:t * GROUPS + GROUPS], tops[:, t, :],
                                                   mid[:, t * GROUPS:t * GROUPS + GROUPS], NEG)
                step.inc(last)
                step.wait()

            def groups_kept():
                step.inc(nc.vector.tensor_scalar(mn1, mx1, 0.1 * NEG, None, ALU.is_lt))
                step.wait()
                step.inc(nc.vector.tensor_tensor(v4, v4, mn1.unsqueeze(2).broadcast_to([P, NT * GROUPS, PER_GROUP]),
                                                 ALU.mult))
                step.wait()
                step.inc(nc.vector.tensor_scalar(sc, sc, 0.0, None, ALU.add))
                step.wait()

            def greatest():
                for t in range(NT):
                    last = nc.vector.max(tops[:, t, :], sc[:, t * E:t * E + E])
                step.inc(last)
                step.wait()

            def struck():
                for t in range(NT):
                    last = nc.vector.match_replace(w8[:, t * E:t * E + E], tops[:, t, :], sc[:, t * E:t * E + E], NEG)
                step.inc(last)
                step.wait()

            def weights():
                step.inc(nc.vector.scalar_tensor_tensor(w8, w8, 0.1 * NEG, score, ALU.is_lt, ALU.mult))
                step.wait()
                step.inc(nc.vector.tensor_reduce(tA[:, :], w8.rearrange("p (t e) -> p t e", e=E), AX.X, ALU.add))
                step.wait()
                step.inc(nc.vector.tensor_scalar(tA[:, :], tA[:, :], 1e-20, None, ALU.add))
                step.wait()
                step.inc(nc.vector.reciprocal(tB[:, :], tA[:, :]))
                step.wait()
                step.inc(nc.vector.tensor_scalar(tB[:, :], tB[:, :], tgw[:, 2:3], SCALE, ALU.mult, ALU.mult))
                step.wait()
                nc.vector.tensor_tensor(weight[:, SHARED:NE, :], w8.rearrange("p (t e) -> p e t", e=E),
                                        tB[:, :].unsqueeze(1).broadcast_to([P, E, NT]), ALU.mult)\
                    .then_inc(weight_ready, 1)
                dve.wait_ge(weight_ready, 2)

            router_parts = {0: group_scores, 1: groups_struck, 2: groups_kept, 3: greatest, 5: struck, 7: weights}

            def add_down(i, u):
                dve.wait_ge(down_done, i * UNITS + u + 1)
                e = 2 * i + u // NC
                for t in range(CT):
                    tile = (u % NC) * CT + t
                    of = weight[:, e, tile:tile + 1] if isinstance(i, int) else weight[:, ds(e, 1), tile]
                    last = nc.vector.scalar_tensor_tensor(
                        X[:, tile, :], ps[:, 4 + 2 * (u % 2) + t // 2, (t % 2) * D:(t % 2) * D + D], of,
                        X[:, tile, :], ALU.mult, ALU.add)
                last.then_inc(added, 1)

            def chunk_stats(u):
                dve.wait_ge(added, LAST * UNITS + u + 1)
                for t in range(CT):
                    last = tile_stats((u % NC) * CT + t)
                return last

            def more_constants():
                step.inc(nc.vector.tensor_tensor(gd[:, :], cols[:, C_GD + 1:C_GD + 4:2], cols[:, C_GD:C_GD + 3:2],
                                                 ALU.subtract))
                step.wait()
                step.inc(nc.vector.tensor_scalar(gd[:, :], gd[:, :], WS, None, ALU.mult))
                step.wait()
                wide = gd[:, :].unsqueeze(2).broadcast_to([P, KC, P])
                step.inc(nc.vector.tensor_copy(gd_hi[:, :, :], wide))
                step.wait()
                nc.vector.tensor_tensor(gd_lo[:, :, :], wide, gd_hi[:, :, :], ALU.subtract).then_inc(gd_ready, 1)
                nc.vector.tensor_scalar(bq4[:, :], cols[:, C_BQ:C_BQ + 4], 0.25, None, ALU.mult)
                nc.vector.tensor_copy(bkc[:, :], cols[:, C_BK:C_BK + 4])
                nc.vector.tensor_scalar(tgb[:, 0, :], rows[:, R_BO:R_BO + D], tg[:, 1:2], None, ALU.mult)
                step.inc(nc.vector.tensor_tensor(tgb[:, 1, :], rows[:, R_B2:R_B2 + D], rows[:, R_B2 + D:R_B2 + 2 * D],
                                                 ALU.add))
                step.wait()
                step.inc(nc.vector.tensor_tensor(tgb[:, 1, :], tgb[:, 1, :], rows[:, R_B2 + 2 * D:R_B2 + 3 * D], ALU.add))
                step.wait()
                nc.vector.tensor_scalar(tgb[:, 1, :], tgb[:, 1, :], tg[:, 3:4], None, ALU.mult).then_inc(bias_rows, 1)
                dve.wait_ge(att_consts, 1)
                nc.vector.tensor_reduce(slotm[:, :], slot4[:, :], AX.X, ALU.add, negate=True)

            def pair(i):
                for u in range(UNITS):
                    if not last_pair(i) or u < UNITS - 2:
                        gated(i * UNITS + u + 2, u + 2)
                    if last_pair(i) and u == UNITS - 2:
                        dve.wait_ge(rstd_ready, 5)
                        turn_rows(turns[1], 0)
                        turn_rows(turns[1], 1)
                    add_down(i, u)
                    if u == 0 and later(i):
                        weights_lo(1, i)
                    if not later(i) and u in router_parts:
                        router_parts[u]()
                    if u == 2 and later(i) and not last_pair(i):
                        piece_lo(i)
                    if u == 4 and not last_pair(i):
                        weights_lo(0, i + 1)
                    if u == 2 and last_pair(i):
                        more_constants()
                    if u == NC and last_pair(i):
                        step.inc(chunk_stats(u))
                        step.wait()
                        moments(0, EARLY)
                    if u == UNITS - 2 and last_pair(i):
                        chunk_stats(u - 1)
                        for n in range(2):
                            turn_lo(turns[1], n, turn_bank(n))

            dve.wait_ge(weight_ready, 1)
            pair(0)
            with dve.Fori(1, LAST) as i:
                pair(i)
            pair(LAST)
            chunk_stats(UNITS - 2)
            step.inc(chunk_stats(UNITS - 1))
            step.wait()
            moments(EARLY, NT)
            for par in range(2):
                nc.vector.memset(V2[par][:, :, DH], 1.0)
                last = nc.vector.memset(V2[par][:, :, DH + HV], 0.0)
            step.inc(last)
            step.wait()

            def split_queries(b):
                dve.wait_ge(qh_done, b + 1)
                since(dve, alone_loaded, 64 * b)
                nc.vector.scalar_tensor_tensor(qs, qh, slotm[:, 0:1], tq, ALU.mult, ALU.add).then_inc(q_ready, 1)

            def split_values(b, par):
                dve.wait_ge(v_done, b + 1)
                step.inc(nc.vector.scalar_tensor_tensor(
                    vt.rearrange("p (k n) -> p k n", k=2), ps[:, 4, :].rearrange("p (k n) -> p k n", k=2), 1.0 / WS,
                    rows[:, R_BV:R_BV + D].unsqueeze(1).broadcast_to([P, 2, D]), ALU.mult, ALU.add))
                step.wait()
                vh = vt.rearrange("p (n d) -> p n d", d=DH)
                nc.vector.tensor_copy(V2[par][:, :, 0:DH], vh).then_inc(v_hi_done, 1)

            def maxima(b, n):
                qt, gp, jp = n // 4, (n // 2) % 2, n % 2
                dve.wait_ge(rows_done, 8 * b + n + 1)
                o = nm[:, qt, gp * 8 + jp * 4:gp * 8 + jp * 4 + 4].rearrange("p (j g) -> p j g", j=2)
                nc.vector.tensor_reduce(o, ps[:, 2:4, 0:2 * SPAN].rearrange("p a (g q) -> p a g q", g=2),
                                        AX.X, ALU.max, negate=True).then_inc(max_done, 1)

            def context_lo(b):
                dve.wait_ge(c_hi_done, b + 1)
                nc.vector.tensor_tensor(cT_lo, ps[:, context_bank(b), :].rearrange("p (k n) -> p k n", k=KC), cT_hi,
                                        ALU.subtract).then_inc(c_split, 1)

            def add_attention(b):
                dve.wait_ge(o_done, b + 1)
                dve.wait_ge(bias_added, b + 1)
                xb = flat(X[:, ds(2 * b, 2), :])
                nc.vector.scalar_tensor_tensor(xb, ps[:, output_bank(b), :], tgw[:, 1:2], xb, ALU.mult, ALU.add)\
                    .then_inc(x_added, 1)

            def batch_stats(b):
                dve.wait_ge(x_added, b + 1)
                tile_stats(2 * b)
                return tile_stats(2 * b + 1)

            def half_context(b, half):
                dve.wait_ge(av_done, 8 * b + 4 * half + 4)
                for qt in range(2):
                    last = nc.vector.tensor_reduce(
                        avs[:, qt, :, :], ps[:, 6 + qt, 0:8 * 2 * HV].rearrange("p (h s d) -> p h d s", h=8, s=2),
                        AX.X, ALU.add)
                last.then_inc(av_read, 1)
                dve.wait_ge(av_read, 2 * b + half + 1)
                step.inc(nc.vector.reciprocal(rc[:, :, :], avs[:, :, :, DH]))
                step.wait()
                for qt in range(2):
                    last = nc.vector.tensor_tensor(
                        cx[:, qt, half * P:half * P + P].rearrange("p (h d) -> p h d", h=8), avs[:, qt, :, 0:DH],
                        rc[:, qt, :].unsqueeze(2).broadcast_to([P, 8, DH]), ALU.mult)
                last.then_inc(cx_ready, 1)

            def probabilities_lo(b, n):
                dve.wait_ge(p_hi_done, 8 * b + n + 1)
                nc.vector.tensor_tensor(P_lo[:, n % 4, :, :], PT[:, n % 4, :, :], P_hi[:, n % 4, :, :], ALU.subtract)\
                    .then_inc(p_split, 1)

            def turn_maxima(b):
                dve.wait_ge(nm_turned, b + 1)
                turned = ps[0:HEADS, 5, 0:2 * P]
                nc.vector.tensor_copy(nmT[0:HEADS, :], turned).then_inc(nm_hi_done, 1)
                dve.wait_ge(nm_hi_done, b + 1)
                nc.vector.tensor_tensor(nmT[LOW_ROWS:LOW_ROWS + HEADS, :], turned, nmT[0:HEADS, :], ALU.subtract)\
                    .then_inc(nm_ready, 1)

            def attend(b, par):
                for n in range(8):
                    if n >= 2:
                        probabilities_lo(b, n - 2)
                    if n == 7:
                        half_context(b, 0)
                    if within(b + 1):
                        maxima(b + 1, n)
                    if n == 2 and later(b):
                        context_lo(b - 1)
                    if n == 4 and later(b):
                        add_attention(b - 1)
                    if n == 3 and not within(b + 1):
                        moments(0, FFN_EARLY)
                    if n in (4, 5) and not within(b + 1):
                        dve.wait_ge(rstd_ready, 7)
                        since(dve, turns[2].turned, n - 4)
                        turn_rows(turns[2], n - 4, 0)
                    if n in (5, 6) and not within(b + 1):
                        turn_lo(turns[2], n - 5, 3)
                probabilities_lo(b, 6)
                if within(b + 1):
                    turn_maxima(b + 1)
                probabilities_lo(b, 7)
                if within(b + 2):
                    split_queries(b + 2)
                if later(b):
                    batch_stats(b - 1)
                half_context(b, 1)
                if within(b + 2):
                    split_values(b + 2, par)

            STEPS = 3

            def turn_two(n):
                turn_lo(turns[1], n, turn_bank(n))
                turn_lo(turns[1], n + 1, turn_bank(n + 1))

            split_queries(0)
            dve.wait_ge(rstd_ready, 6)
            turn_rows(turns[1], 2)
            turn_rows(turns[1], 3)
            for n in range(8):
                maxima(0, n)
                if n == 0:
                    split_values(0, 0)
                if n in (0, 2, 4):
                    turn_two(n + 2)
                if n in (0, 2):
                    turn_rows(turns[1], n + 4)
                    turn_rows(turns[1], n + 5)
            turn_maxima(0)
            split_queries(1)
            split_values(1, 1)
            attend(0, 0)
            base = step.at
            with dve.Fori(0, LOOPED // 2) as i:
                for par in (1, 0):
                    step.at = base + 2 * STEPS * i + STEPS * (1 - par)
                    attend(2 * i + 2 - par, par)
            step.at = base + STEPS * LOOPED
            for b in range(LOOPED + 1, B):
                attend(b, b % 2)

            def source(c, n):
                cc = ds(c * CH, CH)
                if n == 0:
                    dve.wait_ge(diff_done, c + 1)
                    nc.vector.tensor_scalar(second_mask, ps[:, 2, :], 0.0, None, ALU.is_gt).then_inc(mask_ready, 1)
                    dve.wait_ge(mask_ready, c + 1)
                if n in (1, 2):
                    mine, of = ((s1_hi, hT_hi), (s1_lo, hT_lo))[n - 1]
                    nc.vector.tensor_tensor(mine, of[:, :, cc], second_mask.unsqueeze(1).broadcast_to([P, KC, CH]),
                                            ALU.mult).then_inc(sources_ready, 1)
                if n in (3, 4):
                    mine, of, other = ((s0_hi, hT_hi, s1_hi), (s0_lo, hT_lo, s1_lo))[n - 3]
                    dve.wait_ge(sources_ready, 4 * c + n - 2)
                    nc.vector.tensor_tensor(mine, of[:, :, cc], other, ALU.subtract).then_inc(sources_ready, 1)

            def add_switched(c):
                dve.wait_ge(d_done, D_AHEAD + BLOCKS * c + BLOCKS)
                dve.wait_ge(bias2_added, c + 1)
                for t in range(CT):
                    xt = one(X[:, ds(CT * c + t, 1), :])
                    last = nc.vector.scalar_tensor_tensor(xt, ps[:, 4 + t // 2, (t % 2) * D:(t % 2) * D + D],
                                                          tgw[:, 3:4], xt, ALU.mult, ALU.add)
                last.then_inc(y_added, 1)

            def switched_chunk(c):
                for u in range(BLOCKS):
                    n = c * BLOCKS + u
                    dve.wait_ge(relu_done, n + 1)
                    dve.wait_ge(d_done, D_AHEAD + n - 3)
                    nc.vector.tensor_copy(H_hi[:, u % 4, :], act_s[:, u % 2, :]).then_inc(h_hi_done, 1)
                    dve.wait_ge(h_hi_done, n + 1)
                    nc.vector.tensor_tensor(H_lo[:, u % 4, :], act_s[:, u % 2, :], H_hi[:, u % 4, :], ALU.subtract)\
                        .then_inc(h_split, 1)
                    if u == 0 and later(c):
                        add_switched(c - 1)
                    source(c, u)
                    if u == 1 and not later(c):
                        context_lo(B - 1)
                    if u == 4 and not later(c):
                        add_attention(B - 1)
                        step.inc(batch_stats(B - 1))
                        step.wait()
                        moments(FFN_EARLY, NT)
                    if u in TURN_ROWS and not last_chunk(c):
                        dve.wait_ge(rstd_ready, 8)
                        turn_rows(turns[2], 2 * c + 2 + TURN_ROWS.index(u), 0)
                    if u in TURN_LO and not last_chunk(c):
                        turn_lo(turns[2], 2 * c + 2 + TURN_LO.index(u), 3)

            switched_chunk(0)
            with dve.Fori(1, NC - 1) as c:
                switched_chunk(c)
            switched_chunk(NC - 1)
            add_switched(NC - 1)

        @block.tensor
        def _(pe):
            pe.sem_inc(d_done, D_AHEAD)

            def three(o, a_hi, a_lo, b_hi, b_lo, start, stop, **kw):
                nc.tensor.matmul(o, a_hi, b_hi, start=start, stop=False, **kw)
                nc.tensor.matmul(o, a_hi, b_lo, start=False, stop=False, **kw)
                return nc.tensor.matmul(o, a_lo, b_hi, start=False, stop=stop, **kw)

            pe.wait_ge(decay_ready, 2)
            for q in range(4):
                pe.wait_ge(squares_ready, q + 1)
                with pe.Fori(2 * q, 2 * q + 2) as b:
                    sq = [one(TM[:, ds(2 * b + h, 1), :]) for h in range(2)]
                    o = [one(ps[:, ds(b, 1), h * D:h * D + D]) for h in range(2)]
                    nc.tensor.matmul(o[0], decay[:, 0:P], sq[0], start=True, stop=True)
                    nc.tensor.matmul(o[1], decay[:, P:D], sq[0], start=True, stop=False)
                    nc.tensor.matmul(o[1], decay[:, 0:P], sq[1], start=False, stop=True).then_inc(scan_done, 1)

            def turn(t, n, at, bank):
                pe.wait_ge(t.rows_ready, n + 1)
                for k in range(KC):
                    for h in range(2):
                        last = nc.tensor.transpose(ps[:, bank, k * 2 * P + h * P:k * 2 * P + h * P + P],
                                                   stage[:, 2 * at + h, k * P:k * P + P], ident[:, 0:P])
                last.then_inc(t.turned, 1)

            def gate_up(i, u):
                buf = (u // NC) % 2
                c = slice((u % NC) * CH, (u % NC) * CH + CH)
                if u % NC == 0:
                    pe.wait_ge(ew_split[buf], i + 1 + u // UNITS)
                since(pe, prod_done, i * UNITS + u - 1)
                for which in range(2):
                    for k in range(KC):
                        w = slice(which * D + k * P, which * D + k * P + P)
                        last = three(ps[:, 2 * which + u % 2, :], ew_hi[:, buf, w], ew_lo[:, buf, w],
                                     hT_hi[:, k, c], hT_lo[:, k, c], k == 0, k == KC - 1)
                last.then_inc(gate_up_done, 1)

            def down(i, u):
                buf = u // NC
                n = i * UNITS + u
                pe.wait_ge(H_lo_done, n + 1)
                since(pe, added, n - 1)
                if not later(i) and u == 1:
                    pe.wait_ge(gate_tanh_done, 1)
                for t in range(CT):
                    c = slice(t * P, t * P + P)
                    last = three(ps[:, 4 + 2 * (u % 2) + t // 2, (t % 2) * D:(t % 2) * D + D],
                                 H_hi[:, u % 4, c], H_lo[:, u % 4, c],
                                 ew_hi[:, buf, 2 * D:3 * D], ew_lo[:, buf, 2 * D:3 * D], True, True)
                last.then_inc(down_done, 1)

            def pair(i):
                for u in range(UNITS):
                    if not last_pair(i) or u < UNITS - 2:
                        gate_up(i, u + 2)
                    down(i, u)
                    if last_pair(i) and u == UNITS - 1:
                        pe.wait_ge(prod_done, PAIRS * UNITS)
                        for n in range(2):
                            turn(turns[1], n, n, turn_bank(n))

            for n in range(NT // 2):
                since(pe, turns[0].lo_done, n - 2)
                if n < 4:
                    pe.wait_ge(mix_done, 4 + n + 1)
                pe.wait_ge(odd_rows_ready, n + 1)
                turn(turns[0], n, n % 2, 4 + n % 3)
                if n in GATES_AFTER:
                    u = GATES_AFTER.index(n)
                    pe.wait_ge(turns[0].lo_done, 2 * u + 2)
                    gate_up(0, u)
            pe.wait_ge(gw_split, 2)
            for t in range(NT):
                if t % 2 == 0:
                    pe.wait_ge(turns[0].lo_done, t // 2 + 1)
                c = slice(t * P, t * P + P)
                for k in range(KC):
                    w = slice(k * E, k * E + E)
                    last = three(ps[:, 7, t * E:t * E + E], hT_hi[:, k, c], hT_lo[:, k, c], gw_hi[:, w], gw_lo[:, w],
                                 k == 0, k == KC - 1)
            last.then_inc(logits_done, 1)
            pair(0)
            with pe.Fori(1, LAST) as i:
                pair(i)
            pair(LAST)

            pe.wait_ge(turns[1].lo_done, 1)
            pe.wait_ge(consts_ready, 1)
            pe.wait_ge(ctx_split, UNITS)

            def project_wide(b, at, bank, hi, lo, done, groups=range(4)):
                for g in groups:
                    for k in range(KC):
                        w = slice(at + k * QD + g * P, at + k * QD + g * P + P)
                        last = three(ps[:, bank + g // 2, (g % 2) * D:(g % 2) * D + D], wr_hi[:, w], wr_lo[:, w],
                                     hi[:, k, ds(b * S, S)], lo[:, k, ds(b * S, S)], k == 0, k == KC - 1)
                    if g == 3:
                        last.then_inc(done, 1)

            def project_queries(b, groups=range(4)):
                project_wide(b, A_Q, 0, hT_hi, hT_lo, q_done, groups)

            def project_keys(b):
                project_wide(b, A_K, 2, uT_hi, uT_lo, k_done)

            def project_values(b):
                since(pe, v_ready, b)
                since(pe, x_added, b - 2)
                for kt in range(2):
                    for k in range(KC):
                        w = slice(A_V + k * D, A_V + k * D + D)
                        c = ds(b * S + kt * P, P)
                        last = three(ps[:, 4, kt * D:kt * D + D], uT_hi[:, k, c], uT_lo[:, k, c], wr_hi[:, w],
                                     wr_lo[:, w], k == 0, k == KC - 1)
                last.then_inc(v_done, 1)

            def by_group(t):
                return t.rearrange("p (g n) -> p g n", g=4)

            def score_rows(b, par, n):
                qt, gp, jp = n // 4, (n // 2) % 2, n % 2
                if n == 0:
                    pe.wait_ge(q_ready, b + 1)
                    pe.wait_ge(kh_done, b + 1)
                else:
                    pe.wait_ge(max_done, 8 * b + n)
                for jj in range(2):
                    j = 2 * jp + jj
                    bank = 2 + jj
                    sl = slice(32 * j, 32 * j + 32)
                    nc.tensor.matmul(ps[:, bank, 0:2 * SPAN], identb[:, :], maskb[:, qt, :], start=True,
                                     stop=False, skip_group_check=True)
                    for gg in range(2):
                        last = nc.tensor.matmul(
                            ps[:, bank, gg * SPAN:gg * SPAN + SPAN],
                            by_group(qs)[sl, 2 * gp + gg, qt * P:qt * P + P],
                            by_group(kh[par])[sl, 2 * gp + gg, qt * WINDOW:qt * WINDOW + SPAN],
                            start=False, stop=(gg == 1), skip_group_check=True)
                last.then_inc(rows_done, 1)

            def score_columns(b, par, n):
                g, jp = n // 2, n % 2
                if n == 0 and within(b + 1):
                    pe.wait_ge(tq_done, b + 2)
                else:
                    pe.wait_ge(exp_done, 8 * b + n)
                for jj in range(2):
                    j = 2 * jp + jj
                    bank = jj
                    at_h = (g // 2) * 8 + j * 2 + g % 2
                    for kt in range(2):
                        o = ps[:, bank, kt * SPAN:kt * SPAN + SPAN]
                        q = by_group(alone[j])[:, g, kt * WINDOW:kt * WINDOW + SPAN]
                        keys = slice(kt * P, kt * P + P)
                        nc.tensor.matmul(o, headsel[:, at_h, :], nmT[:, kt * WINDOW:kt * WINDOW + SPAN],
                                         start=True, stop=False)
                        nc.tensor.matmul(o, by_group(kh[par])[:, g, keys], q, start=False, stop=False)
                        last = nc.tensor.matmul(o, by_group(kl[par])[:, g, keys], q, start=False, stop=True)
                last.then_inc(sT_done, 1)

            def values(b, par, n):
                g, jp = n // 2, n % 2
                pe.wait_ge(p_split, 8 * b + n + 1)
                if n % 4 == 0:
                    since(pe, av_read, 2 * b + n // 4)
                for jj in range(2):
                    h = 4 * g + 2 * jp + jj
                    w = slice((h % 8) * 2 * HV, (h % 8 + 1) * 2 * HV)
                    v = [V2[par][:, kt * HEADS + h, :] for kt in range(2)]
                    for bank, full, q_full, part, q_part, rows_part in (
                            (6, 0, slice(0, P), 1, slice(SPAN, SPAN + WINDOW), slice(WINDOW, P)),
                            (7, 1, slice(SPAN + WINDOW, 2 * SPAN), 0, slice(P, SPAN), slice(0, WINDOW))):
                        for first, p in ((True, P_hi), (False, P_lo)):
                            nc.tensor.matmul(ps[:, bank, w], p[:, n % 4, jj, q_full], v[full], start=first,
                                             stop=False, skip_group_check=True)
                        for end, p in ((False, P_hi), (True, P_lo)):
                            last = nc.tensor.matmul(ps[rows_part, bank, w], p[:, n % 4, jj, q_part], v[part],
                                                    start=False, stop=end, skip_group_check=True)
                last.then_inc(av_done, 1)

            def turn_context(b):
                pe.wait_ge(cx_ready, 2 * b + 2)
                for k in range(KC):
                    for qt in range(2):
                        last = nc.tensor.transpose(ps[:, context_bank(b), k * 2 * P + qt * P:k * 2 * P + qt * P + P],
                                                   cx[:, qt, k * P:k * P + P], ident[:, 0:P])
                last.then_inc(cx_turned, 1)

            def project_out(b):
                pe.wait_ge(c_split, b + 1)
                if within(b + 2):
                    pe.wait_ge(v_ready, b + 3)
                elif within(b + 1):
                    pe.wait_ge(v_ready, B)
                    pe.wait_ge(x_added, b)
                else:
                    pe.wait_ge(mask_ready, 1)
                for qt in range(2):
                    for k in range(KC):
                        w = slice(A_O + k * D, A_O + k * D + D)
                        c = slice(qt * P, qt * P + P)
                        last = three(ps[:, output_bank(b), qt * D:qt * D + D], cT_hi[:, k, c], cT_lo[:, k, c], wr_hi[:, w],
                                     wr_lo[:, w], k == 0, k == KC - 1)
                last.then_inc(o_done, 1)

            sources = ((hT_hi, hT_lo), (s0_hi, s0_lo), (s1_hi, s1_lo))

            def difference(c):
                cc = ds(c * CH, CH)
                for k in range(KC):
                    last = three(ps[:, 2, :], gd_hi[:, k, :], gd_lo[:, k, :], hT_hi[:, k, cc], hT_lo[:, k, cc],
                                 k == 0, k == KC - 1)
                last.then_inc(diff_done, 1)

            def hidden(c, u):
                which = u // (HIDDEN // P)
                hi, lo = sources[which]
                since(pe, relu_done, c * BLOCKS + u - 1)
                if u == HIDDEN // P:
                    pe.wait_ge(sources_ready, 4 * c + 4)
                cc = slice(0, CH) if which else ds(c * CH, CH)
                for k in range(KC):
                    a = u * 2 * D + k * P
                    last = three(ps[:, u % 2, :], wr_hi[:, a:a + P], wr_lo[:, a:a + P], hi[:, k, cc], lo[:, k, cc],
                                 k == 0, k == KC - 1)
                last.then_inc(h_done, 1)

            def second(c, u):
                pe.wait_ge(h_split, SPLIT_AHEAD + c * BLOCKS + u + 1)
                if u == 0 and later(c):
                    pe.wait_ge(y_added, Y_AHEAD + c)
                if u == 0 and not later(c):
                    pe.wait_ge(x_added, B - 1)
                    pe.wait_ge(c_split, B - 1)
                    pe.wait_ge(av_read, 2 * B)
                w = slice(u * 2 * D + D, (u + 1) * 2 * D)
                for t in range(CT):
                    c4 = slice(t * P, t * P + P)
                    last = three(ps[:, 4 + t // 2, (t % 2) * D:(t % 2) * D + D], H_hi[:, u % 4, c4],
                                 H_lo[:, u % 4, c4], wr_hi[:, w], wr_lo[:, w], u == 0 and t % 2 == 0,
                                 u == BLOCKS - 1, skip_group_check=True)
                last.then_inc(d_done, 1)

            def chunk(c):
                for u in range(BLOCKS):
                    if u + 2 < BLOCKS:
                        hidden(c, u + 2)
                    elif not last_chunk(c):
                        if u + 2 == BLOCKS:
                            pe.wait_ge(turns[2].lo_done, 2 * c + 4)
                            difference(c + 1)
                        hidden(c + 1, u + 2 - BLOCKS)
                    if u in TURN and not last_chunk(c):
                        n = 2 * c + 2 + TURN.index(u)
                        pe.wait_ge(turns[2].lo_done, n)
                        turn(turns[2], n, 0, 3)
                    second(c, u)
                    if not later(c) and u == 0:
                        turn_context(B - 1)
                    if not later(c) and u == 2:
                        project_out(B - 1)

            def first_hidden():
                pe.wait_ge(gd_ready, 1)
                pe.wait_ge(turns[2].lo_done, 2)
                pe.wait_ge(exp_done, 8 * B)
                difference(0)
                hidden(0, 0)
                hidden(0, 1)

            def turn_maxima(b):
                pe.wait_ge(max_done, 8 * b + 8)
                since(pe, c_split, b - 1)
                for qt in range(2):
                    last = nc.tensor.transpose(ps[0:HEADS, 5, qt * P:qt * P + P], nm[:, qt, :], ident[:, 0:P])
                last.then_inc(nm_turned, 1)

            def attend(b, par):
                pe.wait_ge(nm_ready, b + 1)
                pe.wait_ge(alone_loaded, 64 * b + 64)
                pe.wait_ge(k_ready, b + 1)
                for n in range(8):
                    score_columns(b, par, n)
                    if within(b + 1):
                        score_rows(b + 1, 1 - par, n)
                    if n == 1 and later(b):
                        turn_context(b - 1)
                    if n == 3 and later(b):
                        project_out(b - 1)
                    if n == 3:
                        pe.wait_ge(v_ready, b + 1)
                    if 3 <= n < 7:
                        values(b, par, n - 3)
                    if n in (5, 6) and not within(b + 1):
                        since(pe, turns[2].lo_done, n - 5)
                        turn(turns[2], n - 5, 0, 3)
                values(b, par, 4)
                if within(b + 2):
                    pe.wait_ge(exp_done, 8 * b + 8)
                    project_queries(b + 2)
                values(b, par, 5)
                if within(b + 1):
                    turn_maxima(b + 1)
                else:
                    first_hidden()
                if within(b + 2):
                    project_keys(b + 2)
                values(b, par, 6)
                if within(b + 2):
                    project_values(b + 2)
                values(b, par, 7)

            def turn_two(m):
                for n in (m, m + 1):
                    since(pe, turns[1].lo_done, n - 2 if n >= 5 else 0)
                    turn(turns[1], n, n % 2, turn_bank(n))

            pe.wait_ge(turns[1].lo_done, 2)
            project_queries(0)
            project_keys(0)
            pe.wait_ge(added, PAIRS * UNITS)
            project_values(0)
            pe.wait_ge(tq_done, 1)
            for n in range(8):
                score_rows(0, 0, n)
                if n in (0, 2, 4):
                    turn_two(n + 2)
                if n in (1, 3):
                    project_queries(1, (n - 1, n))
                if n == 5:
                    project_values(1)
            turn_maxima(0)
            project_keys(1)
            pe.wait_ge(turns[1].lo_done, NT // 2)
            attend(0, 0)
            with pe.Fori(0, LOOPED // 2) as i:
                attend(2 * i + 1, 1)
                attend(2 * i + 2, 0)
            for b in range(LOOPED + 1, B):
                attend(b, b % 2)

            chunk(0)
            with pe.Fori(1, NC - 1) as c:
                chunk(c)
            chunk(NC - 1)


def _layout(a):
    import numpy as np

    c = np.ascontiguousarray

    def halves(w):
        return w.reshape(KC, P, -1).transpose(1, 0, 2).reshape(P, -1)

    x = c(a["x"].reshape(NT, P, D).transpose(1, 0, 2))
    ctx = c(a["ctx_1024"].reshape(NT, P, D).transpose(1, 0, 2))
    ctxT = c(halves(a["ctx_1024"].reshape(TOK, D).T))
    experts = []
    for s in range(SHARED):
        cut = slice(s * P, s * P + P)
        experts.append(np.concatenate([halves(a["L0_ffn_sh_gate"][cut].T), halves(a["L0_ffn_sh_up"][cut].T),
                                       a["L0_ffn_sh_down"][:, cut].T], 1))
    for e in range(E):
        experts.append(np.concatenate([halves(a["L0_ffn_w_gate"][e].T), halves(a["L0_ffn_w_up"][e].T),
                                       a["L0_ffn_w_down"][e].T], 1))
    wexp = c(np.stack(experts))
    rest = []
    firsts = [a["L1_ffn_sw1"], a["L1_ffn_w1"][0], a["L1_ffn_w1"][1]]
    seconds = [a["L1_ffn_sw2"], a["L1_ffn_w2"][0], a["L1_ffn_w2"][1]]
    for w1, w2 in zip(firsts, seconds):
        for n in range(HIDDEN // P):
            rest += [halves(w1[:, n * P:n * P + P]), w2[n * P:n * P + P]]
    twice = np.stack([np.arange(D).reshape(HEADS, DH)] * 2, 1).reshape(-1)
    rest += [halves(a["L1_xattn_Wq"].T[:, twice]), halves(a["L1_xattn_Wk"].T[:, twice]),
             halves(a["L1_xattn_Wv"].T), halves(a["L1_xattn_Wo"].T)]
    wrest = c(np.concatenate(rest, 1))
    rows = c(np.concatenate([a["g_xattn"], a["g_ffn"], a["L0_ffn_gate_bias"], a["L1_xattn_bv"], a["L1_xattn_bo"],
                             a["L1_ffn_sb2"], a["L1_ffn_b2"][0], a["L1_ffn_b2"][1]]).reshape(1, -1))
    b1 = np.concatenate([a["L1_ffn_sb1"], a["L1_ffn_b1"].reshape(-1)]).reshape(BLOCKS, P).T
    cols = c(np.concatenate([a["L1_xattn_bq"][twice].reshape(4, P).T, a["L1_xattn_bk"][twice].reshape(4, P).T, b1,
                             halves(a["L0_ffn_gate_w"].T), halves(a["L1_ffn_gate_w"].T)], 1))
    return {"x": x, "ctx": ctx, "ctxT": ctxT, "wexp": wexp, "wrest": wrest, "rows": rows, "cols": cols}


def kernel(**inputs):
    import numpy as np
    import concourse.bacc as bacc
    from concourse.bass_utils import run_bass_kernel_spmd

    packed = _layout({k: np.asarray(v) for k, v in inputs.items()})
    nc = bacc.Bacc("TRN2", target_bir_lowering=False, num_devices=1)
    args = [nc.dram_tensor(f"in_{n}", v.shape, F32, kind="ExternalInput").ap() for n, v in packed.items()]
    out = nc.dram_tensor("out_x", [P, NT, D], F32, kind="ExternalOutput").ap()
    two_layers(nc, *args, out)
    r = run_bass_kernel_spmd(nc, [{f"in_{n}": v for n, v in packed.items()}], core_ids=[0])
    return r.results[0]["out_x"].reshape(P, NT, D).transpose(1, 0, 2).reshape(B, S, D)
```
